# Optimizing a Trainium2 kernel written in Bass

```python
import numpy as np
import jax
import jax.numpy as jnp

def _softmax(x, axis=-1):
    return jax.nn.softmax(x, axis=axis)

def _gelu(x):
    return jax.nn.gelu(x, approximate=True)

def _silu(x):
    return jax.nn.silu(x)

def _sigmoid(x):
    return jax.nn.sigmoid(x)

def _layernorm(x, axis=-1, eps=1e-05):
    m = jnp.mean(x, axis=axis, keepdims=True)
    v = jnp.var(x, axis=axis, keepdims=True)
    return (x - m) / jnp.sqrt(v + eps)

def _scatter_add(tgt, idx, src, axis=0):
    return tgt.at[idx].add(src)

def _segment_sum(src, seg, n):
    return jax.ops.segment_sum(src, seg, n)
kernel_name = 'mk_perceiver_d1_seqx_r2_5db698'

def setup_inputs(seed: int=0):
    np.random.seed(seed)
    _w = jnp.asarray

    def _rec_inputs():
        import jax
        import jax.numpy as jnp
        _rk = jax.random.key(seed)
        x = -0.0002928 + 1 * jax.random.normal(jax.random.fold_in(_rk, 1), (8, 128, 512), jnp.float32)
        _lenS = 128 - jax.random.randint(jax.random.fold_in(_rk, 7), (8,), 0, max(1, 128 // 4) + 1, jnp.int32)
        _lenS2 = 2048 - jax.random.randint(jax.random.fold_in(_rk, 8), (8,), 0, max(1, 2048 // 4) + 1, jnp.int32)
        _ctx_1024P = jax.random.normal(jax.random.fold_in(_rk, 11), (8, 16, 512), jnp.float32)
        _ctx_1024c = jax.random.dirichlet(jax.random.fold_in(_rk, 511), 0.3 * jnp.ones((16,), jnp.float32), (8, 2048))
        _ctx_1024t = jnp.einsum('bsk,bkd->bsd', _ctx_1024c, _ctx_1024P)
        _ctx_1024t = _ctx_1024t * jax.lax.rsqrt(jnp.mean(jnp.square(_ctx_1024t)) + 1e-12) * 0.953939
        ctx_1024 = 2.81802e-05 + 1.00001 * (_ctx_1024t + 0.3 * jax.random.normal(jax.random.fold_in(_rk, 611), (8, 2048, 512), jnp.float32))
        _validS = jnp.arange(128)[None, :] < _lenS[:, None]
        _validS2 = jnp.arange(2048)[None, :] < _lenS2[:, None]
        _causal = jnp.tril(jnp.ones((128, 128), dtype=bool))
        mask_BxS2_bk1 = jnp.broadcast_to(_validS2[:, :], (8, 2048))
        return (x, ctx_1024, mask_BxS2_bk1)
    x, ctx_1024, mask_BxS2_bk1 = _rec_inputs()

    def _L0_xattn_setup():
        import jax, jax.numpy as jnp
        import numpy as np
        B, N, M = (4, 512, 2048)
        DQ, DC = (512, 512)
        H, DH = (16, 64)
        INNER = H * DH
        SCALE = DH ** (-0.5)
        key = jax.random.key(seed)
        ks = jax.random.split(key, 6)
        x = jax.random.normal(ks[0], (B, N, DQ), dtype=jnp.float32)
        context = jax.random.normal(ks[1], (B, M, DC), dtype=jnp.float32)
        mask = jax.random.bernoulli(ks[2], 0.9, (B, M))
        Wq = jax.random.normal(ks[3], (DQ, INNER), dtype=jnp.float32) / np.sqrt(DQ)
        Wkv = jax.random.normal(ks[4], (DC, 2 * INNER), dtype=jnp.float32) / np.sqrt(DC)
        Wo = jax.random.normal(ks[5], (INNER, DQ), dtype=jnp.float32) / np.sqrt(INNER)
        bo = jnp.zeros((DQ,), dtype=jnp.float32)
        return {'x': x, 'context': context, 'mask': mask, 'Wq': Wq, 'Wkv': Wkv, 'Wo': Wo, 'bo': bo}
    _L0_xattn_all = _L0_xattn_setup()
    _L0_xattn_in = {k: v for k, v in _L0_xattn_all.items() if k in ('Wq', 'Wkv', 'Wo', 'bo')}
    del _L0_xattn_all

    def _L0_attn_setup():
        import jax, jax.numpy as jnp
        import numpy as np
        import math
        N_HEAD = 16
        V_HEAD = 32
        NOPE = 32
        ROPE_D = 64
        KEEP = 128
        EPS = 1e-06

        def _freqs(T, dim=ROPE_D, theta=10000.0):
            f = 1.0 / theta ** (jnp.arange(0, dim, 2, dtype=jnp.float32) / dim)
            t = jnp.arange(T, dtype=jnp.float32)
            a = jnp.outer(t, f)
            return (jnp.cos(a), jnp.sin(a))

        def _rope(x, cos, sin):
            S = x.shape[-2]
            c = cos[:S][None, None]
            s = sin[:S][None, None]
            x1, x2 = jnp.split(x, 2, axis=-1)
            return jnp.concatenate([x1 * c - x2 * s, x1 * s + x2 * c], axis=-1)

        def _rms(x, g, eps=EPS):
            return x * jax.lax.rsqrt(jnp.mean(x * x, axis=-1, keepdims=True) + eps) * g

        def _attn(q, k, v, causal):
            scale = 1.0 / math.sqrt(q.shape[-1])
            s = jnp.einsum('bhqd,bhkd->bhqk', q, k) * scale
            if causal:
                Tq, Tk = (s.shape[-2], s.shape[-1])
                mask = jnp.tril(jnp.ones((Tq, Tk), dtype=bool))
                s = jnp.where(mask, s, jnp.finfo(s.dtype).min)
            return jnp.einsum('bhqk,bhkd->bhqd', jax.nn.softmax(s, axis=-1), v)

        def _forward(x, w_cq, g_qnorm, w_dq_nope, w_dq_rope, w_ckv, g_kvnorm, w_dk_nope, w_dv, w_krope, w_imp, w_selk, w_selv, w_wink, w_winv, w_gate, w_proj):
            B, T, C = x.shape
            cos, sin = _freqs(T)
            nq = _rms(x @ w_cq, g_qnorm)
            q_nope = (nq @ w_dq_nope).reshape(B, T, N_HEAD, NOPE).transpose(0, 2, 1, 3)
            q_rope = (nq @ w_dq_rope).reshape(B, T, N_HEAD, ROPE_D).transpose(0, 2, 1, 3)
            q_rope = _rope(q_rope, cos, sin)
            q = jnp.concatenate([q_nope, q_rope], axis=-1)
            gate = jax.nn.softmax((x @ w_gate).mean(axis=1), axis=-1)
            ckv = _rms(x @ w_ckv, g_kvnorm)
            k_nope = (ckv @ w_dk_nope).reshape(B, T, N_HEAD, NOPE).transpose(0, 2, 1, 3)
            v1 = (ckv @ w_dv).reshape(B, T, N_HEAD, V_HEAD).transpose(0, 2, 1, 3)
            k_rope = (x @ w_krope).reshape(B, T, 1, ROPE_D).transpose(0, 2, 1, 3) / N_HEAD
            k_rope = _rope(k_rope, cos, sin)
            k1 = jnp.concatenate([k_nope, jnp.broadcast_to(k_rope, (B, N_HEAD, T, ROPE_D))], axis=-1)
            scores = (x @ w_imp)[..., 0]
            _, idx = jax.lax.top_k(scores, KEEP)
            idx = jnp.sort(idx, axis=1)
            sel = jnp.take_along_axis(x, idx[:, :, None], axis=1)
            ks = (sel @ w_selk).reshape(B, KEEP, N_HEAD, NOPE + ROPE_D).transpose(0, 2, 1, 3)
            vs = (sel @ w_selv).reshape(B, KEEP, N_HEAD, V_HEAD).transpose(0, 2, 1, 3)
            ks = jnp.concatenate([ks[..., :NOPE], _rope(ks[..., NOPE:], cos, sin)], axis=-1)
            kw = (x @ w_wink).reshape(B, T, N_HEAD, NOPE + ROPE_D).transpose(0, 2, 1, 3)
            vw = (x @ w_winv).reshape(B, T, N_HEAD, V_HEAD).transpose(0, 2, 1, 3)
            kw = jnp.concatenate([kw[..., :NOPE], _rope(kw[..., NOPE:], cos, sin)], axis=-1)
            a1 = _attn(q, k1, v1, causal=True)
            a2 = _attn(q, ks, vs, causal=False)
            a3 = _attn(q, kw, vw, causal=True)
            g = gate[:, :, None, None, None]
            out = g[:, 0] * a1 + g[:, 1] * a2 + g[:, 2] * a3
            out = out.transpose(0, 2, 1, 3).reshape(B, T, N_HEAD * V_HEAD)
            return out @ w_proj
        key = jax.random.key(seed)
        ks = jax.random.split(key, 20)
        B, T, C = (2, 512, 512)
        q_lora, kv_lora = (96, 32)
        std = 0.02

        def w(k, shape):
            return jax.random.normal(k, shape, dtype=jnp.float32) * std
        return {'x': jax.random.normal(ks[0], (B, T, C), dtype=jnp.float32), 'w_cq': w(ks[1], (C, q_lora)), 'g_qnorm': jnp.ones((q_lora,), jnp.float32), 'w_dq_nope': w(ks[2], (q_lora, N_HEAD * NOPE)), 'w_dq_rope': w(ks[3], (q_lora, N_HEAD * ROPE_D)), 'w_ckv': w(ks[4], (C, kv_lora)), 'g_kvnorm': jnp.ones((kv_lora,), jnp.float32), 'w_dk_nope': w(ks[5], (kv_lora, N_HEAD * NOPE)), 'w_dv': w(ks[6], (kv_lora, N_HEAD * V_HEAD)), 'w_krope': w(ks[7], (C, ROPE_D)), 'w_imp': w(ks[8], (C, 1)), 'w_selk': w(ks[9], (C, N_HEAD * (NOPE + ROPE_D))), 'w_selv': w(ks[10], (C, N_HEAD * V_HEAD)), 'w_wink': w(ks[11], (C, N_HEAD * (NOPE + ROPE_D))), 'w_winv': w(ks[12], (C, N_HEAD * V_HEAD)), 'w_gate': w(ks[13], (C, 3)), 'w_proj': w(ks[14], (N_HEAD * V_HEAD, C))}
    _L0_attn_all = _L0_attn_setup()
    _L0_attn_in = {k: v for k, v in _L0_attn_all.items() if k in ('w_cq', 'g_qnorm', 'w_dq_nope', 'w_dq_rope', 'w_ckv', 'g_kvnorm', 'w_dk_nope', 'w_dv', 'w_krope', 'w_imp', 'w_selk', 'w_selv', 'w_wink', 'w_winv', 'w_gate', 'w_proj')}
    del _L0_attn_all

    def _L0_ffn_setup():
        import jax, jax.numpy as jnp
        import numpy as np
        D = 512
        H = 16
        DH = D // H
        DC = D // 4
        HID = 1024
        G = 2
        EPG = 4
        E = G * EPG
        TOPK = 2
        EPS = 1e-06
        B, T = (2, 1024)

        def _rope_sincos(t, dh):
            inv_freq = 1.0 / 10000.0 ** (jnp.arange(0, dh, 2, dtype=jnp.float32) / dh)
            ang = jnp.arange(t, dtype=jnp.float32)[:, None] * inv_freq[None, :]
            return (jnp.sin(ang), jnp.cos(ang))

        def _apply_rope(x, sin, cos):
            x1 = x[..., ::2]
            x2 = x[..., 1::2]
            r = jnp.stack([x1 * cos - x2 * sin, x1 * sin + x2 * cos], axis=-1)
            return r.reshape(x.shape)

        def _swiglu(x):
            a, b = jnp.split(x, 2, axis=-1)
            return jax.nn.silu(a) * b

        def _rmsnorm(x, w):
            return x * jax.lax.rsqrt(jnp.mean(x * x, axis=-1, keepdims=True) + EPS) * w
        key = jax.random.key(seed)
        ks = jax.random.split(key, 14)
        s = 0.02
        return {'src': jax.random.normal(ks[0], (B, T, D), jnp.float32), 'Wq': jax.random.normal(ks[1], (D, D), jnp.float32) * s, 'Wk_c': jax.random.normal(ks[2], (D, DC), jnp.float32) * s, 'Wv_c': jax.random.normal(ks[3], (D, DC), jnp.float32) * s, 'Wk': jax.random.normal(ks[4], (DC, D), jnp.float32) * s, 'Wv': jax.random.normal(ks[5], (DC, D), jnp.float32) * s, 'Wo': jax.random.normal(ks[6], (D, D), jnp.float32) * s, 'W_shared_in': jax.random.normal(ks[7], (D, 2 * HID), jnp.float32) * s, 'W_shared_out': jax.random.normal(ks[8], (HID, D), jnp.float32) * s, 'W1_shared': jax.random.normal(ks[9], (D, 2 * HID), jnp.float32) * s, 'W2_experts': jax.random.normal(ks[10], (E, HID, D), jnp.float32) * s, 'Wg_gate': jax.random.normal(ks[11], (D, G), jnp.float32) * s, 'We_gate': jax.random.normal(ks[12], (D, E), jnp.float32) * s, 'group_bias': jnp.zeros((G,), jnp.float32), 'expert_bias': jnp.zeros((E,), jnp.float32), 'norm1_w': jnp.ones((D,), jnp.float32), 'norm2_w': jnp.ones((D,), jnp.float32)}
    _L0_ffn_all = _L0_ffn_setup()
    _L0_ffn_in = {k: v for k, v in _L0_ffn_all.items() if k in ('Wq', 'Wk_c', 'Wv_c', 'Wk', 'Wv', 'Wo', 'W_shared_in', 'W_shared_out', 'W1_shared', 'W2_experts', 'Wg_gate', 'We_gate', 'group_bias', 'expert_bias', 'norm1_w', 'norm2_w')}
    del _L0_ffn_all
    return {'x': x, 'ctx_1024': ctx_1024, 'mask_BxS2_bk1': mask_BxS2_bk1, 'L0_xattn_Wq': _L0_xattn_in['Wq'], 'L0_xattn_Wkv': _L0_xattn_in['Wkv'], 'L0_xattn_Wo': _L0_xattn_in['Wo'], 'L0_xattn_bo': _L0_xattn_in['bo'], 'L0_attn_w_cq': _L0_attn_in['w_cq'], 'L0_attn_g_qnorm': _L0_attn_in['g_qnorm'], 'L0_attn_w_dq_nope': _L0_attn_in['w_dq_nope'], 'L0_attn_w_dq_rope': _L0_attn_in['w_dq_rope'], 'L0_attn_w_ckv': _L0_attn_in['w_ckv'], 'L0_attn_g_kvnorm': _L0_attn_in['g_kvnorm'], 'L0_attn_w_dk_nope': _L0_attn_in['w_dk_nope'], 'L0_attn_w_dv': _L0_attn_in['w_dv'], 'L0_attn_w_krope': _L0_attn_in['w_krope'], 'L0_attn_w_imp': _L0_attn_in['w_imp'], 'L0_attn_w_selk': _L0_attn_in['w_selk'], 'L0_attn_w_selv': _L0_attn_in['w_selv'], 'L0_attn_w_wink': _L0_attn_in['w_wink'], 'L0_attn_w_winv': _L0_attn_in['w_winv'], 'L0_attn_w_gate': _L0_attn_in['w_gate'], 'L0_attn_w_proj': _L0_attn_in['w_proj'], 'L0_ffn_Wq': _L0_ffn_in['Wq'], 'L0_ffn_Wk_c': _L0_ffn_in['Wk_c'], 'L0_ffn_Wv_c': _L0_ffn_in['Wv_c'], 'L0_ffn_Wk': _L0_ffn_in['Wk'], 'L0_ffn_Wv': _L0_ffn_in['Wv'], 'L0_ffn_Wo': _L0_ffn_in['Wo'], 'L0_ffn_W_shared_in': _L0_ffn_in['W_shared_in'], 'L0_ffn_W_shared_out': _L0_ffn_in['W_shared_out'], 'L0_ffn_W1_shared': _L0_ffn_in['W1_shared'], 'L0_ffn_W2_experts': _L0_ffn_in['W2_experts'], 'L0_ffn_Wg_gate': _L0_ffn_in['Wg_gate'], 'L0_ffn_We_gate': _L0_ffn_in['We_gate'], 'L0_ffn_group_bias': _L0_ffn_in['group_bias'], 'L0_ffn_expert_bias': _L0_ffn_in['expert_bias'], 'L0_ffn_norm1_w': _L0_ffn_in['norm1_w'], 'L0_ffn_norm2_w': _L0_ffn_in['norm2_w']}

def reference(x, ctx_1024, mask_BxS2_bk1, L0_xattn_Wq, L0_xattn_Wkv, L0_xattn_Wo, L0_xattn_bo, L0_attn_w_cq, L0_attn_g_qnorm, L0_attn_w_dq_nope, L0_attn_w_dq_rope, L0_attn_w_ckv, L0_attn_g_kvnorm, L0_attn_w_dk_nope, L0_attn_w_dv, L0_attn_w_krope, L0_attn_w_imp, L0_attn_w_selk, L0_attn_w_selv, L0_attn_w_wink, L0_attn_w_winv, L0_attn_w_gate, L0_attn_w_proj, L0_ffn_Wq, L0_ffn_Wk_c, L0_ffn_Wv_c, L0_ffn_Wk, L0_ffn_Wv, L0_ffn_Wo, L0_ffn_W_shared_in, L0_ffn_W_shared_out, L0_ffn_W1_shared, L0_ffn_W2_experts, L0_ffn_Wg_gate, L0_ffn_We_gate, L0_ffn_group_bias, L0_ffn_expert_bias, L0_ffn_norm1_w, L0_ffn_norm2_w):
    import jax
    import jax.numpy as jnp

    def _L0_xattn_ref(x, context, mask, Wq, Wkv, Wo, bo):
        import jax, jax.numpy as jnp
        import numpy as np
        B, N, M = (4, 512, 2048)
        DQ, DC = (512, 512)
        H, DH = (16, 64)
        INNER = H * DH
        SCALE = DH ** (-0.5)
        q = x @ Wq
        kv = context @ Wkv
        k, v = jnp.split(kv, 2, axis=-1)

        def heads(t):
            b, s, _ = t.shape
            return t.reshape(b, s, H, DH).transpose(0, 2, 1, 3)
        q, k, v = (heads(q), heads(k), heads(v))
        sim = jnp.einsum('bhid,bhjd->bhij', q, k) * SCALE
        max_neg = -jnp.finfo(sim.dtype).max
        sim = jnp.where(mask[:, None, None, :], sim, max_neg)
        sim = jnp.clip(sim, -5.0, 5.0)
        attn = jax.nn.softmax(sim, axis=-1)
        out = jnp.einsum('bhij,bhjd->bhid', attn, v)
        out = out.transpose(0, 2, 1, 3).reshape(x.shape[0], x.shape[1], INNER)
        return out @ Wo + bo

    def _L0_attn_ref(x, w_cq, g_qnorm, w_dq_nope, w_dq_rope, w_ckv, g_kvnorm, w_dk_nope, w_dv, w_krope, w_imp, w_selk, w_selv, w_wink, w_winv, w_gate, w_proj):
        import jax, jax.numpy as jnp
        import numpy as np
        import math
        N_HEAD = 16
        V_HEAD = 32
        NOPE = 32
        ROPE_D = 64
        KEEP = 128
        EPS = 1e-06

        def _freqs(T, dim=ROPE_D, theta=10000.0):
            f = 1.0 / theta ** (jnp.arange(0, dim, 2, dtype=jnp.float32) / dim)
            t = jnp.arange(T, dtype=jnp.float32)
            a = jnp.outer(t, f)
            return (jnp.cos(a), jnp.sin(a))

        def _rope(x, cos, sin):
            S = x.shape[-2]
            c = cos[:S][None, None]
            s = sin[:S][None, None]
            x1, x2 = jnp.split(x, 2, axis=-1)
            return jnp.concatenate([x1 * c - x2 * s, x1 * s + x2 * c], axis=-1)

        def _rms(x, g, eps=EPS):
            return x * jax.lax.rsqrt(jnp.mean(x * x, axis=-1, keepdims=True) + eps) * g

        def _attn(q, k, v, causal):
            scale = 1.0 / math.sqrt(q.shape[-1])
            s = jnp.einsum('bhqd,bhkd->bhqk', q, k) * scale
            if causal:
                Tq, Tk = (s.shape[-2], s.shape[-1])
                mask = jnp.tril(jnp.ones((Tq, Tk), dtype=bool))
                s = jnp.where(mask, s, jnp.finfo(s.dtype).min)
            return jnp.einsum('bhqk,bhkd->bhqd', jax.nn.softmax(s, axis=-1), v)

        def _forward(x, w_cq, g_qnorm, w_dq_nope, w_dq_rope, w_ckv, g_kvnorm, w_dk_nope, w_dv, w_krope, w_imp, w_selk, w_selv, w_wink, w_winv, w_gate, w_proj):
            B, T, C = x.shape
            cos, sin = _freqs(T)
            nq = _rms(x @ w_cq, g_qnorm)
            q_nope = (nq @ w_dq_nope).reshape(B, T, N_HEAD, NOPE).transpose(0, 2, 1, 3)
            q_rope = (nq @ w_dq_rope).reshape(B, T, N_HEAD, ROPE_D).transpose(0, 2, 1, 3)
            q_rope = _rope(q_rope, cos, sin)
            q = jnp.concatenate([q_nope, q_rope], axis=-1)
            gate = jax.nn.softmax((x @ w_gate).mean(axis=1), axis=-1)
            ckv = _rms(x @ w_ckv, g_kvnorm)
            k_nope = (ckv @ w_dk_nope).reshape(B, T, N_HEAD, NOPE).transpose(0, 2, 1, 3)
            v1 = (ckv @ w_dv).reshape(B, T, N_HEAD, V_HEAD).transpose(0, 2, 1, 3)
            k_rope = (x @ w_krope).reshape(B, T, 1, ROPE_D).transpose(0, 2, 1, 3) / N_HEAD
            k_rope = _rope(k_rope, cos, sin)
            k1 = jnp.concatenate([k_nope, jnp.broadcast_to(k_rope, (B, N_HEAD, T, ROPE_D))], axis=-1)
            scores = (x @ w_imp)[..., 0]
            _, idx = jax.lax.top_k(scores, KEEP)
            idx = jnp.sort(idx, axis=1)
            sel = jnp.take_along_axis(x, idx[:, :, None], axis=1)
            ks = (sel @ w_selk).reshape(B, KEEP, N_HEAD, NOPE + ROPE_D).transpose(0, 2, 1, 3)
            vs = (sel @ w_selv).reshape(B, KEEP, N_HEAD, V_HEAD).transpose(0, 2, 1, 3)
            ks = jnp.concatenate([ks[..., :NOPE], _rope(ks[..., NOPE:], cos, sin)], axis=-1)
            kw = (x @ w_wink).reshape(B, T, N_HEAD, NOPE + ROPE_D).transpose(0, 2, 1, 3)
            vw = (x @ w_winv).reshape(B, T, N_HEAD, V_HEAD).transpose(0, 2, 1, 3)
            kw = jnp.concatenate([kw[..., :NOPE], _rope(kw[..., NOPE:], cos, sin)], axis=-1)
            a1 = _attn(q, k1, v1, causal=True)
            a2 = _attn(q, ks, vs, causal=False)
            a3 = _attn(q, kw, vw, causal=True)
            g = gate[:, :, None, None, None]
            out = g[:, 0] * a1 + g[:, 1] * a2 + g[:, 2] * a3
            out = out.transpose(0, 2, 1, 3).reshape(B, T, N_HEAD * V_HEAD)
            return out @ w_proj
        return _forward(x, w_cq, g_qnorm, w_dq_nope, w_dq_rope, w_ckv, g_kvnorm, w_dk_nope, w_dv, w_krope, w_imp, w_selk, w_selv, w_wink, w_winv, w_gate, w_proj)

    def _L0_ffn_ref(src, Wq, Wk_c, Wv_c, Wk, Wv, Wo, W_shared_in, W_shared_out, W1_shared, W2_experts, Wg_gate, We_gate, group_bias, expert_bias, norm1_w, norm2_w):
        import jax, jax.numpy as jnp
        import numpy as np
        D = 512
        H = 16
        DH = D // H
        DC = D // 4
        HID = 1024
        G = 2
        EPG = 4
        E = G * EPG
        TOPK = 2
        EPS = 1e-06
        B, T = (2, 1024)

        def _rope_sincos(t, dh):
            inv_freq = 1.0 / 10000.0 ** (jnp.arange(0, dh, 2, dtype=jnp.float32) / dh)
            ang = jnp.arange(t, dtype=jnp.float32)[:, None] * inv_freq[None, :]
            return (jnp.sin(ang), jnp.cos(ang))

        def _apply_rope(x, sin, cos):
            x1 = x[..., ::2]
            x2 = x[..., 1::2]
            r = jnp.stack([x1 * cos - x2 * sin, x1 * sin + x2 * cos], axis=-1)
            return r.reshape(x.shape)

        def _swiglu(x):
            a, b = jnp.split(x, 2, axis=-1)
            return jax.nn.silu(a) * b

        def _rmsnorm(x, w):
            return x * jax.lax.rsqrt(jnp.mean(x * x, axis=-1, keepdims=True) + EPS) * w
        Bb, Tt, C = src.shape
        q = (src @ Wq).reshape(Bb, Tt, H, DH).transpose(0, 2, 1, 3)
        k = (src @ Wk_c @ Wk).reshape(Bb, Tt, H, DH).transpose(0, 2, 1, 3)
        v = (src @ Wv_c @ Wv).reshape(Bb, Tt, H, DH).transpose(0, 2, 1, 3)
        sin, cos = _rope_sincos(Tt, DH)
        q = _apply_rope(q, sin, cos)
        k = _apply_rope(k, sin, cos)
        attn = jnp.einsum('bhqd,bhkd->bhqk', q, k) / np.sqrt(DH).astype(np.float32)
        attn = jax.nn.softmax(attn, axis=-1)
        sa = jnp.einsum('bhqk,bhkd->bhqd', attn, v)
        sa = sa.transpose(0, 2, 1, 3).reshape(Bb, Tt, C) @ Wo
        x = _rmsnorm(src + sa, norm1_w)
        S = Bb * Tt
        flat = x.reshape(S, C)
        shared = _swiglu(flat @ W_shared_in) @ W_shared_out
        g_probs = jax.nn.softmax(flat @ Wg_gate + group_bias, -1)
        g_idx = jnp.argmax(g_probs, axis=-1)
        e_logits = flat @ We_gate + expert_bias
        e_group = jnp.arange(E) // EPG
        in_group = e_group[None, :] == g_idx[:, None]
        e_probs = jax.nn.softmax(jnp.where(in_group, e_logits, -jnp.inf), -1)
        g_prob = jnp.take_along_axis(g_probs, g_idx[:, None], axis=1)
        p_expert = e_probs * g_prob
        topv, topi = jax.lax.top_k(p_expert, TOPK)
        w = jnp.zeros((S, E), flat.dtype).at[jnp.arange(S)[:, None], topi].set(topv)
        h = _swiglu(flat @ W1_shared)
        routed = jnp.zeros_like(shared)
        for e in range(E):
            routed = routed + h @ W2_experts[e] * w[:, e:e + 1]
        out = x + (shared + routed).reshape(Bb, Tt, C)
        return _rmsnorm(out, norm2_w)
    x = x + _L0_xattn_ref(_layernorm(x, axis=-1), ctx_1024, mask_BxS2_bk1, L0_xattn_Wq, L0_xattn_Wkv, L0_xattn_Wo, L0_xattn_bo)
    x = x + _L0_attn_ref(_layernorm(x, axis=-1), L0_attn_w_cq, L0_attn_g_qnorm, L0_attn_w_dq_nope, L0_attn_w_dq_rope, L0_attn_w_ckv, L0_attn_g_kvnorm, L0_attn_w_dk_nope, L0_attn_w_dv, L0_attn_w_krope, L0_attn_w_imp, L0_attn_w_selk, L0_attn_w_selv, L0_attn_w_wink, L0_attn_w_winv, L0_attn_w_gate, L0_attn_w_proj)
    x = x + _L0_ffn_ref(_layernorm(x, axis=-1), L0_ffn_Wq, L0_ffn_Wk_c, L0_ffn_Wv_c, L0_ffn_Wk, L0_ffn_Wv, L0_ffn_Wo, L0_ffn_W_shared_in, L0_ffn_W_shared_out, L0_ffn_W1_shared, L0_ffn_W2_experts, L0_ffn_Wg_gate, L0_ffn_We_gate, L0_ffn_group_bias, L0_ffn_expert_bias, L0_ffn_norm1_w, L0_ffn_norm2_w)
    return x

_drawn_inputs = setup_inputs


def setup_inputs(seed=0):
    import zlib

    import numpy as np

    out = dict(_drawn_inputs(seed))
    spreads = {'L0_xattn_bo': (0.0, 0.1),
     'L0_attn_g_qnorm': (1.0, 0.6),
     'L0_attn_g_kvnorm': (1.0, 0.6),
     'L0_ffn_group_bias': (0.0, 2.0),
     'L0_ffn_expert_bias': (0.0, 0.8),
     'L0_ffn_norm1_w': (1.0, 0.2),
     'L0_ffn_norm2_w': (1.0, 0.2)}
    factors = {'L0_attn_w_cq': 8.0,
     'L0_attn_w_dq_nope': 8.0,
     'L0_attn_w_dq_rope': 8.0,
     'L0_attn_w_ckv': 7.81,
     'L0_attn_w_dk_nope': 8.0,
     'L0_attn_w_dv': 7.815,
     'L0_attn_w_krope': 8.0,
     'L0_attn_w_selk': 8.0,
     'L0_attn_w_wink': 8.0,
     'L0_attn_w_gate': 6.815,
     'L0_ffn_Wq': 8.0,
     'L0_ffn_Wk_c': 8.0,
     'L0_ffn_Wv_c': 5.557,
     'L0_ffn_Wk': 8.0,
     'L0_ffn_Wv': 5.514,
     'L0_ffn_Wo': 5.642,
     'L0_ffn_W1_shared': 5.355,
     'L0_ffn_W2_experts': 5.337,
     'L0_ffn_Wg_gate': 7.395,
     'L0_ffn_We_gate': 7.617,
     'L0_ffn_W_shared_in': 8.0,
     'L0_ffn_W_shared_out': 8.0}
    for name, (base, spread) in spreads.items():
        noise = np.random.default_rng([zlib.crc32(name.encode()), seed]).standard_normal(out[name].shape)
        drawn = base * np.exp(spread * noise) if base else spread * noise
        out[name] = jnp.asarray(drawn.astype(out[name].dtype))
    for name, factor in factors.items():
        out[name] = (out[name] * factor).astype(out[name].dtype)
    return out
```

```python
from contextlib import ExitStack

import numpy as np
import concourse.bass as bass
from concourse import mybir

F32 = mybir.dt.float32
F32R = mybir.dt.float32r
I32 = mybir.dt.int32
U8 = mybir.dt.uint8
ALU = mybir.AluOpType
ACT = mybir.ActivationFunctionType
AX = mybir.AxisListType

P = 128
B = 8
D = 512
KC = D // P
TOK = B * P
M = 2048
H = 16
DH = 64
INNER = H * DH
PAIRS = H // 2
BLK = 512
BPI = 2
NIT = B * M // (BLK * BPI)
KT = BLK // P
GRP = 4
SLOTS = GRP * KT
SPI = SLOTS * BPI
LAG = 2
VW = DH + 2
GW = 4 * VW
LN_EPS = 1e-5
CLIP = 5.0
EXP_HI = 148.4131591025766
EXP_LO = 0.006737946999085467


RSQRT_GUESS = 0x5F3759DF
RSQRT_STEPS = 11


def rsqrt_column(v, y, x, tmp, done, base):
    v.tensor_scalar(tmp.bitcast(I32), x.bitcast(I32), 1, None, ALU.arith_shift_right).then_inc(done, 1)
    v.wait_ge(done, base + 1)
    v.tensor_scalar(y.bitcast(I32), tmp.bitcast(I32), -1, RSQRT_GUESS, ALU.mult, ALU.add).then_inc(done, 1)
    for n in range(3):
        v.wait_ge(done, base + 2 + 3 * n)
        v.scalar_tensor_tensor(out=tmp, in0=y, scalar=x, in1=y, op0=ALU.mult, op1=ALU.mult).then_inc(done, 1)
        v.wait_ge(done, base + 3 + 3 * n)
        v.tensor_scalar(tmp, tmp, -0.5, 1.5, ALU.mult, ALU.add).then_inc(done, 1)
        v.wait_ge(done, base + 4 + 3 * n)
        v.tensor_tensor(y, y, tmp, ALU.mult).then_inc(done, 1)


LN_STEPS = RSQRT_STEPS + 4


def layernorm_rows(v, out, x, stats, col, done, base):
    v.bn_stats(stats, x).then_inc(done, 1)
    v.wait_ge(done, base + 1)
    v.bn_aggr(col[:, 0:2], stats).then_inc(done, 1)
    v.wait_ge(done, base + 2)
    v.tensor_scalar(col[:, 2:3], col[:, 1:2], LN_EPS, None, ALU.add).then_inc(done, 1)
    v.wait_ge(done, base + 3)
    rsqrt_column(v, col[:, 3:4], col[:, 2:3], col[:, 4:5], done, base + 3)
    v.wait_ge(done, base + 3 + RSQRT_STEPS)
    v.tensor_scalar(out, x, col[:, 0:1], col[:, 3:4], ALU.subtract, ALU.mult).then_inc(done, 1)


def stage_queries(nc, x, wq, ident, q_hi_d, q_lo_d):
    with ExitStack() as ctx:
        sb = lambda n, s, d=F32: ctx.enter_context(nc.sbuf_tensor(n, s, d))
        sem = lambda n: ctx.enter_context(nc.semaphore(n))
        W = sb("qa_w", [P, KC, INNER])
        I = sb("qa_ident", [P, P])
        X = sb("qa_x", [P, 2, D])
        XN = sb("qa_xn", [P, D])
        XT = sb("qa_xt", [P, KC, TOK])
        stats = sb("qa_stats", [P, 6])
        col = sb("qa_col", [P, 5])
        QH = sb("qa_qh", [P, 2, 512], F32R)
        QL = sb("qa_ql", [P, 2, 512], F32R)
        ps_t = ctx.enter_context(nc.psum_tensor("qa_pst", [P, KC, P], F32))
        ps_q = ctx.enter_context(nc.psum_tensor("qa_psq", [P, 2, 512], F32))
        w_in, x_in = sem("qa_w_in"), [sem("qa_x_in0"), sem("qa_x_in1")]
        normed, turned, xt_done = sem("qa_normed"), sem("qa_turned"), sem("qa_xt_done")
        q_done, hi_done, lo_done, q_out = sem("qa_q"), sem("qa_hi"), sem("qa_lo"), [sem("qa_out0"), sem("qa_out1")]
        NQ = PAIRS * (TOK // 512)
        block = ctx.enter_context(nc.Block())

        @block.sync
        def _(sp):
            sp.dma_start(I[:], ident).then_inc(w_in, 16)
            for b in range(2):
                sp.dma_start(X[:, b, :], x[b]).then_inc(x_in[b], 16)
            sp.dma_start(W[:], wq.rearrange("(k p) n -> p k n", p=P)).then_inc(w_in, 16)
            for b in range(2, B):
                sp.wait_ge(normed, LN_STEPS * (b - 1))
                sp.dma_start(X[:, b % 2, :], x[b]).then_inc(x_in[b % 2], 16)
            for n in range(NQ):
                c, h = n // 2, n % 2
                sp.wait_ge(lo_done, n + 1)
                sp.dma_start(q_hi_d[c, :, h * 512:(h + 1) * 512], QH[:, n % 2, :].bitcast(F32)).then_inc(q_out[n % 2], 16)
                sp.dma_start(q_lo_d[c, :, h * 512:(h + 1) * 512], QL[:, n % 2, :].bitcast(F32)).then_inc(q_out[n % 2], 16)
            for n in range(2):
                sp.wait_ge(q_out[n], 16 * NQ)

        @block.vector
        def _(v):
            for b in range(B):
                v.wait_ge(x_in[b % 2], 16 * (b // 2 + 1))
                if b:
                    v.wait_ge(turned, b)
                layernorm_rows(v, XN[:], X[:, b % 2, :], stats[:], col, normed, LN_STEPS * b)
                v.wait_ge(turned, b + 1)
                v.tensor_copy(XT[:, :, b * P:(b + 1) * P], ps_t[:]).then_inc(xt_done, 1)
            for n in range(NQ):
                v.wait_ge(hi_done, n + 1)
                v.tensor_tensor(QL[:, n % 2, :], ps_q[:, n % 2, :], QH[:, n % 2, :].bitcast(F32), ALU.subtract).then_inc(lo_done, 1)

        @block.scalar
        def _(a):
            for n in range(NQ):
                a.wait_ge(q_done, n + 1)
                if n >= 2:
                    a.wait_ge(q_out[n % 2], 32 * (n // 2))
                a.copy(QH[:, n % 2, :], ps_q[:, n % 2, :]).then_inc(hi_done, 1)

        @block.tensor
        def _(t):
            t.wait_ge(w_in, 32)
            for b in range(B):
                t.wait_ge(normed, LN_STEPS * (b + 1))
                if b:
                    t.wait_ge(xt_done, b)
                for k in range(KC):
                    mm = t.transpose(ps_t[:, k, :], XN[:, k * P:(k + 1) * P], I[:])
                mm.then_inc(turned, 1)
            t.wait_ge(xt_done, B)
            for n in range(NQ):
                c, h = n // 2, n % 2
                if n >= 2:
                    t.wait_ge(lo_done, n - 1)
                for k in range(KC):
                    mm = t.matmul(ps_q[:, n % 2, :], W[:, k, c * P:(c + 1) * P], XT[:, k, h * 512:(h + 1) * 512],
                                  start=k == 0, stop=k == KC - 1)
                mm.then_inc(q_done, 1)


def stage_cross(nc, ctx_t, mask, wkv, q_hi_d, q_lo_d, o_part):
    with ExitStack() as ctx:
        sb = lambda n, s, d=F32: ctx.enter_context(nc.sbuf_tensor(n, s, d))
        sem = lambda n: ctx.enter_context(nc.semaphore(n))
        W_hi = sb("w_hi", [P, KC, 2 * INNER], F32R)
        W_lo = sb("w_lo", [P, KC, 2 * INNER], F32R)
        C_hi = sb("c_hi", [P, 2, KC, BLK], F32R)
        C_lo = sb("c_lo", [P, 2, KC, BLK], F32R)
        RAW = sb("raw", [P, 2, KC, BLK])
        K_hi = sb("k_hi", [P, PAIRS, BLK], F32R)
        K_lo = sb("k_lo", [P, PAIRS, BLK], F32R)
        V_hi = sb("v_hi", [P, KT, H, VW], F32R)
        V_lo = sb("v_lo", [P, KT, H, VW], F32R)
        Q_hi = sb("q_hi", [P, PAIRS, 2 * P], F32R)
        Q_lo = sb("q_lo", [P, PAIRS, 2 * P], F32R)
        E = sb("e", [P, 2, 512])
        E_hi = sb("e_hi", [P, 2, 512], F32R)
        E_lo = sb("e_lo", [P, 2, 512], F32R)
        O_sb = sb("o_sb", [P, GW])
        mask_u8 = sb("mask_u8", [P, P], U8)
        top = sb("top", [P, P])
        topi = sb("topi", [P, SPI // GRP])
        ps_s = ctx.enter_context(nc.psum_tensor("ps_s", [P, 2, 512], F32))
        ps_p = ctx.enter_context(nc.psum_tensor("ps_p", [P, 2, 512], F32))
        ps_o = ctx.enter_context(nc.psum_tensor("ps_o", [P, GRP, 512], F32))
        mask_in = sem("mask_in")
        raw_in = [sem("raw_in0"), sem("raw_in1")]
        q_in = [sem(f"q_in{g}") for g in range(GRP)]
        w_hi_done, w_lo_done = sem("w_hi_done"), sem("w_lo_done")
        zeroed, ones_set = sem("zeroed"), sem("ones_set")
        top_done, topi_done = sem("top_done"), sem("topi_done")
        chi_done, clo_done = sem("chi_done"), sem("clo_done")
        proj_done = sem("proj_done")
        kv_hi, kv_lo = sem("kv_hi"), sem("kv_lo")
        scored, expd, clipped = sem("scored"), sem("expd"), sem("clipped")
        e_hi, e_lo = sem("e_hi_done"), sem("e_lo_done")
        pv_done = sem("pv_done")
        o_copied, o_out = sem("o_copied"), sem("o_out")
        block = ctx.enter_context(nc.Block())

        K, V = "K", "V"
        AHEAD = [(K, c) for c in range(6)] + [(V, 0, t) for t in range(KT)]
        IN_SLOT = {0: (K, 6, 0), 1: (K, 7, 0), 2: (V, 1, 0, 0), 3: (V, 1, 1, 0), 6: (V, 1, 2, 0), 7: (V, 1, 3, 0),
                   4: (K, 0, 1), 5: (K, 1, 1), 8: (K, 2, 1), 9: (K, 3, 1), 12: (K, 4, 1), 13: (K, 5, 1),
                   10: (V, 0, 0, 1), 11: (V, 0, 1, 1), 14: (V, 0, 2, 1), 15: (V, 0, 3, 1)}
        NA = len(AHEAD)
        SPLIT_SLOT = 10

        def group_of(s):
            g = IN_SLOT[s % SLOTS]
            return g[:-1], (s // SLOTS + g[-1]) % 2

        def has_group(s, last):
            return not (last and s >= SLOTS and IN_SLOT[s % SLOTS][-1])

        def before(s, last):
            return sum(has_group(x, last) for x in range(s))

        def has_split(s, last):
            return not last and SPLIT_SLOT <= s % SLOTS < SPLIT_SLOT + KC

        def over_iterations(eng, body):
            body(0, True, False)
            with eng.Fori(1, NIT - 1) as i:
                body(i, False, False)
            body(NIT - 1, False, True)

        @block.sync
        def _(sp):
            sp.dma_start(mask_u8[:], mask).then_inc(mask_in, 16)
            for k in range(KC):
                if k >= 2:
                    sp.wait_ge(w_lo_done, k - 1)
                sp.dma_start(RAW[:, k % 2].rearrange("p k f -> p (k f)"), wkv[k * P:(k + 1) * P, :]).then_inc(raw_in[k % 2], 16)
            for n in range(2):
                sp.wait_ge(w_lo_done, KC - 1 + n)
                sp.dma_start(RAW[:, n], ctx_t[n]).then_inc(raw_in[n], 16)

            def queries(i, g):
                b0 = (i // 2) * P
                for par, (dst, src) in enumerate(((Q_hi, q_hi_d), (Q_lo, q_lo_d))):
                    for hh in range(2):
                        sp.dma_start(dst[hh * DH:(hh + 1) * DH, 2 * g:2 * g + 2, hh * P:(hh + 1) * P].bitcast(F32),
                                     src[2 * g:2 * g + 2, hh * DH:(hh + 1) * DH, bass.ds(b0, P)].rearrange("c p t -> p c t")
                                     ).then_inc(q_in[g], 16)
            sp.wait_ge(zeroed, 2)
            for g in range(GRP):
                queries(0, g)

            def body(i, first, last):
                for s in range(SPI):
                    S = i * SPI + s
                    blk, r = divmod(s, SLOTS)
                    if r == 0 and not last:
                        sp.wait_ge(clo_done, KC * (2 * i + blk + 1))
                        nxt = 2 * i + blk + 2
                        sp.dma_start(RAW[:, blk], ctx_t[bass.ds(nxt, 1)].rearrange("o p k f -> (o p) k f")).then_inc(raw_in[blk], 16)
                    if not last and s >= SLOTS and r % KT == KT - 1:
                        sp.wait_ge(scored, S + 1)
                        queries(i + 1, r // KT)
                    g = (s - SLOTS - KT - LAG + 1)
                    if (g >= 0 and g % KT == 0 and g // KT < GRP - 1) or (s == LAG - 1 and not first):
                        gg = GRP - 1 if s < SLOTS else g // KT
                        ii = i - 1 if s < SLOTS else i
                        sp.wait_ge(o_copied, GRP * ii + gg + 1)
                        sp.dma_start(o_part[bass.ds(ii, 1), :, gg].rearrange("o p f -> (o p) f"), O_sb[:]).then_inc(o_out, 16)
            over_iterations(sp, body)
            sp.wait_ge(o_copied, GRP * NIT)
            sp.dma_start(o_part[NIT - 1, :, GRP - 1], O_sb[:]).then_inc(o_out, 16)
            sp.wait_ge(o_out, 16 * GRP * NIT)

        @block.gpsimd
        def _(g):
            for Q in (Q_hi, Q_lo):
                g.memset(Q[:].bitcast(F32), 0.0).then_inc(zeroed, 1)
            for n in range(2):
                for k in range(KC):
                    g.wait_ge(chi_done, KC * n + k + 1)
                    g.tensor_tensor(C_lo[:, n, k, :], RAW[:, n, k, :], C_hi[:, n, k, :].bitcast(F32),
                                    ALU.subtract).then_inc(clo_done, 1)

            def body(i, first, last):
                for s in range(SPI):
                    S = i * SPI + s
                    if has_split(s, last):
                        blk, k = s // SLOTS, s % SLOTS - SPLIT_SLOT
                        g.wait_ge(chi_done, KC * (2 * i + blk + 2) + k + 1)
                        g.tensor_tensor(C_lo[:, blk, k, :], RAW[:, blk, k, :], C_hi[:, blk, k, :].bitcast(F32),
                                        ALU.subtract).then_inc(clo_done, 1)
                    g.wait_ge(e_hi, S + 1)
                    g.tensor_tensor(E_lo[:, s % 2, :], E[:, s % 2, :], E_hi[:, s % 2, :].bitcast(F32), ALU.subtract
                                    ).then_inc(e_lo, 1)
            over_iterations(g, body)

        def kv_slice(hi, kind):
            if kind[0] == K:
                return (K_hi if hi else K_lo)[:, kind[1], :]
            return (V_hi if hi else V_lo)[:, kind[2], 8 * kind[1]:8 * kind[1] + 8, 0:DH]

        def ps_view(G, kind):
            out = ps_p[:, G % 2, :]
            return out if kind[0] == K else out.rearrange("p (h d) -> p h d", d=DH)

        @block.scalar
        def _(a):
            def evac_hi(par, kind, value):
                a.wait_ge(proj_done, value)
                a.copy(kv_slice(True, kind), ps_view(par, kind)).then_inc(kv_hi, 1)

            for k in range(KC):
                a.wait_ge(raw_in[k % 2], 16 * (k // 2 + 1))
                a.copy(W_hi[:, k], RAW[:, k % 2].rearrange("p k f -> p (k f)")).then_inc(w_hi_done, 1)
            for n in range(2):
                a.wait_ge(raw_in[n], 16 * 3)
                for k in range(KC):
                    a.copy(C_hi[:, n, k, :], RAW[:, n, k, :]).then_inc(chi_done, 1)
            for G, kind in enumerate(AHEAD):
                evac_hi(G, kind, G + 1)

            def body(i, first, last):
                for s in range(SPI):
                    S = i * SPI + s
                    if s and has_group(s - 1, last):
                        n = before(s, last)
                        evac_hi(n - 1, group_of(s - 1)[0], NA + i * SPI + n)
                    a.wait_ge(scored, S + 1)
                    if not (first and s < 2):
                        a.wait_ge(e_lo, S - 1)
                    a.activation(E[:, s % 2, :], ps_s[:, s % 2, :], ACT.Exp, scale=DH ** -0.5).then_inc(expd, 1)
                    if has_split(s, last):
                        blk, k = s // SLOTS, s % SLOTS - SPLIT_SLOT
                        if k == 0:
                            a.wait_ge(raw_in[blk], 16 * (i + 4))
                            a.wait_ge(proj_done, NA + S - 2)
                        a.copy(C_hi[:, blk, k, :], RAW[:, blk, k, :]).then_inc(chi_done, 1)
                    g = s - SLOTS - KT - LAG + 1
                    if g >= 0 and g % KT == 0 and g // KT < GRP - 1:
                        copy_out(g // KT, i, S)
                    if s == LAG - 1 and not first:
                        copy_out(GRP - 1, i - 1, S)
                if not last:
                    evac_hi(SPI - 1, group_of(SPI - 1)[0], NA + S + 1)

            def copy_out(gg, i, S):
                a.wait_ge(pv_done, S - LAG + 1)
                n = GRP * i + gg
                if not isinstance(n, int) or n > 0:
                    a.wait_ge(o_out, 16 * n)
                a.copy(O_sb[:], ps_o[:, gg, 0:GW]).then_inc(o_copied, 1)
            over_iterations(a, body)
            copy_out(GRP - 1, NIT - 1, SPI * NIT + LAG - 1)

        @block.vector
        def _(v):
            for k in range(KC):
                v.wait_ge(w_hi_done, k + 1)
                v.tensor_tensor(W_lo[:, k], RAW[:, k % 2].rearrange("p k f -> p (k f)"), W_hi[:, k].bitcast(F32),
                                ALU.subtract).then_inc(w_lo_done, 1)
            v.memset(V_hi[:].bitcast(F32), 1.0).then_inc(ones_set, 1)
            v.memset(V_lo[:].bitcast(F32), 0.0).then_inc(ones_set, 1)
            v.wait_ge(ones_set, 2)
            v.memset(V_hi[:, :, :, DH + 1:VW].bitcast(F32), 0.0).then_inc(ones_set, 1)
            v.wait_ge(mask_in, 16)
            v.tensor_scalar(top[:], mask_u8[:], EXP_HI - EXP_LO, EXP_LO, ALU.mult, ALU.add).then_inc(top_done, 1)
            v.wait_ge(top_done, 1)

            def evac_lo(par, kind, value):
                v.wait_ge(kv_hi, value)
                v.tensor_tensor(kv_slice(False, kind), ps_view(par, kind), kv_slice(True, kind).bitcast(F32),
                                ALU.subtract).then_inc(kv_lo, 1)
            for G, kind in enumerate(AHEAD):
                evac_lo(G, kind, G + 1)

            def body(i, first, last):
                n0 = i * (SPI // GRP)
                for s in range(SPI):
                    S = i * SPI + s
                    if s == 0:
                        v.tensor_copy(topi[:], top[:, bass.ds(n0, SPI // GRP)]).then_inc(topi_done, 1)
                        v.wait_ge(topi_done, i + 1)
                    if s and has_group(s - 1, last):
                        n = before(s, last)
                        evac_lo(n - 1, group_of(s - 1)[0], NA + i * SPI + n)
                    kt = (s // SLOTS) * KT + s % KT
                    v.wait_ge(expd, S + 1)
                    v.tensor_scalar(E[:, s % 2, :], E[:, s % 2, :], topi[:, kt:kt + 1], EXP_LO, ALU.min, ALU.max
                                    ).then_inc(clipped, 1)
                    if not (first and s < LAG):
                        v.wait_ge(pv_done, S - 1)
                    v.wait_ge(clipped, S + 1)
                    v.tensor_copy(E_hi[:, s % 2, :], E[:, s % 2, :]).then_inc(e_hi, 1)
                if not last:
                    evac_lo(SPI - 1, group_of(SPI - 1)[0], NA + S + 1)
            over_iterations(v, body)

        @block.tensor
        def _(t):
            def project(kind, cb, par):
                n = 0
                for k in range(KC):
                    for w, c in ((W_lo, C_hi), (W_hi, C_lo), (W_hi, C_hi)):
                        if kind[0] == K:
                            lhs, rhs = w[:, k, kind[1] * P:(kind[1] + 1) * P], c[:, cb, k, :]
                        else:
                            lhs = c[:, cb, k, kind[2] * P:(kind[2] + 1) * P]
                            rhs = w[:, k, INNER + kind[1] * 512:INNER + (kind[1] + 1) * 512]
                        mm = t.matmul(ps_p[:, par % 2, :], lhs, rhs, start=n == 0, stop=n == 3 * KC - 1)
                        n += 1
                mm.then_inc(proj_done, 1)

            def values(s, value):
                s = s % SPI
                g, kt = s % SLOTS // KT, s % KT
                t.wait_ge(e_lo, value)
                for j in range(4):
                    h = 4 * g + j
                    for n, (e, vv) in enumerate(((E_lo, V_hi), (E_hi, V_lo), (E_hi, V_hi))):
                        mm = t.matmul(ps_o[:, g, j * VW:(j + 1) * VW], e[:, s % 2, j * P:(j + 1) * P], vv[:, kt, h, :],
                                      start=(s < SLOTS and kt == 0 and j == 0 and n == 0),
                                      stop=(s >= SLOTS and kt == KT - 1 and n == 2), skip_group_check=True)
                mm.then_inc(pv_done, 1)

            t.wait_ge(w_lo_done, KC)
            t.wait_ge(clo_done, KC)
            for G, kind in enumerate(AHEAD):
                if G >= 2:
                    t.wait_ge(kv_lo, G - 1)
                project(kind, 0, G)
            t.wait_ge(ones_set, 3)
            t.wait_ge(zeroed, 2)

            def body(i, first, last):
                for s in range(SPI):
                    S = i * SPI + s
                    g, kt = s % SLOTS // KT, s % KT
                    t.wait_ge(kv_lo, NA + i * SPI + (before(s - 1, last) if s else -1))
                    if s < SLOTS and kt == 0:
                        t.wait_ge(q_in[g], 64 * (i + 1))
                    if not (first and s < 2):
                        t.wait_ge(expd, S - 1)
                    for pr in range(2):
                        c = 2 * g + pr
                        for n, (k_, q_) in enumerate(((K_lo, Q_hi), (K_hi, Q_lo), (K_hi, Q_hi))):
                            mm = t.matmul(ps_s[:, s % 2, pr * 256:(pr + 1) * 256], k_[:, c, kt * P:(kt + 1) * P],
                                          q_[:, c, :], start=n == 0, stop=n == 2)
                    mm.then_inc(scored, 1)
                    if has_group(s, last):
                        kind, cb = group_of(s)
                        if s % SLOTS == 4:
                            t.wait_ge(clo_done, KC * (2 * i + s // SLOTS + 2))
                        project(kind, cb, before(s, last))
                    if not (first and s < LAG):
                        u = s - LAG
                        if s % SPI >= LAG and u < SLOTS and u % KT == 0:
                            if not first:
                                t.wait_ge(o_copied, GRP * (i - 1) + u // KT + 1)
                        values(u, S - LAG + 1)

            over_iterations(t, body)
            for s in range(SPI - LAG, SPI):
                values(s, SPI * (NIT - 1) + s + 1)

NOPE, ROPE, VH = 32, 64, 32
QK = NOPE + ROPE
QL, KVL = 96, 32
NEG = -3.0e38
RMS_EPS = 1e-6


class Chain:

    def __init__(self, eng, sem, i, length):
        self.eng, self.sem, self.i, self.length, self.n = eng, sem, i, length, 0

    def link(self, ins):
        self.n += 1
        ins.then_inc(self.sem, 1)
        self.eng.wait_ge(self.sem, self.i * self.length + self.n)

    def end(self):
        assert self.n == self.length, self.n


def rsqrt_cols(v, c, y, x, tmp):
    c.link(v.tensor_scalar(tmp.bitcast(I32), x.bitcast(I32), 1, None, ALU.arith_shift_right))
    c.link(v.tensor_scalar(y.bitcast(I32), tmp.bitcast(I32), -1, RSQRT_GUESS, ALU.mult, ALU.add))
    for n in range(3):
        c.link(v.tensor_tensor(tmp, y, y, ALU.mult))
        c.link(v.tensor_tensor(tmp, tmp, x, ALU.mult))
        c.link(v.tensor_scalar(tmp, tmp, -0.5, 1.5, ALU.mult, ALU.add))
        c.link(v.tensor_tensor(y, y, tmp, ALU.mult))


def moments(v, c, out, x, stats, carry):
    c.link(v.bn_stats(stats, x))
    v.tensor_copy(carry, stats[:, 0:1])
    c.link(v.bn_aggr(out, stats))


def layernorm(v, c, out, x, stats, col):
    moments(v, c, col[:, 0:2], x, stats, col[:, 5:6])
    c.link(v.tensor_scalar(col[:, 2:3], col[:, 1:2], LN_EPS, None, ALU.add))
    rsqrt_cols(v, c, col[:, 3:4], col[:, 2:3], col[:, 4:5])
    c.link(v.tensor_scalar(out, x, col[:, 0:1], col[:, 3:4], ALU.subtract, ALU.mult))


def heads(ap, h):
    return ap.rearrange("p (h d) -> p h d", h=h)


def stage_middle(nc, x, o_part, x2_d, wts, tables):
    (wo, bo, w_cq, g_q, w_dqn, w_dqr, w_ckv, g_kv, w_dkn, w_dv, w_kr, w_selk, w_selv, w_wink, w_winv, w_gate, w_proj) = wts
    ident, rope, causal = tables
    with ExitStack() as ctx:
        sb = lambda n, s, d=F32: ctx.enter_context(nc.sbuf_tensor("m_" + n, s, d))
        sem = lambda n: ctx.enter_context(nc.semaphore("m_" + n))
        I = sb("ident", [P, P])
        ROPE_T = sb("rope", [P, 2, ROPE])
        CAUSAL = sb("causal", [P, 3, P])
        MEAN = sb("mean", [P, P])
        BO = sb("bo", [P, D])
        GQ = sb("gq", [P, QL + KVL])
        WO = sb("wo", [P, INNER // P, D])
        NS = QL + KVL + ROPE + 3
        WS = sb("ws", [P, KC, NS])
        SELK = sb("selk", [P, KC, H * QK])
        WINK = sb("wink", [P, KC, H * QK])
        VV = sb("vv", [P, KC, 2 * D])
        DQ = sb("dq", [QL, H * QK])
        DK = sb("dk", [KVL, 2 * H * VH])
        PROJ = sb("proj", [P, KC, D])
        OP = sb("op", [P, 2, GRP * GW])
        R1 = OP[:, 0, 0:H * ROPE].rearrange("p (h d) -> p h d", h=H)
        R2 = OP[:, 1, 0:H * ROPE].rearrange("p (h d) -> p h d", h=H)
        X = sb("x", [P, D])
        REC = sb("rec", [P, H])
        X1 = sb("x1", [P, D])
        XN = sb("xn", [P, D])
        XT = sb("xt", [P, KC, P])
        stats = sb("stats", [P, 2, 6])
        col = sb("col", [P, 16])
        S3 = sb("s3", [P, NS])
        NQ = sb("nq", [P, QL + KVL])
        NQT = sb("nqt", [QL, 2, P])
        KR = sb("kr", [P, 2, ROPE])
        Q = sb("q", [P, H, QK])
        K1 = sb("k1", [P, H, QK])
        KS = sb("ks", [P, H, QK])
        KW = sb("kw", [P, H, QK])
        ON = Q[:].rearrange("p h d -> p (h d)")[:, 0:INNER].rearrange("p (h d) -> p h d", h=H)
        OT = KW[:].rearrange("p h d -> p (h d)")[:, 0:INNER].rearrange("p (k f) -> p k f", f=P)
        V3 = sb("v3", [P, 3, D])
        QT = sb("qt", [QK, H, P])
        K3T = sb("k3t", [QK, H, 3, P])
        S = sb("s", [P, 4, 3, P])
        mx = sb("mx", [P, 12])
        sm = sb("sm", [P, 12])
        gate = sb("gate", [P, 6])
        PT = sb("pt", [P, 4, 3, P])
        O2 = sb("o2", [P, D])
        O2T = sb("o2t", [P, KC, P])
        X2 = sb("x2", [P, D])
        ps = ctx.enter_context(nc.psum_tensor("m_ps", [P, 8 * 512], F32))

        def bank(n, w=512, rows=P):
            return ps[0:rows, n * 512:n * 512 + w]

        sems = {}

        def done(n):
            if n not in sems:
                sems[n] = sem(n)
            return sems[n]

        const_in, consts_in, loaded, x2_out = done("const_in"), done("consts_in"), done("loaded"), done("x2_out")
        setup, vchain, kchain = done("setup"), done("vchain"), done("kchain")
        o_normed, x_normed, s3_copied, nq_done, nqt_copied = done("o_normed"), done("x_normed"), done("s3_copied"), done("nq_done"), done("nqt_copied")
        gate_shifted, kw_copied, kw_roped, k1_roped, q_roped = done("gate_shifted"), done("kw_copied"), done("kw_roped"), done("k1_roped"), done("q_roped")
        odd_copied, s_read, s_shifted, p_done, x2_done = done("odd_copied"), done("s_read"), done("s_shifted"), done("p_done"), done("x2_done")
        xo_read = done("xo_read")
        ks_roped = done("ks_roped")
        ot_copied, xt_copied, vv_copied, ks_copied, gate_expd = done("ot_copied"), done("xt_copied"), done("vv_copied"), done("ks_copied"), done("gate_expd")
        q_copied, k1_copied, even_copied, s_expd, pt_copied = done("q_copied"), done("k1_copied"), done("even_copied"), done("s_expd"), done("pt_copied")
        o2_copied, o2t_copied = done("o2_copied"), done("o2t_copied")
        o_turned, xo_done, x_turned, s3_done, gate_done = done("o_turned"), done("xo_done"), done("x_turned"), done("s3_done"), done("gate_done")
        vv_done, ks_done, kw_done, nq_turned, q_done, k1_done = done("vv_done"), done("ks_done"), done("kw_done"), done("nq_turned"), done("q_done"), done("k1_done")
        heads_turned, s_done, p_turned, pv_done, o2_turned, y_done = done("heads_turned"), done("s_done"), done("p_turned"), done("pv_done"), done("o2_turned"), done("y_done")
        block = ctx.enter_context(nc.Block())
        GROUPS = H // 4
        NC = 19
        TURNS = [(T, g) for T in ("ks", "kw", "k1", "q") for g in range(GROUPS)]

        def turned_from(n):
            return bank(4 + n % 4, 512, QK).rearrange("p (h f) -> p h f", h=4)

        def turned_to(T, g):
            if T == "q":
                return QT[:, 4 * g:4 * g + 4, :]
            return K3T[:, 4 * g:4 * g + 4, ("k1", "ks", "kw").index(T), :]

        @block.sync
        def _(sp):
            sp.dma_start(I[:], ident).then_inc(const_in, 16)
            rows = lambda w: w.rearrange("(k p) n -> p k n", p=P)
            pieces = ((ROPE_T[:], rope), (CAUSAL[:], causal), (BO[:], bo.partition_broadcast(P)),
                      (GQ[:, 0:QL], g_q.partition_broadcast(P)), (GQ[:, QL:QL + KVL], g_kv.partition_broadcast(P)),
                      (WO[:], rows(wo)), (WS[:, :, 0:QL], rows(w_cq)), (WS[:, :, QL:QL + KVL], rows(w_ckv)),
                      (WS[:, :, QL + KVL:NS - 3], rows(w_kr)), (WS[:, :, NS - 3:NS], rows(w_gate)),
                      (VV[:, :, 0:D], rows(w_selv)), (VV[:, :, D:2 * D], rows(w_winv)), (SELK[:], rows(w_selk)),
                      (WINK[:], rows(w_wink)), (DQ[:, 0:H * NOPE], w_dqn), (DQ[:, H * NOPE:], w_dqr),
                      (DK[:, 0:H * NOPE], w_dkn), (DK[:, H * NOPE:], w_dv), (PROJ[:], rows(w_proj)))
            assert len(pieces) == NC
            for dst, src in pieces:
                sp.dma_start(dst, src).then_inc(consts_in, 16)
            sp.sem_inc(x2_done, 1)
            sp.sem_inc(x2_out, 16)
            with sp.Fori(0, B) as b:
                sp.wait_ge(x2_done, b + 1)
                for h in range(2):
                    sp.dma_start(OP[:, h, :], o_part[bass.ds(2 * b + h, 1)].rearrange("o p g f -> (o p) (g f)")).then_inc(loaded, 16)
                sp.dma_start(X[:], x[bass.ds(b, 1)].rearrange("o p f -> (o p) f")).then_inc(loaded, 16)
                sp.wait_ge(x2_done, b + 2)
                sp.dma_start(x2_d[bass.ds(b, 1)].rearrange("o p f -> (o p) f"), X2[:]).then_inc(x2_out, 16)
            sp.wait_ge(x2_out, 16 * (B + 1))

        def rope_rows(eng, link, x_, r1, r2):
            n, R = x_.shape[1], ROPE // 2
            link(eng.tensor_tensor(r1, x_, ROPE_T[:, 0:1, :].broadcast_to([P, n, ROPE]), ALU.mult))
            link(eng.tensor_tensor(r2, x_, ROPE_T[:, 1:2, :].broadcast_to([P, n, ROPE]), ALU.mult))
            link(eng.tensor_tensor(x_[:, :, 0:R], r1[:, :, 0:R], r2[:, :, R:], ALU.add))
            return eng.tensor_tensor(x_[:, :, R:], r1[:, :, R:], r2[:, :, 0:R], ALU.add)

        @block.gpsimd
        def _(g):
            g.memset(MEAN[:], 1.0 / P).then_inc(setup, 1)
            g.wait_ge(consts_in, 16 * NC)
            with g.Fori(0, B) as b:
                c = Chain(g, kchain, b, 3)
                g.wait_ge(ks_copied, b + 1)
                rope_rows(g, c.link, KS[:, :, NOPE:], R1, R2).then_inc(ks_roped, 1)
                c.end()

        @block.vector
        def _(v):
            v.wait_ge(consts_in, 16 * NC)
            O16 = OP[:, 0, :].rearrange("p (h d) -> p h d", h=H)
            SF = S[:].rearrange("p a b f -> p (a b f)")
            PF = PT[:].rearrange("p a b f -> p (a b f)")
            VR1, VR2 = (heads(t[:, 0:H * ROPE], H) for t in (SF, PF))
            S12 = S[:].rearrange("p a b f -> p (a b) f")
            with v.Fori(0, B) as b:
                c = Chain(v, vchain, b, 72)
                link = c.link
                v.wait_ge(loaded, 48 * (b + 1))
                link(v.tensor_tensor(OP[:, 0, :], OP[:, 0, :], OP[:, 1, :], ALU.add))
                link(v.reciprocal(REC[:], O16[:, :, DH]))
                link(v.tensor_tensor(X[:], X[:], BO[:], ALU.add))
                v.tensor_tensor(ON, O16[:, :, 0:DH], REC[:].unsqueeze(2).broadcast_to([P, H, DH]), ALU.mult).then_inc(o_normed, 1)
                v.wait_ge(xo_done, b + 1)
                v.tensor_tensor(X1[:], bank(2), X[:], ALU.add).then_inc(xo_read, 1)
                v.wait_ge(xo_read, b + 1)
                moments(v, c, col[:, 0:2], X1[:], stats[:, 0], col[:, 15:16])
                link(v.tensor_scalar(col[:, 2:3], col[:, 1:2], LN_EPS, None, ALU.add))
                rsqrt_cols(v, c, col[:, 3:4], col[:, 2:3], col[:, 4:5])
                v.tensor_scalar(XN[:], X1[:], col[:, 0:1], col[:, 3:4], ALU.subtract, ALU.mult).then_inc(x_normed, 1)
                v.wait_ge(s3_done, b + 1)
                v.tensor_copy(S3[:], bank(4, NS)).then_inc(s3_copied, 1)
                v.wait_ge(s3_copied, b + 1)
                moments(v, c, col[:, 0:2], S3[:, 0:QL], stats[:, 0], col[:, 15:16])
                moments(v, c, col[:, 2:4], S3[:, QL:QL + KVL], stats[:, 1], col[:, 15:16])
                means, vars_ = (col[:, 0:4].rearrange("p (a t) -> p t a", t=2)[:, t] for t in range(2))
                link(v.tensor_tensor(col[:, 4:6], means, means, ALU.mult))
                link(v.tensor_tensor(col[:, 4:6], col[:, 4:6], vars_, ALU.add))
                link(v.tensor_scalar(col[:, 4:6], col[:, 4:6], RMS_EPS, None, ALU.add))
                rsqrt_cols(v, c, col[:, 6:8], col[:, 4:6], col[:, 8:10])
                link(v.scalar_tensor_tensor(out=NQ[:, 0:QL], in0=S3[:, 0:QL], scalar=col[:, 6:7], in1=GQ[:, 0:QL],
                                            op0=ALU.mult, op1=ALU.mult))
                v.scalar_tensor_tensor(out=NQ[:, QL:], in0=S3[:, QL:QL + KVL], scalar=col[:, 7:8], in1=GQ[:, QL:],
                                       op0=ALU.mult, op1=ALU.mult).then_inc(nq_done, 1)
                v.wait_ge(nq_turned, b + 1)
                v.tensor_copy(NQT[:, 0, :], bank(6, P, QL)).then_inc(nqt_copied, 1)
                v.tensor_copy(NQT[0:KVL, 1, :], bank(6, 2 * P, KVL)[:, P:]).then_inc(nqt_copied, 1)
                KRV = S3[:, QL + KVL:NS - 3].unsqueeze(1)
                link(rope_rows(v, link, KRV, KR[:, 0:1, :], KR[:, 1:2, :]))
                v.wait_ge(gate_done, b + 1)
                link(v.tensor_reduce(col[:, 10:11], bank(7, 3), AX.X, ALU.max))
                v.tensor_scalar(gate[:, 0:3], bank(7, 3), col[:, 10:11], None, ALU.subtract).then_inc(gate_shifted, 1)
                v.wait_ge(kw_done, b + 1)
                v.tensor_copy(KW[:].rearrange("p h d -> p (h d)"), ps[:, 3 * 512:6 * 512]).then_inc(kw_copied, 1)
                v.wait_ge(kw_copied, b + 1)
                rope_rows(v, link, KW[:, :, NOPE:], VR1, VR2).then_inc(kw_roped, 1)
                v.wait_ge(gate_expd, b + 1)
                link(v.tensor_reduce(col[:, 11:12], gate[:, 3:6], AX.X, ALU.add))
                link(v.reciprocal(col[:, 12:13], col[:, 11:12]))
                link(v.tensor_scalar(gate[:, 0:3], gate[:, 3:6], col[:, 12:13], None, ALU.mult))
                v.tensor_scalar(K1[:, :, NOPE:], KRV.broadcast_to([P, H, ROPE]), 1.0 / H, None, ALU.mult).then_inc(k1_roped, 1)
                v.wait_ge(q_copied, 2 * b + 2)
                v.wait_ge(kw_roped, b + 1)
                rope_rows(v, link, Q[:, :, NOPE:], VR1, VR2).then_inc(q_roped, 1)
                for n, (T, g) in enumerate(TURNS):
                    if n % 2:
                        v.wait_ge(heads_turned, 16 * b + n + 1)
                        v.tensor_copy(turned_to(T, g), turned_from(n)).then_inc(odd_copied, 1)
                v.wait_ge(q_roped, b + 1)
                for g in range(GROUPS):
                    v.wait_ge(s_done, GROUPS * b + g + 1)
                    if g:
                        v.wait_ge(p_turned, GROUPS * b + g)
                    v.tensor_tensor(S[:].rearrange("p a b f -> p a (b f)"), ps[:, 0:4 * 512].rearrange("p (a f) -> p a f", a=4)[:, :, 0:3 * P],
                                    CAUSAL[:].rearrange("p b f -> p (b f)").unsqueeze(1).broadcast_to([P, 4, 3 * P]), ALU.add).then_inc(s_read, 1)
                    v.wait_ge(s_read, GROUPS * b + g + 1)
                    link(v.tensor_reduce(mx[:], S12, AX.X, ALU.max))
                    v.tensor_tensor(S12, S12, mx[:].unsqueeze(2).broadcast_to([P, 12, P]), ALU.subtract).then_inc(s_shifted, 1)
                    v.wait_ge(s_expd, GROUPS * b + g + 1)
                    link(v.tensor_reduce(sm[:], S12, AX.X, ALU.add))
                    link(v.reciprocal(sm[:], sm[:]))
                    sm4 = sm[:].rearrange("p (a b) -> p a b", b=3)
                    link(v.tensor_tensor(sm4, sm4, gate[:, 0:3].unsqueeze(1).broadcast_to([P, 4, 3]), ALU.mult))
                    v.tensor_tensor(S12, S12, sm[:].unsqueeze(2).broadcast_to([P, 12, P]), ALU.mult).then_inc(p_done, 1)
                v.wait_ge(y_done, b + 1)
                v.wait_ge(x2_out, 16 * (b + 1))
                v.tensor_tensor(X2[:], bank(1), X1[:], ALU.add).then_inc(x2_done, 1)
                c.end()

        @block.scalar
        def _(a):
            with a.Fori(0, B) as b:
                a.wait_ge(o_turned, b + 1)
                a.copy(OT.rearrange("p k f -> p (k f)"), ps[:, 0:2 * 512]).then_inc(ot_copied, 1)
                a.wait_ge(x_turned, b + 1)
                a.copy(XT[:].rearrange("p k f -> p (k f)"), bank(3)).then_inc(xt_copied, 1)
                a.wait_ge(vv_done, b + 1)
                a.copy(V3[:, 1:3, :].rearrange("p k f -> p (k f)"), ps[:, 6 * 512:8 * 512]).then_inc(vv_copied, 1)
                a.wait_ge(ks_done, b + 1)
                a.copy(KS[:].rearrange("p h d -> p (h d)"), ps[:, 0:3 * 512]).then_inc(ks_copied, 1)
                a.wait_ge(gate_shifted, b + 1)
                a.activation(gate[:, 3:6], gate[:, 0:3], ACT.Exp).then_inc(gate_expd, 1)
                a.wait_ge(q_done, b + 1)
                a.copy(Q[:, :, 0:NOPE], heads(bank(0), H)).then_inc(q_copied, 1)
                a.copy(Q[:, :, NOPE:], heads(ps[:, 512:3 * 512], H)).then_inc(q_copied, 1)
                a.wait_ge(k1_done, b + 1)
                a.copy(K1[:, :, 0:NOPE], heads(bank(3), H)).then_inc(k1_copied, 1)
                a.copy(V3[:, 0, :], bank(4)).then_inc(k1_copied, 1)
                for n, (T, g) in enumerate(TURNS):
                    if n % 2 == 0:
                        a.wait_ge(heads_turned, 16 * b + n + 1)
                        a.copy(turned_to(T, g), turned_from(n)).then_inc(even_copied, 1)
                for g in range(GROUPS):
                    a.wait_ge(s_shifted, GROUPS * b + g + 1)
                    SF = S[:].rearrange("p a b f -> p (a b f)")
                    a.activation(SF, SF, ACT.Exp, scale=QK ** -0.5).then_inc(s_expd, 1)
                    a.wait_ge(p_turned, GROUPS * b + g + 1)
                    if g:
                        a.wait_ge(pv_done, GROUPS * b + g)
                    a.copy(PT[:].rearrange("p a b f -> p (a b f)"), ps[:, 4 * 512:7 * 512]).then_inc(pt_copied, 1)
                a.wait_ge(pv_done, GROUPS * (b + 1))
                a.copy(O2[:], bank(7)).then_inc(o2_copied, 1)
                a.wait_ge(o2_turned, b + 1)
                a.copy(O2T[:].rearrange("p k f -> p (k f)"), bank(0)).then_inc(o2t_copied, 1)

        @block.tensor
        def _(t):
            t.wait_ge(const_in, 16)
            t.wait_ge(consts_in, 16 * NC)
            t.wait_ge(setup, 1)

            def rows_times(bank0, lhs, w, n_k, n0, n1):
                for j in range(n0, n1, 512):
                    e = min(j + 512, n1)
                    for k in range(n_k):
                        mm = t.matmul(bank(bank0 + (j - n0) // 512, e - j), lhs[:, k, :], w[:, k, j:e],
                                      start=k == 0, stop=k == n_k - 1)
                return mm

            def turn(outs, src, w=P):
                for k, o in enumerate(outs):
                    mm = t.transpose(o, src(k), I[:])
                return mm

            with t.Fori(0, B) as b:
                t.wait_ge(x2_done, b + 1)
                t.wait_ge(o_normed, b + 1)
                ONF = ON.rearrange("p h d -> p (h d)")
                turn([ps[:, k * P:(k + 1) * P] for k in range(8)], lambda k: ONF[:, k * P:(k + 1) * P]).then_inc(o_turned, 1)
                t.wait_ge(ot_copied, b + 1)
                rows_times(2, OT, WO, INNER // P, 0, D).then_inc(xo_done, 1)
                t.wait_ge(x_normed, b + 1)
                turn([ps[:, 3 * 512 + k * P:3 * 512 + (k + 1) * P] for k in range(KC)], lambda k: XN[:, k * P:(k + 1) * P]).then_inc(x_turned, 1)
                t.wait_ge(xt_copied, b + 1)
                rows_times(4, XT, WS, KC, 0, NS).then_inc(s3_done, 1)
                rows_times(6, XT, VV, KC, 0, 2 * D).then_inc(vv_done, 1)
                t.wait_ge(xo_read, b + 1)
                rows_times(0, XT, SELK, KC, 0, H * QK).then_inc(ks_done, 1)
                t.wait_ge(s3_copied, b + 1)
                rows_times(3, XT, WINK, KC, 0, H * QK).then_inc(kw_done, 1)
                t.wait_ge(vv_copied, b + 1)
                t.matmul(bank(7, 3), MEAN[:], S3[:, NS - 3:NS], start=True, stop=True).then_inc(gate_done, 1)
                t.wait_ge(nq_done, b + 1)
                t.transpose(bank(6, P, QL), NQ[:, 0:QL], I[:])
                t.transpose(bank(6, 2 * P, KVL)[:, P:], NQ[:, QL:], I[:]).then_inc(nq_turned, 1)
                t.wait_ge(nqt_copied, 2 * b + 2)
                t.wait_ge(ks_copied, b + 1)
                for j in range(3):
                    mm = t.matmul(bank(j), NQT[:, 0, :], DQ[:, j * 512:(j + 1) * 512], start=True, stop=True)
                mm.then_inc(q_done, 1)
                t.wait_ge(kw_copied, b + 1)
                for j in range(2):
                    mm = t.matmul(bank(3 + j), NQT[0:KVL, 1, :], DK[:, j * 512:(j + 1) * 512], start=True, stop=True)
                mm.then_inc(k1_done, 1)
                src = {"ks": KS, "kw": KW, "k1": K1, "q": Q}
                for n, (T, g) in enumerate(TURNS):
                    if g == 0:
                        for s_, val in {"ks": ((ks_roped, b + 1), (gate_shifted, b + 1), (k1_copied, 2 * b + 2)),
                                        "kw": ((kw_roped, b + 1),), "k1": ((k1_roped, b + 1),), "q": ((q_roped, b + 1),)}[T]:
                            t.wait_ge(s_, val)
                    if n >= 4:
                        t.wait_ge(odd_copied if n % 2 else even_copied, 8 * b + (n - 4) // 2 + 1)
                    for j in range(4):
                        mm = t.transpose(turned_from(n)[:, j, :], src[T][:, 4 * g + j, :], I[:])
                    mm.then_inc(heads_turned, 1)
                t.wait_ge(even_copied, 8 * b + 8)
                t.wait_ge(odd_copied, 8 * b + 8)

                def scores(g):
                    if g:
                        t.wait_ge(s_read, GROUPS * b + g)
                    for j in range(4):
                        mm = t.matmul(bank(j, 3 * P), QT[:, 4 * g + j, :], K3T[:, 4 * g + j].rearrange("p a f -> p (a f)"),
                                      start=True, stop=True)
                    mm.then_inc(s_done, 1)
                scores(0)
                for g in range(GROUPS):
                    if g + 1 < GROUPS:
                        scores(g + 1)
                    t.wait_ge(p_done, GROUPS * b + g + 1)
                    for j in range(12):
                        mm = t.transpose(ps[:, 4 * 512 + j * P:4 * 512 + (j + 1) * P], S[:, j // 3, j % 3, :], I[:])
                    mm.then_inc(p_turned, 1)
                    t.wait_ge(pt_copied, GROUPS * b + g + 1)
                    for j in range(4):
                        h = 4 * g + j
                        for n in range(3):
                            mm = t.matmul(bank(7)[:, h * VH:(h + 1) * VH], PT[:, j, n, :], V3[:, n, h * VH:(h + 1) * VH],
                                          start=(h == 0 and n == 0), stop=n == 2, skip_group_check=True)
                    mm.then_inc(pv_done, 1)
                t.wait_ge(o2_copied, b + 1)
                turn([ps[:, k * P:(k + 1) * P] for k in range(KC)], lambda k: O2[:, k * P:(k + 1) * P]).then_inc(o2_turned, 1)
                t.wait_ge(o2t_copied, b + 1)
                rows_times(1, O2T, PROJ, KC, 0, D).then_inc(y_done, 1)

HF = D // H
DC = D // 4
HID = 1024
GROUPS_E, EPG = 2, 4
E_ALL = GROUPS_E * EPG


def rms_scale(v, c, y, out, weight, stats, col):
    moments(v, c, col[:, 0:2], y, stats, col[:, 5:6])
    c.link(v.scalar_tensor_tensor(out=col[:, 2:3], in0=col[:, 0:1], scalar=col[:, 0:1], in1=col[:, 1:2], op0=ALU.mult, op1=ALU.add))
    c.link(v.tensor_scalar(col[:, 2:3], col[:, 2:3], RMS_EPS, None, ALU.add))
    rsqrt_cols(v, c, col[:, 3:4], col[:, 2:3], col[:, 4:5])
    return v.scalar_tensor_tensor(out=out, in0=y, scalar=col[:, 3:4], in1=weight, op0=ALU.mult, op1=ALU.mult)


def stage_ffn(nc, x2_d, x3_d, h1t_d, w8_d, wts, tables):
    wq, wk_c, wv_c, wk, wv, wo, w_in, w_out, w1, wg, we, g_bias, e_bias, norm1 = wts
    ident, rope2, earlier = tables
    with ExitStack() as ctx:
        sb = lambda n, s, d=F32: ctx.enter_context(nc.sbuf_tensor("f_" + n, s, d))
        I = sb("ident", [P, P])
        ROPE_T = sb("rope", [P, 2, HF])
        EARLIER = sb("earlier", [P, EPG, EPG])
        BIAS = sb("bias", [P, GROUPS_E + E_ALL])
        N1 = sb("n1", [P, D])
        WQ = sb("wq", [P, KC, D])
        WC = sb("wc", [P, KC, 2 * DC])
        WKV = sb("wkv", [P, 2, D])
        WO = sb("wo", [P, KC, D])
        WG = sb("wg", [P, KC, GROUPS_E + E_ALL])
        WI = sb("wi", [P, KC, 2 * HID])
        W1 = sb("w1", [P, KC, 2 * HID])
        WOUT = sb("wout", [P, HID // P, D])
        X = sb("x", [P, D])
        SRC = sb("src", [P, D])
        XT = sb("xt", [P, KC, P])
        stats = sb("stats", [P, 6])
        col = sb("col", [P, 8])
        Q = sb("q", [P, H, HF])
        K = sb("k", [P, H, HF])
        V = sb("v", [P, D])
        CT = sb("ct", [P, 2, P])
        R = sb("r", [P, 4, D])
        QT = sb("qt", [P, KC, P])
        BK = sb("bk", [P, KC, 4, P])
        S = sb("s", [P, H, P])
        PT = sb("pt", [P, H, P])
        mx = sb("mx", [P, H])
        sm = sb("sm", [P, H])
        O = sb("o", [P, D])
        OT = sb("ot", [P, KC, P])
        XF = sb("xf", [P, D])
        FT = sb("ft", [P, KC, P])
        G = sb("g", [P, 64])
        RK = sb("rk", [P, 2, EPG, EPG])
        SG = S[:].rearrange("p h f -> p (h f)").rearrange("p (a f) -> p a f", a=2)
        HS = PT[:].rearrange("p h f -> p (h f)").rearrange("p (a f) -> p a f", a=2)
        HT = sb("ht", [P, 2, HID // P, P])
        X3 = sb("x3", [P, D])
        ps = ctx.enter_context(nc.psum_tensor("f_ps", [P, 8 * 512], F32))
        sems = {}

        def done(n):
            if n not in sems:
                sems[n] = ctx.enter_context(nc.semaphore("f_" + n))
            return sems[n]

        def bank(n, w=512, rows=P):
            return ps[0:rows, n * 512:n * 512 + w]
        consts_in, loaded, stored = done("consts_in"), done("loaded"), done("stored")
        vchain, kchain = done("vchain"), done("kchain")
        src_done, x_turned, xt_copied, q_done, c_done = done("src_done"), done("x_turned"), done("xt_copied"), done("q_done"), done("c_done")
        q_copied, ct_copied, kv_done, k_copied, v_copied = done("q_copied"), done("ct_copied"), done("kv_done"), done("k_copied"), done("v_copied")
        q_roped, k_roped, q_turned, k_turned, qt_copied, bk_copied = (done(n) for n in ("q_roped", "k_roped", "q_turned", "k_turned", "qt_copied", "bk_copied"))
        bk_zeroed = done("bk_zeroed")
        s_done, s_shifted, s_expd, p_turned, pt_copied, pv_done = (done(n) for n in ("s_done", "s_shifted", "s_expd", "p_turned", "pt_copied", "pv_done"))
        o_done, o_turned, ot_copied, y_done, xf_done, f_turned, ft_copied = (done(n) for n in ("o_done", "o_turned", "ot_copied", "y_done", "xf_done", "f_turned", "ft_copied"))
        logits_done, logits_read, g_shifted, g_expd, w8_done = (done(n) for n in ("logits_done", "logits_read", "g_shifted", "g_expd", "w8_done"))
        in_done, silu_done, hidden_done, h_turned, ht_copied, out_done, x3_done = (done(n) for n in ("in_done", "silu_done", "hidden_done", "h_turned", "ht_copied", "out_done", "x3_done"))
        sums_done = done("sums_done")
        block = ctx.enter_context(nc.Block())
        NC = 19

        @block.sync
        def _(sp):
            rows = lambda w: w.rearrange("(k p) n -> p k n", p=P)
            pieces = ((I[:], ident), (ROPE_T[:].rearrange("p a f -> p a f"), None), (EARLIER[:], earlier.partition_broadcast(P)),
                      (BIAS[:, 0:GROUPS_E], g_bias.partition_broadcast(P)), (BIAS[:, GROUPS_E:], e_bias.partition_broadcast(P)),
                      (N1[:], norm1.partition_broadcast(P)), (WQ[:], rows(wq)), (WC[:, :, 0:DC], rows(wk_c)),
                      (WC[:, :, DC:], rows(wv_c)), (WKV[:, 0], wk), (WKV[:, 1], wv), (WO[:], rows(wo)),
                      (WG[:, :, 0:GROUPS_E], rows(wg)), (WG[:, :, GROUPS_E:], rows(we)), (WI[:], rows(w_in)),
                      (W1[:], rows(w1)), (WOUT[:], rows(w_out)))
            n = 0
            for dst, src in pieces:
                sp.dma_start(dst, rope2 if src is None else src).then_inc(consts_in, 16)
                n += 1
            assert n == 17
            sp.sem_inc(x3_done, 1)
            sp.sem_inc(stored, 48)
            with sp.Fori(0, B) as b:
                sp.wait_ge(x3_done, b + 1)
                at = lambda d: d[bass.ds(b, 1)]
                sp.dma_start(X[:], at(x2_d).rearrange("o p f -> (o p) f")).then_inc(loaded, 16)
                sp.wait_ge(w8_done, b + 1)
                sp.dma_start(at(w8_d).rearrange("o p f -> (o p) f"), G[:, 56:64]).then_inc(stored, 16)
                sp.wait_ge(ht_copied, 2 * b + 2)
                sp.dma_start(at(h1t_d).rearrange("o p k f -> (o p) k f"), HT[:, 1]).then_inc(stored, 16)
                sp.wait_ge(x3_done, b + 2)
                sp.dma_start(at(x3_d).rearrange("o p f -> (o p) f"), X3[:]).then_inc(stored, 16)
            sp.wait_ge(stored, 48 * (B + 1))

        def rope_pairs(eng, link, x_, r1, r2):
            cc, ss = (ROPE_T[:, n:n + 1, :].broadcast_to([P, H, HF]) for n in range(2))
            link(eng.tensor_tensor(r1, x_, cc, ALU.mult))
            link(eng.tensor_tensor(r2, x_, ss, ALU.mult))
            link(eng.tensor_tensor(x_[:, :, 0::2], r1[:, :, 0::2], r2[:, :, 1::2], ALU.add))
            return eng.tensor_tensor(x_[:, :, 1::2], r1[:, :, 1::2], r2[:, :, 0::2], ALU.add)

        @block.gpsimd
        def _(g):
            g.memset(BK[:], 0.0).then_inc(bk_zeroed, 1)
            g.wait_ge(consts_in, 16 * 17)
            with g.Fori(0, B) as b:
                c = Chain(g, kchain, b, 3)
                g.wait_ge(k_copied, b + 1)
                rope_pairs(g, c.link, K[:], heads(R[:, 2], H), heads(R[:, 3], H)).then_inc(k_roped, 1)
                c.end()

        @block.scalar
        def _(a):
            flat = lambda t: t.rearrange("p k f -> p (k f)")
            with a.Fori(0, B) as b:
                a.wait_ge(x_turned, b + 1)
                a.copy(flat(XT[:]), bank(0)).then_inc(xt_copied, 1)
                a.wait_ge(q_done, b + 1)
                a.copy(flat(Q[:]), bank(1)).then_inc(q_copied, 1)
                a.wait_ge(kv_done, b + 1)
                a.copy(flat(K[:]), bank(3)).then_inc(k_copied, 1)
                a.copy(V[:], bank(4)).then_inc(v_copied, 1)
                a.wait_ge(q_turned, b + 1)
                a.copy(flat(QT[:]), bank(5)).then_inc(qt_copied, 1)
                for g in range(2):
                    a.wait_ge(s_shifted, 2 * b + g + 1)
                    s_ = flat(S[:, 8 * g:8 * g + 8])
                    a.activation(s_, s_, ACT.Exp, scale=HF ** -0.5).then_inc(s_expd, 1)
                for g in range(2):
                    a.wait_ge(p_turned, 2 * b + g + 1)
                    a.copy(flat(PT[:, 8 * g:8 * g + 8]), ps[:, (4 + 2 * g) * 512:(6 + 2 * g) * 512]).then_inc(pt_copied, 1)
                a.wait_ge(o_turned, b + 1)
                a.copy(flat(OT[:]), bank(1)).then_inc(ot_copied, 1)
                a.wait_ge(f_turned, b + 1)
                a.copy(flat(FT[:]), bank(3)).then_inc(ft_copied, 1)
                a.wait_ge(g_shifted, b + 1)
                a.activation(G[:, 18:24], G[:, 12:18], ACT.Exp).then_inc(g_expd, 1)
                for n in range(2):
                    a.wait_ge(in_done, 2 * b + n + 1)
                    a.activation(SG[:, n], ps[:, 4 * n * 512:(4 * n + 2) * 512], ACT.Silu).then_inc(silu_done, 1)
                for n in range(2):
                    a.wait_ge(h_turned, 2 * b + n + 1)
                    if n == 1:
                        a.wait_ge(stored, 48 * (b + 1))
                    a.copy(flat(HT[:, n]), ps[:, 4 * n * 512:(4 * n + 2) * 512]).then_inc(ht_copied, 1)

        @block.vector
        def _(v):
            v.wait_ge(consts_in, 16 * 17)
            with v.Fori(0, B) as b:
                c = Chain(v, vchain, b, 61)
                link = c.link
                v.wait_ge(loaded, 16 * (b + 1))
                layernorm_(v, c, SRC[:], X[:], stats[:], col[:]).then_inc(src_done, 1)
                v.wait_ge(c_done, b + 1)
                v.tensor_copy(CT[:].rearrange("p k f -> p (k f)"), bank(2, 2 * DC)).then_inc(ct_copied, 1)
                v.wait_ge(q_copied, b + 1)
                rope_pairs(v, link, Q[:], heads(R[:, 0], H), heads(R[:, 1], H)).then_inc(q_roped, 1)
                v.wait_ge(k_turned, b + 1)
                v.wait_ge(bk_zeroed, 1)
                for j in range(4):
                    q_ = slice(32 * j, 32 * j + 32)
                    v.tensor_copy(BK[q_, :, j, :], bank(6)[q_].rearrange("p (c f) -> p c f", c=KC)).then_inc(bk_copied, 1)
                for g in range(2):
                    v.wait_ge(s_done, 2 * b + g + 1)
                    s_ps = ps[:, 2 * g * 512:(2 * g + 2) * 512].rearrange("p (h f) -> p h f", f=P)
                    hs = slice(8 * g, 8 * g + 8)
                    link(v.tensor_reduce(mx[:, hs], s_ps, AX.X, ALU.max))
                    v.tensor_tensor(S[:, hs], s_ps, mx[:, hs].unsqueeze(2).broadcast_to([P, 8, P]), ALU.subtract).then_inc(s_shifted, 1)
                for g in range(2):
                    hs = slice(8 * g, 8 * g + 8)
                    v.wait_ge(s_expd, 2 * b + g + 1)
                    v.tensor_reduce(sm[:, hs], S[:, hs], AX.X, ALU.add).then_inc(sums_done, 1)
                v.wait_ge(sums_done, 2 * b + 2)
                link(v.reciprocal(sm[:], sm[:]))
                v.wait_ge(pv_done, b + 1)
                v.tensor_tensor(heads(O[:], H), heads(bank(0), H), sm[:].unsqueeze(2).broadcast_to([P, H, HF]), ALU.mult).then_inc(o_done, 1)
                v.wait_ge(y_done, b + 1)
                link(v.tensor_tensor(SRC[:], bank(2), SRC[:], ALU.add))
                rms_scale(v, c, SRC[:], XF[:], N1[:], stats[:], col[:]).then_inc(xf_done, 1)
                v.wait_ge(logits_done, b + 1)
                v.wait_ge(stored, 48 * (b + 1))
                v.tensor_tensor(G[:, 0:10], bank(4, 10), BIAS[:], ALU.add).then_inc(logits_read, 1)
                v.wait_ge(logits_read, b + 1)
                link(v.tensor_reduce(G[:, 10:11], G[:, 0:2], AX.X, ALU.max))
                link(v.tensor_scalar(G[:, 12:14], G[:, 0:2], G[:, 10:11], None, ALU.subtract))
                link(v.tensor_tensor(G[:, 25:26], G[:, 1:2], G[:, 0:1], ALU.is_gt))
                link(v.tensor_scalar(G[:, 24:25], G[:, 25:26], -1.0, 1.0, ALU.mult, ALU.add))
                link(v.tensor_scalar(G[:, 26:30], G[:, 2:6], G[:, 24:25], None, ALU.mult))
                link(v.scalar_tensor_tensor(out=G[:, 26:30], in0=G[:, 6:10], scalar=G[:, 25:26], in1=G[:, 26:30], op0=ALU.mult, op1=ALU.add))
                link(v.tensor_reduce(G[:, 11:12], G[:, 26:30], AX.X, ALU.max))
                v.tensor_scalar(G[:, 14:18], G[:, 26:30], G[:, 11:12], None, ALU.subtract).then_inc(g_shifted, 1)
                v.wait_ge(g_expd, b + 1)
                link(v.tensor_reduce(G[:, 30:31], G[:, 18:20], AX.X, ALU.add))
                link(v.tensor_reduce(G[:, 31:32], G[:, 20:24], AX.X, ALU.add))
                link(v.reciprocal(G[:, 32:34], G[:, 30:32]))
                link(v.tensor_scalar(G[:, 36:40], G[:, 20:24], G[:, 33:34], G[:, 32:33], ALU.mult, ALU.mult))
                pj = G[:, 36:40].unsqueeze(1).broadcast_to([P, EPG, EPG])
                pi = G[:, 36:40].unsqueeze(2).broadcast_to([P, EPG, EPG])
                link(v.tensor_tensor(RK[:, 0], pj, pi, ALU.is_gt))
                link(v.tensor_tensor(RK[:, 1], pj, pi, ALU.is_equal))
                link(v.tensor_tensor(RK[:, 1], RK[:, 1], EARLIER[:], ALU.mult))
                link(v.tensor_tensor(RK[:, 0], RK[:, 0], RK[:, 1], ALU.add))
                link(v.tensor_reduce(G[:, 40:44], RK[:, 0], AX.X, ALU.add))
                link(v.tensor_scalar(G[:, 44:48], G[:, 40:44], 1.5, None, ALU.is_lt))
                link(v.tensor_tensor(G[:, 44:48], G[:, 44:48], G[:, 36:40], ALU.mult))
                link(v.tensor_scalar(G[:, 56:60], G[:, 44:48], G[:, 24:25], None, ALU.mult))
                v.tensor_scalar(G[:, 60:64], G[:, 44:48], G[:, 25:26], None, ALU.mult).then_inc(w8_done, 1)
                for n in range(2):
                    v.wait_ge(silu_done, 2 * b + n + 1)
                    v.tensor_tensor(HS[:, n], SG[:, n], ps[:, (4 * n + 2) * 512:(4 * n + 4) * 512], ALU.mult).then_inc(hidden_done, 1)
                v.wait_ge(out_done, b + 1)
                v.tensor_tensor(X3[:], bank(2), XF[:], ALU.add).then_inc(x3_done, 1)
                c.end()

        @block.tensor
        def _(t):
            t.wait_ge(consts_in, 16 * 17)

            def rows_times(bank0, lhs, w, n_k, n0, n1):
                for j in range(n0, n1, 512):
                    e = min(j + 512, n1)
                    for k in range(n_k):
                        mm = t.matmul(bank(bank0 + (j - n0) // 512, e - j), lhs[:, k, :], w[:, k, j:e],
                                      start=k == 0, stop=k == n_k - 1)
                return mm

            def turn(bank0, src, n):
                for k in range(n):
                    mm = t.transpose(ps[:, bank0 * 512 + k * P:bank0 * 512 + (k + 1) * P], src[:, k * P:(k + 1) * P], I[:])
                return mm

            with t.Fori(0, B) as b:
                t.wait_ge(x3_done, b + 1)
                t.wait_ge(src_done, b + 1)
                turn(0, SRC[:], KC).then_inc(x_turned, 1)
                t.wait_ge(xt_copied, b + 1)
                rows_times(1, XT, WQ, KC, 0, D).then_inc(q_done, 1)
                for n in range(2):
                    for k in range(KC):
                        mm = t.matmul(bank(2)[:, n * P:(n + 1) * P], WC[:, k, n * DC:(n + 1) * DC], XT[:, k, :],
                                      start=k == 0, stop=k == KC - 1)
                mm.then_inc(c_done, 1)
                t.wait_ge(ct_copied, b + 1)
                for n in range(2):
                    mm = t.matmul(bank(3 + n), CT[:, n, :], WKV[:, n, :], start=True, stop=True)
                mm.then_inc(kv_done, 1)
                t.wait_ge(q_roped, b + 1)
                turn(5, Q[:].rearrange("p h d -> p (h d)"), KC).then_inc(q_turned, 1)
                t.wait_ge(k_roped, b + 1)
                turn(6, K[:].rearrange("p h d -> p (h d)"), KC).then_inc(k_turned, 1)
                t.wait_ge(qt_copied, b + 1)
                t.wait_ge(v_copied, b + 1)
                t.wait_ge(bk_copied, 4 * b + 4)
                for c in range(KC):
                    mm = t.matmul(bank(c), QT[:, c, :], BK[:, c].rearrange("p j f -> p (j f)"), start=True, stop=True)
                    if c % 2:
                        mm.then_inc(s_done, 1)
                SF = S[:].rearrange("p h f -> p (h f)")
                for g in range(2):
                    t.wait_ge(s_expd, 2 * b + g + 1)
                    turn(4 + 2 * g, SF[:, g * 1024:(g + 1) * 1024], 8).then_inc(p_turned, 1)
                for g in range(2):
                    t.wait_ge(pt_copied, 2 * b + g + 1)
                    for h in range(8 * g, 8 * g + 8):
                        mm = t.matmul(bank(0)[:, h * HF:(h + 1) * HF], PT[:, h, :], V[:, h * HF:(h + 1) * HF],
                                      start=h == 0, stop=True, skip_group_check=True)
                mm.then_inc(pv_done, 1)
                t.wait_ge(o_done, b + 1)
                turn(1, O[:], KC).then_inc(o_turned, 1)
                t.wait_ge(ot_copied, b + 1)
                rows_times(2, OT, WO, KC, 0, D).then_inc(y_done, 1)
                t.wait_ge(xf_done, b + 1)
                turn(3, XF[:], KC).then_inc(f_turned, 1)
                t.wait_ge(ft_copied, b + 1)
                rows_times(4, FT, WG, KC, 0, GROUPS_E + E_ALL).then_inc(logits_done, 1)
                rows_times(0, FT, WI, KC, 0, 2 * HID).then_inc(in_done, 1)
                t.wait_ge(logits_read, b + 1)
                rows_times(4, FT, W1, KC, 0, 2 * HID).then_inc(in_done, 1)
                for n in range(2):
                    t.wait_ge(hidden_done, 2 * b + n + 1)
                    turn(4 * n, HS[:, n], 8).then_inc(h_turned, 1)
                t.wait_ge(ht_copied, 2 * b + 1)
                rows_times(2, HT[:, 0], WOUT, HID // P, 0, D).then_inc(out_done, 1)


def layernorm_(v, c, out, x, stats, col):
    moments(v, c, col[:, 0:2], x, stats, col[:, 5:6])
    c.link(v.tensor_scalar(col[:, 2:3], col[:, 1:2], LN_EPS, None, ALU.add))
    rsqrt_cols(v, c, col[:, 3:4], col[:, 2:3], col[:, 4:5])
    return v.tensor_scalar(out, x, col[:, 0:1], col[:, 3:4], ALU.subtract, ALU.mult)


def stage_experts(nc, x2_d, x3_d, h1t_d, w8_d, w2, norm2, out):
    with ExitStack() as ctx:
        sb = lambda n, s, d=F32: ctx.enter_context(nc.sbuf_tensor("e_" + n, s, d))
        sem = lambda n: ctx.enter_context(nc.semaphore("e_" + n))
        HK = HID // P
        W2 = sb("w2", [P, E_ALL, HK, D])
        N2 = sb("n2", [P, D])
        HT = sb("ht", [P, 2, HK, P])
        W8 = sb("w8", [P, 2, E_ALL])
        ACC = sb("acc", [P, 2, D])
        X2 = sb("x2", [P, 2, D])
        OUT = sb("out", [P, 2, D])
        stats = sb("stats", [P, 6])
        col = sb("col", [P, 8])
        ps = ctx.enter_context(nc.psum_tensor("e_ps", [P, E_ALL, 512], F32))
        w_in = [sem(f"w_in{e}") for e in range(E_ALL)]
        loaded = [sem("loaded0"), sem("loaded1")]
        n2_in, vchain, e_done, summed, out_done, stored = (sem(n) for n in ("n2_in", "vchain", "e_done", "summed", "out_done", "stored"))
        block = ctx.enter_context(nc.Block())

        @block.sync
        def _(sp):
            sp.dma_start(N2[:], norm2.partition_broadcast(P)).then_inc(n2_in, 16)

            def load(b, par):
                at = lambda d: d[bass.ds(b, 1)]
                sp.dma_start(HT[:, par], at(h1t_d).rearrange("o p k f -> (o p) k f")).then_inc(loaded[par], 16)
                sp.dma_start(W8[:, par], at(w8_d).rearrange("o p f -> (o p) f")).then_inc(loaded[par], 16)
                sp.dma_start(ACC[:, par], at(x3_d).rearrange("o p f -> (o p) f")).then_inc(loaded[par], 16)
                sp.dma_start(X2[:, par], at(x2_d).rearrange("o p f -> (o p) f")).then_inc(loaded[par], 16)
            sp.sem_inc(stored, 32)
            load(0, 0)
            sp.dma_start(W2[:, 0], w2[0].rearrange("(k p) n -> p k n", p=P)).then_inc(w_in[0], 16)
            load(1, 1)
            for e in range(1, E_ALL):
                sp.dma_start(W2[:, e], w2[e].rearrange("(k p) n -> p k n", p=P)).then_inc(w_in[e], 16)
            with sp.Fori(0, B // 2 - 1) as i:
                for par in range(2):
                    sp.wait_ge(out_done, 2 * i + par + 1)
                    sp.dma_start(out[bass.ds(2 * i + par, 1)].rearrange("o p f -> (o p) f"), OUT[:, par]).then_inc(stored, 16)
                    load(2 * i + par + 2, par)
            for par in range(2):
                sp.wait_ge(out_done, B - 1 + par)
                sp.dma_start(out[B - 2 + par], OUT[:, par]).then_inc(stored, 16)
            sp.wait_ge(stored, 16 * (B + 2))

        @block.vector
        def _(v):
            v.wait_ge(n2_in, 16)
            with v.Fori(0, B // 2) as i:
                c = Chain(v, vchain, i, 38)
                for par in range(2):
                    b = 2 * i + par
                    v.wait_ge(loaded[par], 64 * (i + 1))
                    for e in range(E_ALL):
                        v.wait_ge(e_done, E_ALL * b + e + 1)
                        if e:
                            v.wait_ge(summed, E_ALL * b + e)
                        v.scalar_tensor_tensor(out=ACC[:, par], in0=ps[:, e], scalar=W8[:, par, e:e + 1], in1=ACC[:, par],
                                               op0=ALU.mult, op1=ALU.add).then_inc(summed, 1)
                    v.wait_ge(summed, E_ALL * (b + 1))
                    c.link(rms_scale(v, c, ACC[:, par], ACC[:, par], N2[:], stats[:], col[:]))
                    v.wait_ge(stored, 16 * (b + 1))
                    v.tensor_tensor(OUT[:, par], ACC[:, par], X2[:, par], ALU.add).then_inc(out_done, 1)
                c.end()

        @block.tensor
        def _(t):
            def experts(par, b, first):
                t.wait_ge(loaded[par], 64 * (b // 2 + 1))
                for e in range(E_ALL):
                    if first:
                        t.wait_ge(w_in[e], 16)
                    else:
                        t.wait_ge(summed, E_ALL * (b - 1) + e + 1)
                    for k in range(HK):
                        mm = t.matmul(ps[:, e], HT[:, par, k, :], W2[:, e, k, :], start=k == 0, stop=k == HK - 1)
                    mm.then_inc(e_done, 1)
            experts(0, 0, True)
            experts(1, 1, False)
            with t.Fori(1, B // 2) as i:
                for par in range(2):
                    experts(par, 2 * i + par, False)


def program(nc, x, ctx_t, mask, ident, rope, causal, rope2, earlier, wq, wkv, middle, ffn, w2, norm2, out):
    scratch = lambda n, s: nc.dram_tensor(n, s, F32, kind="Internal").ap()
    q_hi = scratch("q_hi_scratch", (PAIRS, P, TOK))
    q_lo = scratch("q_lo_scratch", (PAIRS, P, TOK))
    o_part = scratch("o_part_scratch", (NIT, P, GRP, GW))
    x2 = scratch("x2_scratch", (B, P, D))
    x3 = scratch("x3_scratch", (B, P, D))
    h1t = scratch("h1t_scratch", (B, P, HID // P, P))
    w8 = scratch("w8_scratch", (B, P, E_ALL))
    stage_queries(nc, x, wq, ident, q_hi, q_lo)
    stage_cross(nc, ctx_t, mask, wkv, q_hi, q_lo, o_part)
    stage_middle(nc, x, o_part, x2, middle, (ident, rope, causal))
    stage_ffn(nc, x2, x3, h1t, w8, ffn, (ident, rope2, earlier))
    stage_experts(nc, x2, x3, h1t, w8, w2, norm2, out)


MIDDLE = ["L0_xattn_Wo", "L0_xattn_bo"] + ["L0_attn_" + n for n in (
    "w_cq", "g_qnorm", "w_dq_nope", "w_dq_rope", "w_ckv", "g_kvnorm", "w_dk_nope", "w_dv", "w_krope",
    "w_selk", "w_selv", "w_wink", "w_winv", "w_gate", "w_proj")]
FFN = ["L0_ffn_" + n for n in ("Wq", "Wk_c", "Wv_c", "Wk", "Wv", "Wo", "W_shared_in", "W_shared_out", "W1_shared",
                               "Wg_gate", "We_gate", "group_bias", "expert_bias", "norm1_w")]


def tables():
    angle = np.outer(np.arange(P), 10000.0 ** (-np.arange(0, ROPE, 2) / ROPE))
    cos, sin = np.cos(angle), np.sin(angle)
    rope = np.stack([np.concatenate([cos, cos], 1), np.concatenate([sin, -sin], 1)], 1)
    angle = np.outer(np.arange(P), 10000.0 ** (-np.arange(0, HF, 2) / HF))
    cos, sin = np.cos(angle), np.sin(angle)
    rope2 = np.stack([np.stack([cos, cos], 2).reshape(P, HF), np.stack([sin, -sin], 2).reshape(P, HF)], 1)
    causal = np.zeros((P, 3, P))
    causal[:, 0] = causal[:, 2] = np.triu(np.full((P, P), NEG), 1)
    f = lambda a: np.ascontiguousarray(a, np.float32)
    return {"ident": f(np.eye(P)), "rope": f(rope), "causal": f(causal), "rope2": f(rope2), "earlier": f(np.tril(np.ones((EPG, EPG)), -1))}


def kernel(**inputs):
    import concourse.bacc as bacc
    from concourse.bass_utils import run_bass_kernel_spmd

    nc = bacc.Bacc("TRN2", target_bir_lowering=False, num_devices=1)
    ctx = np.asarray(inputs["ctx_1024"]).reshape(B * M // BLK, BLK, KC, P)
    mask = np.asarray(inputs["mask_BxS2_bk1"]).reshape(B, M // P, P)
    arrays = {
        "x": np.asarray(inputs["x"]),
        "ctx_t": ctx.transpose(0, 3, 2, 1),
        "mask": np.ascontiguousarray(mask.transpose(2, 0, 1)).reshape(P, P),
        **tables(),
        **{n: np.asarray(inputs[n]) for n in ["L0_xattn_Wq", "L0_xattn_Wkv", *MIDDLE, *FFN, "L0_ffn_W2_experts", "L0_ffn_norm2_w"]},
    }
    arrays = {"in_" + n: np.ascontiguousarray(a) for n, a in arrays.items()}
    ap = {n[3:]: nc.dram_tensor(n, a.shape, mybir.dt.from_np(a.dtype), kind="ExternalInput").ap() for n, a in arrays.items()}
    out = nc.dram_tensor("out", (B, P, D), F32, kind="ExternalOutput").ap()
    program(nc, *(ap[n] for n in ("x", "ctx_t", "mask", "ident", "rope", "causal", "rope2", "earlier", "L0_xattn_Wq", "L0_xattn_Wkv")),
            [ap[n] for n in MIDDLE], [ap[n] for n in FFN], ap["L0_ffn_W2_experts"], ap["L0_ffn_norm2_w"], out)
    r = run_bass_kernel_spmd(nc, [arrays], core_ids=[0])
    return r.results[0]["out"]
```

```python
from contextlib import ExitStack

import numpy as np
import concourse.bass as bass
from concourse import mybir

F32 = mybir.dt.float32
F32R = mybir.dt.float32r
I32 = mybir.dt.int32
U8 = mybir.dt.uint8
ALU = mybir.AluOpType
ACT = mybir.ActivationFunctionType
AX = mybir.AxisListType

P = 128
B = 8
D = 512
KC = D // P
TOK = B * P
M = 2048
H = 16
DH = 64
INNER = H * DH
PAIRS = H // 2
BLK = 512
BPI = 2
NIT = B * M // (BLK * BPI)
KT = BLK // P
GRP = 4
SLOTS = GRP * KT
SPI = SLOTS * BPI
LAG = 2
VW = DH + 1
GW = 4 * P
LN_EPS = 1e-5
CLIP = 5.0
EXP_HI = 148.4131591025766
EXP_LO = 0.006737946999085467


RSQRT_GUESS = 0x5F3759DF

NOPE, ROPE, VH = 32, 64, 32
QK = NOPE + ROPE
QL, KVL = 96, 32
NEG = -3.0e38
RMS_EPS = 1e-6


class Chain:

    def __init__(self, eng, sem, i, length):
        self.eng, self.sem, self.i, self.length, self.n = eng, sem, i, length, 0

    def link(self, ins):
        self.n += 1
        ins.then_inc(self.sem, 1)
        self.eng.wait_ge(self.sem, self.i * self.length + self.n)

    def end(self):
        assert self.n == self.length, self.n


def rsqrt_cols(v, c, y, x, tmp):
    c.link(v.tensor_scalar(tmp.bitcast(I32), x.bitcast(I32), 1, None, ALU.arith_shift_right))
    c.link(v.tensor_scalar(y.bitcast(I32), tmp.bitcast(I32), -1, RSQRT_GUESS, ALU.mult, ALU.add))
    for n in range(3):
        c.link(v.tensor_tensor(tmp, y, y, ALU.mult))
        c.link(v.tensor_tensor(tmp, tmp, x, ALU.mult))
        c.link(v.tensor_scalar(tmp, tmp, -0.5, 1.5, ALU.mult, ALU.add))
        c.link(v.tensor_tensor(y, y, tmp, ALU.mult))


def moments(v, c, out, x, stats, carry):
    c.link(v.bn_stats(stats, x))
    v.tensor_copy(carry, stats[:, 0:1])
    c.link(v.bn_aggr(out, stats))


def layernorm_(v, c, out, x, stats, col):
    moments(v, c, col[:, 0:2], x, stats, col[:, 5:6])
    c.link(v.tensor_scalar(col[:, 2:3], col[:, 1:2], LN_EPS, None, ALU.add))
    rsqrt_cols(v, c, col[:, 3:4], col[:, 2:3], col[:, 4:5])
    return v.tensor_scalar(out, x, col[:, 0:1], col[:, 3:4], ALU.subtract, ALU.mult)


def heads(ap, h):
    return ap.rearrange("p (h d) -> p h d", h=h)


def flat(ap):
    return ap.rearrange("p k f -> p (k f)")


def stage_queries(nc, x, wq, wkv, ctx_t, ident, q_hi_d, q_lo_d, WKV, C, RAW):
    (W_hi, W_lo), (C_hi, C_lo) = WKV, C
    with ExitStack() as ctx:
        sb = lambda n, s, d=F32: ctx.enter_context(nc.sbuf_tensor("qa_" + n, s, d))
        sem = lambda n: ctx.enter_context(nc.semaphore("qa_" + n))
        QR = 3
        I = sb("ident", [P, P])
        WQ_hi = sb("wq_hi", [P, KC, INNER], F32R)
        WQ_lo = sb("wq_lo", [P, KC, INNER], F32R)
        X = sb("x", [P, B, D])
        XT_hi = sb("xt_hi", [P, KC, TOK], F32R)
        XT_lo = sb("xt_lo", [P, KC, TOK], F32R)
        stats = sb("stats", [P, 6])
        mom = sb("mom", [P, B, 2])
        rs = sb("rs", [P, 3, B])
        QH = sb("qh", [P, QR, 512], F32R)
        QL_ = sb("ql", [P, QR, 512], F32R)
        ps_t = ctx.enter_context(nc.psum_tensor("qa_pst", [P, 2, 512], F32))
        ps_q = ctx.enter_context(nc.psum_tensor("qa_psq", [P, 2, 512], F32))
        ident_in, raw_in, x_in = sem("ident_in"), [sem("raw_in0"), sem("raw_in1")], [sem(f"x_in{b}") for b in range(B)]
        hi_split, lo_split = sem("hi_split"), sem("lo_split")
        vchain, normed, turned, xt_hi, xt_lo = sem("vchain"), sem("normed"), sem("turned"), sem("xt_hi_done"), sem("xt_lo_done")
        q_done, hi_done, lo_done, q_out = sem("q_done"), sem("hi_done"), sem("lo_done"), [sem(f"out{n}") for n in range(QR)]
        GROUPS = [(c, t) for t in range(2) for c in range(PAIRS)]
        NQ = len(GROUPS)
        block = ctx.enter_context(nc.Block())
        HB = B // 2
        piece_of = lambda w, n: flat(w[:, 2 * n:2 * n + 2])
        PIECES = [tuple(piece_of(w, n) for w in (WQ_hi, WQ_lo)) for n in range(2)]
        PIECES += [(W_hi[:, k], W_lo[:, k]) for k in range(KC)]
        PIECES += [tuple(flat(c[:, n]) for c in (C_hi, C_lo)) for n in range(2)]
        raw = lambda n: flat(RAW[:, n % 2])

        @block.sync
        def _(sp):
            def load(n):
                if n >= 2:
                    sp.wait_ge(lo_split, n - 1)
                if n < 2:
                    dst = RAW[:, n].rearrange("p k f -> p (k f)").rearrange("p (k f) -> p k f", k=2)
                    sp.dma_start(dst, wq.rearrange("(k p) n -> p k n", p=P)[:, 2 * n:2 * n + 2]).then_inc(raw_in[n % 2], 16)
                elif n < 2 + KC:
                    sp.dma_start(raw(n), wkv[(n - 2) * P:(n - 1) * P, :]).then_inc(raw_in[n % 2], 16)
                else:
                    sp.dma_start(RAW[:, n % 2], ctx_t[n - 2 - KC]).then_inc(raw_in[n % 2], 16)

            def store(n):
                c, t = GROUPS[n]
                sp.wait_ge(lo_done, n + 1)
                for q_d, part in ((q_hi_d, QH), (q_lo_d, QL_)):
                    sp.dma_start(q_d[c, :, t * 512:(t + 1) * 512], part[:, n % QR, :].bitcast(F32)).then_inc(q_out[n % QR], 16)
            sp.dma_start(I[:], ident).then_inc(ident_in, 16)
            for b in range(HB):
                sp.dma_start(X[:, b, :], x[b]).then_inc(x_in[b], 16)
            load(0)
            load(1)
            for b in range(HB, B):
                sp.dma_start(X[:, b, :], x[b]).then_inc(x_in[b], 16)
            for n in range(2, 6):
                load(n)
            store(0)
            store(1)
            load(6)
            store(2)
            store(3)
            load(7)
            for n in range(4, NQ):
                store(n)
            for n in range(QR):
                sp.wait_ge(q_out[n], 32 * len(range(n, NQ, QR)))

        @block.gpsimd
        def _(g):
            for n, (hi, lo) in enumerate(PIECES):
                g.wait_ge(hi_split, n + 1)
                g.tensor_tensor(lo, raw(n), hi.bitcast(F32), ALU.subtract).then_inc(lo_split, 1)

        @block.vector
        def _(v):
            c = Chain(v, vchain, 0, 0)
            for hb in range(2):
                bs = range(hb * HB, (hb + 1) * HB)
                for b in bs:
                    v.wait_ge(x_in[b], 16)
                    moments(v, c, mom[:, b], X[:, b], stats[:], rs[:, 2, 0:1])
                s_ = slice(hb * HB, (hb + 1) * HB)
                c.link(v.tensor_scalar(rs[:, 0, s_], mom[:, s_, 1], LN_EPS, None, ALU.add))
                rsqrt_cols(v, c, rs[:, 1, s_], rs[:, 0, s_], rs[:, 2, s_])
                for b in bs:
                    v.tensor_scalar(X[:, b], X[:, b], mom[:, b, 0:1], rs[:, 1, b:b + 1], ALU.subtract, ALU.mult).then_inc(normed, 1)
                for b in bs:
                    v.wait_ge(xt_hi, b + 1)
                    t_ = slice(b * P, (b + 1) * P)
                    v.tensor_tensor(XT_lo[:, :, t_], ps_t[:, b % 2].rearrange("p (k f) -> p k f", k=KC), XT_hi[:, :, t_].bitcast(F32),
                                    ALU.subtract).then_inc(xt_lo, 1)
            for n in range(NQ):
                v.wait_ge(hi_done, n + 1)
                v.tensor_tensor(QL_[:, n % QR, :], ps_q[:, n % 2, :], QH[:, n % QR, :].bitcast(F32), ALU.subtract).then_inc(lo_done, 1)

        @block.scalar
        def _(a):
            def split(n):
                a.wait_ge(raw_in[n % 2], 16 * (n // 2 + 1))
                a.copy(PIECES[n][0], raw(n)).then_inc(hi_split, 1)

            def turned_hi(b):
                a.wait_ge(turned, b + 1)
                a.copy(XT_hi[:, :, b * P:(b + 1) * P], ps_t[:, b % 2].rearrange("p (k f) -> p k f", k=KC)).then_inc(xt_hi, 1)
            split(0)
            split(1)
            for b in range(B):
                turned_hi(b)
            split(2)
            split(3)
            for n in range(NQ):
                a.wait_ge(q_done, n + 1)
                if n >= QR:
                    a.wait_ge(q_out[n % QR], 32 * (n // QR))
                a.copy(QH[:, n % QR, :], ps_q[:, n % 2, :]).then_inc(hi_done, 1)
                if n in (0, 2, 4, 6):
                    split(4 + n // 2)

        @block.tensor
        def _(t_):
            t_.wait_ge(ident_in, 16)
            for b in range(B):
                t_.wait_ge(normed, b + 1)
                if b >= 2:
                    t_.wait_ge(xt_lo, b - 1)
                for k in range(KC):
                    mm = t_.transpose(ps_t[:, b % 2, k * P:(k + 1) * P], X[:, b, k * P:(k + 1) * P], I[:])
                mm.then_inc(turned, 1)
            t_.wait_ge(lo_split, 2)
            t_.wait_ge(xt_lo, B)
            for n, (c, t) in enumerate(GROUPS):
                if n >= 2:
                    t_.wait_ge(lo_done, n - 1)
                m = 0
                for k in range(KC):
                    for w, x_ in ((WQ_lo, XT_hi), (WQ_hi, XT_lo), (WQ_hi, XT_hi)):
                        mm = t_.matmul(ps_q[:, n % 2, :], w[:, k, c * P:(c + 1) * P], x_[:, k, t * 512:(t + 1) * 512],
                                       start=m == 0, stop=m == 3 * KC - 1)
                        m += 1
                mm.then_inc(q_done, 1)


def stage_cross(nc, ctx_t, mask, q_hi_d, q_lo_d, o_part, WKV, C, RAW):
    (W_hi, W_lo), (C_hi, C_lo) = WKV, C
    with ExitStack() as ctx:
        sb = lambda n, s, d=F32: ctx.enter_context(nc.sbuf_tensor(n, s, d))
        sem = lambda n: ctx.enter_context(nc.semaphore(n))
        K_hi = sb("k_hi", [P, PAIRS, BLK], F32R)
        K_lo = sb("k_lo", [P, PAIRS, BLK], F32R)
        V_hi = sb("v_hi", [P, KT, H, VW], F32R)
        V_lo = sb("v_lo", [P, KT, H, VW], F32R)
        Q_hi = sb("q_hi", [P, PAIRS, 2 * P], F32R)
        Q_lo = sb("q_lo", [P, PAIRS, 2 * P], F32R)
        E = sb("e", [P, 2, 512])
        E_hi = sb("e_hi", [P, 2, 512], F32R)
        E_lo = sb("e_lo", [P, 2, 512], F32R)
        O_sb = sb("o_sb", [VW, GW])
        mask_u8 = sb("mask_u8", [P, P], U8)
        top = sb("top", [P, P])
        topi = sb("topi", [P, SPI // GRP])
        ps_s = ctx.enter_context(nc.psum_tensor("ps_s", [P, 2, 512], F32))
        ps_p = ctx.enter_context(nc.psum_tensor("ps_p", [P, 2, 512], F32))
        ps_o = ctx.enter_context(nc.psum_tensor("ps_o", [P, GRP, 512], F32))
        mask_in = sem("mask_in")
        raw_in = [sem("raw_in0"), sem("raw_in1")]
        q_in = [sem(f"q_in{g}") for g in range(GRP)]
        zeroed, ones_set = sem("zeroed"), sem("ones_set")
        top_done, topi_done = sem("top_done"), sem("topi_done")
        chi_done, clo_done = sem("chi_done"), sem("clo_done")
        proj_done = sem("proj_done")
        kv_hi, kv_lo = sem("kv_hi"), sem("kv_lo")
        scored, expd, clipped = sem("scored"), sem("expd"), sem("clipped")
        e_hi, e_lo = sem("e_hi_done"), sem("e_lo_done")
        pv_done = sem("pv_done")
        o_copied, o_out = sem("o_copied"), sem("o_out")
        block = ctx.enter_context(nc.Block())

        K, V = "K", "V"
        AHEAD = [(K, c) for c in range(6)] + [(V, 0, t) for t in range(KT)]
        IN_SLOT = {0: (K, 6, 0), 1: (K, 7, 0), 2: (V, 1, 0, 0), 3: (V, 1, 1, 0), 6: (V, 1, 2, 0), 7: (V, 1, 3, 0),
                   4: (K, 0, 1), 5: (K, 1, 1), 8: (K, 2, 1), 9: (K, 3, 1), 12: (K, 4, 1), 13: (K, 5, 1),
                   10: (V, 0, 0, 1), 11: (V, 0, 1, 1), 14: (V, 0, 2, 1), 15: (V, 0, 3, 1)}
        NA = len(AHEAD)
        SPLIT_SLOT = 10

        def group_of(s):
            g = IN_SLOT[s % SLOTS]
            return g[:-1], (s // SLOTS + g[-1]) % 2

        def has_group(s, last):
            return not (last and s >= SLOTS and IN_SLOT[s % SLOTS][-1])

        def before(s, last):
            return sum(has_group(x, last) for x in range(s))

        def has_split(s, last):
            return not last and SPLIT_SLOT <= s % SLOTS < SPLIT_SLOT + KC

        def over_iterations(eng, body):
            body(0, True, False)
            with eng.Fori(1, NIT - 1) as i:
                body(i, False, False)
            body(NIT - 1, False, True)

        @block.sync
        def _(sp):
            sp.dma_start(mask_u8[:], mask).then_inc(mask_in, 16)

            def queries(i, g):
                b0 = (i // 2) * P
                for par, (dst, src) in enumerate(((Q_hi, q_hi_d), (Q_lo, q_lo_d))):
                    for hh in range(2):
                        sp.dma_start(dst[hh * DH:(hh + 1) * DH, 2 * g:2 * g + 2, hh * P:(hh + 1) * P].bitcast(F32),
                                     src[2 * g:2 * g + 2, hh * DH:(hh + 1) * DH, bass.ds(b0, P)].rearrange("c p t -> p c t")
                                     ).then_inc(q_in[g], 16)
            sp.wait_ge(zeroed, 2)
            for g in range(GRP):
                queries(0, g)

            def body(i, first, last):
                for s in range(SPI):
                    S = i * SPI + s
                    blk, r = divmod(s, SLOTS)
                    if r == 0 and not last:
                        if not first:
                            sp.wait_ge(clo_done, KC * (2 * i + blk - 1))
                        nxt = 2 * i + blk + 2
                        sp.dma_start(RAW[:, blk], ctx_t[bass.ds(nxt, 1)].rearrange("o p k f -> (o p) k f")).then_inc(raw_in[blk], 16)
                    if not last and s >= SLOTS and r % KT == KT - 1:
                        sp.wait_ge(scored, S + 1)
                        queries(i + 1, r // KT)
                    g = (s - SLOTS - KT - LAG + 1)
                    if (g >= 0 and g % KT == 0 and g // KT < GRP - 1) or (s == LAG - 1 and not first):
                        gg = GRP - 1 if s < SLOTS else g // KT
                        ii = i - 1 if s < SLOTS else i
                        sp.wait_ge(o_copied, GRP * ii + gg + 1)
                        sp.dma_start(o_part[bass.ds(ii, 1), :, gg].rearrange("o p f -> (o p) f"), O_sb[:]).then_inc(o_out, 16)
            over_iterations(sp, body)
            sp.wait_ge(o_copied, GRP * NIT)
            sp.dma_start(o_part[NIT - 1, :, GRP - 1], O_sb[:]).then_inc(o_out, 16)
            sp.wait_ge(o_out, 16 * GRP * NIT)

        @block.gpsimd
        def _(g):
            for Q in (Q_hi, Q_lo):
                g.memset(Q[:].bitcast(F32), 0.0).then_inc(zeroed, 1)

            def body(i, first, last):
                for s in range(SPI):
                    S = i * SPI + s
                    if has_split(s, last):
                        blk, k = s // SLOTS, s % SLOTS - SPLIT_SLOT
                        g.wait_ge(chi_done, KC * (2 * i + blk) + k + 1)
                        g.tensor_tensor(C_lo[:, blk, k, :], RAW[:, blk, k, :], C_hi[:, blk, k, :].bitcast(F32),
                                        ALU.subtract).then_inc(clo_done, 1)
                    g.wait_ge(e_hi, S + 1)
                    g.tensor_tensor(E_lo[:, s % 2, :], E[:, s % 2, :], E_hi[:, s % 2, :].bitcast(F32), ALU.subtract
                                    ).then_inc(e_lo, 1)
            over_iterations(g, body)

        def kv_slice(hi, kind):
            if kind[0] == K:
                return (K_hi if hi else K_lo)[:, kind[1], :]
            return (V_hi if hi else V_lo)[:, kind[2], 8 * kind[1]:8 * kind[1] + 8, 0:DH]

        def ps_view(G, kind):
            out = ps_p[:, G % 2, :]
            return out if kind[0] == K else out.rearrange("p (h d) -> p h d", d=DH)

        @block.scalar
        def _(a):
            def evac_hi(par, kind, value):
                a.wait_ge(proj_done, value)
                a.copy(kv_slice(True, kind), ps_view(par, kind)).then_inc(kv_hi, 1)

            for G, kind in enumerate(AHEAD):
                evac_hi(G, kind, G + 1)

            def body(i, first, last):
                for s in range(SPI):
                    S = i * SPI + s
                    if s and has_group(s - 1, last):
                        n = before(s, last)
                        evac_hi(n - 1, group_of(s - 1)[0], NA + i * SPI + n)
                    a.wait_ge(scored, S + 1)
                    if not (first and s < 2):
                        a.wait_ge(e_lo, S - 1)
                    a.activation(E[:, s % 2, :], ps_s[:, s % 2, :], ACT.Exp, scale=DH ** -0.5).then_inc(expd, 1)
                    if has_split(s, last):
                        blk, k = s // SLOTS, s % SLOTS - SPLIT_SLOT
                        if k == 0:
                            a.wait_ge(raw_in[blk], 16 * (i + 1))
                            a.wait_ge(proj_done, NA + S - 2)
                        a.copy(C_hi[:, blk, k, :], RAW[:, blk, k, :]).then_inc(chi_done, 1)
                    g = s - SLOTS - KT - LAG + 1
                    if g >= 0 and g % KT == 0 and g // KT < GRP - 1:
                        copy_out(g // KT, i, S)
                    if s == LAG - 1 and not first:
                        copy_out(GRP - 1, i - 1, S)
                if not last:
                    evac_hi(SPI - 1, group_of(SPI - 1)[0], NA + S + 1)

            def copy_out(gg, i, S):
                a.wait_ge(pv_done, S - LAG + 1)
                n = GRP * i + gg
                if not isinstance(n, int) or n > 0:
                    a.wait_ge(o_out, 16 * n)
                a.copy(O_sb[:], ps_o[0:VW, gg, 0:GW]).then_inc(o_copied, 1)
            over_iterations(a, body)
            copy_out(GRP - 1, NIT - 1, SPI * NIT + LAG - 1)

        @block.vector
        def _(v):
            v.memset(V_hi[:, :, :, DH:VW].bitcast(F32), 1.0).then_inc(ones_set, 1)
            v.memset(V_lo[:, :, :, DH:VW].bitcast(F32), 0.0).then_inc(ones_set, 1)
            v.wait_ge(mask_in, 16)
            v.tensor_scalar(top[:], mask_u8[:], EXP_HI - EXP_LO, EXP_LO, ALU.mult, ALU.add).then_inc(top_done, 1)
            v.wait_ge(top_done, 1)

            def evac_lo(par, kind, value):
                v.wait_ge(kv_hi, value)
                v.tensor_tensor(kv_slice(False, kind), ps_view(par, kind), kv_slice(True, kind).bitcast(F32),
                                ALU.subtract).then_inc(kv_lo, 1)
            for G, kind in enumerate(AHEAD):
                evac_lo(G, kind, G + 1)

            def body(i, first, last):
                n0 = i * (SPI // GRP)
                for s in range(SPI):
                    S = i * SPI + s
                    if s == 0:
                        v.tensor_copy(topi[:], top[:, bass.ds(n0, SPI // GRP)]).then_inc(topi_done, 1)
                        v.wait_ge(topi_done, i + 1)
                    if s and has_group(s - 1, last):
                        n = before(s, last)
                        evac_lo(n - 1, group_of(s - 1)[0], NA + i * SPI + n)
                    kt = (s // SLOTS) * KT + s % KT
                    v.wait_ge(expd, S + 1)
                    v.tensor_scalar(E[:, s % 2, :], E[:, s % 2, :], topi[:, kt:kt + 1], EXP_LO, ALU.min, ALU.max
                                    ).then_inc(clipped, 1)
                    if not (first and s < LAG):
                        v.wait_ge(pv_done, S - 1)
                    v.wait_ge(clipped, S + 1)
                    v.tensor_copy(E_hi[:, s % 2, :], E[:, s % 2, :]).then_inc(e_hi, 1)
                if not last:
                    evac_lo(SPI - 1, group_of(SPI - 1)[0], NA + S + 1)
            over_iterations(v, body)

        @block.tensor
        def _(t):
            def project(kind, cb, par):
                n = 0
                for k in range(KC):
                    for w, c in ((W_lo, C_hi), (W_hi, C_lo), (W_hi, C_hi)):
                        if kind[0] == K:
                            lhs, rhs = w[:, k, kind[1] * P:(kind[1] + 1) * P], c[:, cb, k, :]
                        else:
                            lhs = c[:, cb, k, kind[2] * P:(kind[2] + 1) * P]
                            rhs = w[:, k, INNER + kind[1] * 512:INNER + (kind[1] + 1) * 512]
                        mm = t.matmul(ps_p[:, par % 2, :], lhs, rhs, start=n == 0, stop=n == 3 * KC - 1)
                        n += 1
                mm.then_inc(proj_done, 1)

            def values(s, value):
                s = s % SPI
                g, kt = s % SLOTS // KT, s % KT
                t.wait_ge(e_lo, value)
                for j in range(4):
                    h = 4 * g + j
                    for n, (e, vv) in enumerate(((E_lo, V_hi), (E_hi, V_lo), (E_hi, V_hi))):
                        mm = t.matmul(ps_o[0:VW, g, j * P:(j + 1) * P], vv[:, kt, h, :], e[:, s % 2, j * P:(j + 1) * P],
                                      start=(s < SLOTS and kt == 0 and j == 0 and n == 0),
                                      stop=(s >= SLOTS and kt == KT - 1 and n == 2), skip_group_check=True)
                mm.then_inc(pv_done, 1)

            for G, kind in enumerate(AHEAD):
                if G >= 2:
                    t.wait_ge(kv_lo, G - 1)
                project(kind, 0, G)
            t.wait_ge(ones_set, 2)
            t.wait_ge(zeroed, 2)

            def body(i, first, last):
                for s in range(SPI):
                    S = i * SPI + s
                    g, kt = s % SLOTS // KT, s % KT
                    t.wait_ge(kv_lo, NA + i * SPI + (before(s - 1, last) if s else -1))
                    if s < SLOTS and kt == 0:
                        t.wait_ge(q_in[g], 64 * (i + 1))
                    if not (first and s < 2):
                        t.wait_ge(expd, S - 1)
                    for pr in range(2):
                        c = 2 * g + pr
                        for n, (k_, q_) in enumerate(((K_lo, Q_hi), (K_hi, Q_lo), (K_hi, Q_hi))):
                            mm = t.matmul(ps_s[:, s % 2, pr * 256:(pr + 1) * 256], k_[:, c, kt * P:(kt + 1) * P],
                                          q_[:, c, :], start=n == 0, stop=n == 2)
                    mm.then_inc(scored, 1)
                    if has_group(s, last):
                        kind, cb = group_of(s)
                        if s % SLOTS == 4 and not (first and s < SLOTS):
                            t.wait_ge(clo_done, KC * (2 * i + s // SLOTS))
                        project(kind, cb, before(s, last))
                    if not (first and s < LAG):
                        u = s - LAG
                        if s % SPI >= LAG and u < SLOTS and u % KT == 0:
                            if not first:
                                t.wait_ge(o_copied, GRP * (i - 1) + u // KT + 1)
                        values(u, S - LAG + 1)

            over_iterations(t, body)
            for s in range(SPI - LAG, SPI):
                values(s, SPI * (NIT - 1) + s + 1)


OV = DH + 1


def stage_front(nc, x, o_part, x1_d, wts, tables, keep):
    wo, bo, w_cq, g_q, w_ckv, g_kv, w_kr, w_gate = wts
    ident, rope = tables
    XT_hi, XT_lo, NQT, CKT, KRT, GATE = keep
    with ExitStack() as ctx:
        sb = lambda n, s, d=F32: ctx.enter_context(nc.sbuf_tensor("t_" + n, s, d))
        I = sb("ident", [P, P])
        ROPE_T = sb("rope", [P, 2, ROPE])
        MEAN = sb("mean", [P, P])
        BO = sb("bo", [P, D])
        GQ = sb("gq", [P, QL + KVL])
        WO_raw = sb("wo_raw", [P, INNER // P, D])
        WO_hi = sb("wo_hi", [P, INNER // P, D], F32R)
        WO_lo = sb("wo_lo", [P, INNER // P, D], F32R)
        NS = QL + KVL + ROPE + 3
        WS = sb("ws", [P, KC, NS])
        OP = sb("op", [OV, 2, 2, H * P])
        OS = sb("os", [OV, 2, H * P])
        X = sb("x", [P, 2, D])
        REC = sb("rec", [P, 4, 4])
        ON = sb("on", [P, 2, H, DH])
        OT_hi = sb("ot_hi", [P, INNER], F32R)
        OT_lo = sb("ot_lo", [P, INNER], F32R)
        X1 = sb("x1", [P, 2, D])
        XN = sb("xn", [P, 2, D])
        stats = sb("stats", [P, 6])
        col = sb("col", [P, 8])
        S3 = sb("s3", [P, B, NS])
        ms = sb("ms", [P, 3, 2 * B])
        NQ = sb("nq", [P, B, QL + KVL])
        KR = sb("kr", [P, 2, B, ROPE])
        gs = sb("gs", [P, 3, B, 3])
        ps = ctx.enter_context(nc.psum_tensor("t_ps", [P, 8 * 512], F32))
        bank = lambda n, w=512, rows=P: ps[0:rows, n * 512:n * 512 + w]
        sems = {}

        def done(n):
            if n not in sems:
                sems[n] = ctx.enter_context(nc.semaphore("t_" + n))
            return sems[n]
        names = """const_in wo_in wo_split_hi wo_split_lo vchain setup summed x_biased o_turned on_done on_turned ot_hi ot_lo
            xo_done x1_done x_normed x_turned xt_hi xt_lo s3_done s3_copied nq_done nq_turned ck_turned nqt_copied
            gate_done gate_shifted gate_expd kr_done""".split()
        (const_in, wo_in, wo_split_hi, wo_split_lo, vchain, setup, summed, x_biased, o_turned, on_done, on_turned, ot_hi, ot_lo,
         xo_done, x1_done, x_normed, x_turned, xt_hi, xt_lo, s3_done, s3_copied, nq_done, nq_turned, ck_turned, nqt_copied,
         gate_done, gate_shifted, gate_expd, kr_done) = (done(n) for n in names)
        loaded, x_in = [done("loaded0"), done("loaded1")], [done("x_in0"), done("x_in1")]
        x1_out = [done("x1_out0"), done("x1_out1")]
        block = ctx.enter_context(nc.Block())
        rows = lambda w: w.rearrange("(k p) n -> p k n", p=P)
        NC = 10
        STEPS = range(B + 3)

        @block.sync
        def _(sp):
            def load_parts(b):
                for h in range(2):
                    sp.dma_start(OP[:, b % 2, h, :], o_part[2 * b + h].rearrange("p g f -> p (g f)")).then_inc(loaded[b % 2], 16)

            def load_x(b):
                sp.dma_start(X[:, b % 2, :], x[b]).then_inc(x_in[b % 2], 16)
            load_parts(0)
            sp.dma_start(WO_raw[:], rows(wo)).then_inc(wo_in, 16)
            pieces = ((I[:], ident), (ROPE_T[:], rope), (BO[:], bo.partition_broadcast(P)),
                      (GQ[:, 0:QL], g_q.partition_broadcast(P)), (GQ[:, QL:], g_kv.partition_broadcast(P)),
                      (WS[:, :, 0:QL], rows(w_cq)), (WS[:, :, QL:QL + KVL], rows(w_ckv)),
                      (WS[:, :, QL + KVL:NS - 3], rows(w_kr)), (WS[:, :, NS - 3:NS], rows(w_gate)))
            for dst, src in pieces:
                sp.dma_start(dst, src).then_inc(const_in, 16)
            load_parts(1)
            load_x(0)
            load_x(1)
            for b in range(2, B):
                sp.wait_ge(summed, b - 1)
                load_parts(b)
                sp.wait_ge(x1_done, b - 1)
                load_x(b)
                sp.dma_start(x1_d[b - 2], X1[:, b % 2, :]).then_inc(x1_out[b % 2], 16)
            for b in range(B - 2, B):
                sp.wait_ge(x1_done, b + 1)
                sp.dma_start(x1_d[b], X1[:, b % 2, :]).then_inc(x1_out[b % 2], 16)
            for par in range(2):
                sp.wait_ge(x1_out[par], 16 * B // 2)

        @block.gpsimd
        def _(g):
            g.memset(MEAN[:], 1.0 / P).then_inc(setup, 1)
            for b in range(B):
                par = b % 2
                g.wait_ge(loaded[par], 32 * (b // 2 + 1))
                if b >= 2:
                    g.wait_ge(o_turned, b - 1)
                g.tensor_tensor(OS[:, par, :], OP[:, par, 0, :], OP[:, par, 1, :], ALU.add).then_inc(summed, 1)
                if b == 0:
                    g.wait_ge(const_in, 16 * 9)
                g.wait_ge(x_in[par], 16 * (b // 2 + 1))
                g.tensor_tensor(X[:, par, :], X[:, par, :], BO[:], ALU.add).then_inc(x_biased, 1)

        @block.scalar
        def _(a):
            a.wait_ge(wo_in, 16)
            for j in range(4):
                a.copy(flat(WO_hi[:, 2 * j:2 * j + 2]), flat(WO_raw[:, 2 * j:2 * j + 2])).then_inc(wo_split_hi, 1)
            for k in STEPS:
                if 0 <= k - 2 < B:
                    b = k - 2
                    a.wait_ge(x_turned, b + 1)
                    a.copy(XT_hi[:, :, b * P:(b + 1) * P], bank(7).rearrange("p (k f) -> p k f", k=KC)).then_inc(xt_hi, 1)
                if k < B:
                    a.wait_ge(on_turned, k + 1)
                    a.copy(OT_hi[:], ps[:, 4 * 512:6 * 512]).then_inc(ot_hi, 1)
            a.wait_ge(gate_shifted, 1)
            a.activation(gs[:, 1], gs[:, 0], ACT.Exp).then_inc(gate_expd, 1)

        @block.vector
        def _(v):
            v.wait_ge(const_in, 16 * 9)
            c = Chain(v, vchain, 0, 0)
            link = c.link
            for k in STEPS:
                if k < B:
                    v.wait_ge(o_turned, k + 1)
                    o4 = ps[:, 0:4 * 512].rearrange("p (a f) -> p a f", a=4)[:, :, 0:4 * OV].rearrange("p a (h d) -> p a h d", d=OV)
                    link(v.reciprocal(REC[:], o4[:, :, :, DH]))
                    if k >= 2:
                        v.wait_ge(on_turned, k - 1)
                    v.tensor_tensor(ON[:, k % 2].rearrange("p (a h) d -> p a h d", a=4), o4[:, :, :, 0:DH],
                                    REC[:].unsqueeze(3).broadcast_to([P, 4, 4, DH]), ALU.mult).then_inc(on_done, 1)
                if k == 0:
                    for j in range(4):
                        v.wait_ge(wo_split_hi, j + 1)
                        v.tensor_tensor(flat(WO_lo[:, 2 * j:2 * j + 2]), flat(WO_raw[:, 2 * j:2 * j + 2]),
                                        flat(WO_hi[:, 2 * j:2 * j + 2]).bitcast(F32), ALU.subtract).then_inc(wo_split_lo, 1)
                if 0 <= k - 1 < B:
                    b = k - 1
                    par = b % 2
                    v.wait_ge(xo_done, b + 1)
                    v.wait_ge(x_biased, b + 1)
                    if b >= 2:
                        v.wait_ge(x1_out[par], 16 * (b // 2))
                    v.tensor_tensor(X1[:, par], bank(6), X[:, par], ALU.add).then_inc(x1_done, 1)
                    v.wait_ge(x1_done, b + 1)
                    if b >= 2:
                        v.wait_ge(x_turned, b - 1)
                    layernorm_(v, c, XN[:, par], X1[:, par], stats[:], col[:]).then_inc(x_normed, 1)
                if 0 <= k - 2 < B:
                    b = k - 2
                    v.wait_ge(xt_hi, b + 1)
                    s_ = slice(b * P, (b + 1) * P)
                    v.tensor_tensor(XT_lo[:, :, s_], bank(7).rearrange("p (k f) -> p k f", k=KC), XT_hi[:, :, s_].bitcast(F32),
                                    ALU.subtract).then_inc(xt_lo, 1)
                if k < B:
                    v.wait_ge(ot_hi, k + 1)
                    v.tensor_tensor(OT_lo[:], ps[:, 4 * 512:6 * 512], OT_hi[:].bitcast(F32), ALU.subtract).then_inc(ot_lo, 1)
                if 0 <= k - 3 < B:
                    v.wait_ge(s3_done, k - 2)
                    v.tensor_copy(S3[:, k - 3], bank(0, NS)).then_inc(s3_copied, 1)
            v.wait_ge(s3_copied, B)
            ranks = S3[:, :, 0:QL + KVL]
            link(v.tensor_tensor(NQ[:], ranks, ranks, ALU.mult))
            for r, s_ in enumerate((slice(0, QL), slice(QL, QL + KVL))):
                sums = ms[:, 0, r * B:(r + 1) * B]
                link(v.tensor_reduce(sums, NQ[:, :, s_], AX.X, ALU.add))
                link(v.tensor_scalar(sums, sums, 1.0 / (s_.stop - s_.start), RMS_EPS, ALU.mult, ALU.add))
            rsqrt_cols(v, c, ms[:, 1], ms[:, 0], ms[:, 2])
            for r, s_ in enumerate((slice(0, QL), slice(QL, QL + KVL))):
                w = s_.stop - s_.start
                link(v.tensor_tensor(NQ[:, :, s_], S3[:, :, s_], ms[:, 1, r * B:(r + 1) * B].unsqueeze(2).broadcast_to([P, B, w]), ALU.mult))
                v.tensor_tensor(NQ[:, :, s_], NQ[:, :, s_], GQ[:, s_].unsqueeze(1).broadcast_to([P, B, w]), ALU.mult).then_inc(nq_done, 1)
            v.wait_ge(gate_done, 1)
            link(v.tensor_reduce(ms[:, 0, 0:B], bank(1, 3 * B).rearrange("p (b g) -> p b g", b=B), AX.X, ALU.max))
            v.tensor_tensor(gs[:, 0], bank(1, 3 * B).rearrange("p (b g) -> p b g", b=B), ms[:, 0, 0:B].unsqueeze(2).broadcast_to([P, B, 3]),
                            ALU.subtract).then_inc(gate_shifted, 1)
            kr = S3[:, :, QL + KVL:NS - 3]
            R = ROPE // 2
            link(v.tensor_scalar(kr, kr, 1.0 / H, None, ALU.mult))
            link(v.tensor_tensor(KR[:, 0], kr, ROPE_T[:, 0:1, :].broadcast_to([P, B, ROPE]), ALU.mult))
            link(v.tensor_tensor(KR[:, 1], kr, ROPE_T[:, 1:2, :].broadcast_to([P, B, ROPE]), ALU.mult))
            v.tensor_tensor(KRT[:, :, 0:R], KR[:, 0, :, 0:R], KR[:, 1, :, R:], ALU.add).then_inc(kr_done, 1)
            v.tensor_tensor(KRT[:, :, R:], KR[:, 0, :, R:], KR[:, 1, :, 0:R], ALU.add).then_inc(kr_done, 1)
            v.wait_ge(gate_expd, 1)
            link(v.tensor_reduce(ms[:, 0, B:2 * B], gs[:, 1], AX.X, ALU.add))
            link(v.reciprocal(ms[:, 0, B:2 * B], ms[:, 0, B:2 * B]))
            v.tensor_tensor(GATE[:], gs[:, 1], ms[:, 0, B:2 * B].unsqueeze(2).broadcast_to([P, B, 3]), ALU.mult)
            for n in range(2):
                v.wait_ge((nq_turned, ck_turned)[n], 1)
                dst, w = ((NQT, QL), (CKT, KVL))[n]
                v.tensor_copy(dst[:], ps[0:w, (2 + 2 * n) * 512:(4 + 2 * n) * 512]).then_inc(nqt_copied, 1)
            v.wait_ge(nqt_copied, 2)

        @block.tensor
        def _(t):
            t.wait_ge(const_in, 16 * 9)
            t.wait_ge(setup, 1)
            for k in STEPS:
                if k < B:
                    t.wait_ge(summed, k + 1)
                    if k >= 1:
                        t.wait_ge(on_done, k)
                    if k - 4 >= 0:
                        t.wait_ge(s3_copied, k - 3)
                    for h in range(H):
                        o = bank(h // 4)[:, (h % 4) * OV:(h % 4 + 1) * OV]
                        mm = t.transpose(o, OS[:, k % 2, h * P:(h + 1) * P], I[0:OV, 0:OV])
                    mm.then_inc(o_turned, 1)
                if 0 <= k - 1 < B:
                    b = k - 1
                    if b == 0:
                        t.wait_ge(wo_split_lo, 4)
                    t.wait_ge(ot_lo, b + 1)
                    if b:
                        t.wait_ge(x1_done, b)
                    n = 0
                    for kk in range(INNER // P):
                        for o, w in ((OT_lo, WO_hi), (OT_hi, WO_lo), (OT_hi, WO_hi)):
                            mm = t.matmul(bank(6), o[:, kk * P:(kk + 1) * P], w[:, kk, :], start=n == 0, stop=n == 23)
                            n += 1
                    mm.then_inc(xo_done, 1)
                if 0 <= k - 2 < B:
                    b = k - 2
                    t.wait_ge(x_normed, b + 1)
                    if b:
                        t.wait_ge(xt_lo, b)
                    for kk in range(KC):
                        mm = t.transpose(bank(7)[:, kk * P:(kk + 1) * P], XN[:, b % 2, kk * P:(kk + 1) * P], I[:])
                    mm.then_inc(x_turned, 1)
                if k < B:
                    t.wait_ge(on_done, k + 1)
                    if k:
                        t.wait_ge(ot_lo, k)
                    for j in range(8):
                        mm = t.transpose(ps[:, 4 * 512 + j * P:4 * 512 + (j + 1) * P],
                                         ON[:, k % 2].rearrange("p h d -> p (h d)")[:, j * P:(j + 1) * P], I[:])
                    mm.then_inc(on_turned, 1)
                if 0 <= k - 3 < B:
                    b = k - 3
                    t.wait_ge(xt_lo, b + 1)
                    t.wait_ge(on_done, min(k + 1, B))
                    if b:
                        t.wait_ge(s3_copied, b)
                    for kk in range(KC):
                        for n, xt in enumerate((XT_lo, XT_hi)):
                            mm = t.matmul(bank(0, NS), xt[:, kk, b * P:(b + 1) * P].bitcast(F32), WS[:, kk, :],
                                          start=kk == 0 and n == 0, stop=kk == KC - 1 and n == 1)
                    mm.then_inc(s3_done, 1)
            t.wait_ge(s3_copied, B)
            t.matmul(bank(1, 3 * B), MEAN[:], S3[:, :, NS - 3:NS], start=True, stop=True).then_inc(gate_done, 1)
            for n, (o, s_, w) in enumerate(((2, slice(0, QL), QL), (4, slice(QL, QL + KVL), KVL))):
                t.wait_ge(nq_done, n + 1)
                for b in range(B):
                    mm = t.transpose(ps[0:w, o * 512 + b * P:o * 512 + (b + 1) * P], NQ[:, b, s_], I[:])
                mm.then_inc((nq_turned, ck_turned)[n], 1)


def stage_attend(nc, wts, tables, keep, O2):
    w_dqn, w_dqr, w_dkn, w_dv, w_selk, w_selv, w_wink, w_winv = wts
    ident, rope, causal = tables
    XT_hi, XT_lo, NQT, CKT, KRT, GATE = keep
    with ExitStack() as ctx:
        sb = lambda n, s, d=F32: ctx.enter_context(nc.sbuf_tensor("a_" + n, s, d))
        G4 = 4
        GK, GV = G4 * QK, G4 * VH
        NW = 2 * GK + 2 * GV
        I = sb("ident", [P, P])
        ROPE_T = sb("rope", [P, 2, ROPE])
        CAUSAL = sb("causal", [P, 3, P])
        RAW = sb("raw", [P, KC, NW])
        W_hi = sb("w_hi", [P, KC, NW], F32R)
        W_lo = sb("w_lo", [P, KC, NW], F32R)
        DQ = sb("dq", [QL, GK])
        DK = sb("dk", [KVL, 2 * GV])
        K1_, KS_, KW_, Q_ = range(4)
        T4 = sb("t4", [P, B, 4, G4, QK])
        V3 = sb("v3", [P, B, 3, G4, VH + 1])
        QT = sb("qt", [QK, 2, G4, P])
        K3T = sb("k3t", [QK, 2, G4, 3, P])
        S = sb("s", [P, 2, 12, P])
        PT = sb("pt", [P, 12, P])
        R = flat(PT[:]).rearrange("p (a n d) -> p a n d", a=2, n=12)
        mx = sb("mx", [P, 2, 12])
        rec = sb("rec", [P, 12])
        ON = sb("on", [P, 12, VH])
        ps = ctx.enter_context(nc.psum_tensor("a_ps", [P, 8 * 512], F32))
        bank = lambda n, w=512, rows=P: ps[0:rows, n * 512:n * 512 + w]
        sem = lambda n: ctx.enter_context(nc.semaphore("a_" + n))
        const_in, w_in, dq_in, w_hi_done, w_lo_done, ones_set, kr_set = (sem(n) for n in
            ("const_in", "w_in", "dq_in", "w_hi_done", "w_lo_done", "ones_set", "kr_set"))
        vchain = sem("vchain")
        ks_done, kw_done, vv_done, q_done = sem("ks_done"), sem("kw_done"), sem("vv_done"), sem("q_done")
        ks_copied, kw_copied, vv_copied, q_copied, roped = sem("ks_copied"), sem("kw_copied"), sem("vv_copied"), sem("q_copied"), sem("roped")
        ring_done, ring_a, ring_v = sem("ring_done"), sem("ring_a"), sem("ring_v")
        s_done, s_read, s_maxed, s_shifted, s_expd, pv_done, o_read, o_scaled = (sem(n) for n in
            ("s_done", "s_read", "s_maxed", "s_shifted", "s_expd", "pv_done", "o_read", "o_scaled"))
        block = ctx.enter_context(nc.Block())
        NR = H // G4
        LAGB = 2
        STEPS = range(B + LAGB)
        RING = [u for k in STEPS for u in ([("turn", k, T) for T in range(4)] if k < B else []) +
                ([("p", k - LAGB, n) for n in range(3)] if k >= LAGB else [])]
        copier = lambda u: "v" if u[0] == "turn" and u[2] == KS_ else "a"
        NRV = sum(copier(u) == "v" for u in RING)
        NRA = len(RING) - NRV
        index = {u: n for n, u in enumerate(RING)}
        nth = {}
        for u in RING:
            nth[u] = sum(copier(w) == copier(u) for w in RING[:index[u] + 1])

        def copied(eng, g, u):
            if copier(u) == "v":
                eng.wait_ge(ring_v, NRV * g + nth[u])
            else:
                eng.wait_ge(ring_a, NRA * g + nth[u])

        def ring_copy(eng, copy, g, u):
            kind, b, n = u
            src = bank(4 + index[u] % 3)
            eng.wait_ge(ring_done, len(RING) * g + index[u] + 1)
            if kind == "p":
                if b > 0:
                    eng.wait_ge(pv_done, B * g + b)
                copy(flat(PT[:, 4 * n:4 * n + 4]), src).then_inc(ring_a, 1)
            else:
                dst = QT[:, b % 2] if n == Q_ else K3T[:, b % 2, :, n, :]
                copy(dst, src[0:QK].rearrange("p (h f) -> p h f", h=G4)).then_inc(ring_v if copier(u) == "v" else ring_a, 1)

        def rounds(eng, body):
            with eng.Fori(0, NR - 1) as g:
                body(g, False)
            body(NR - 1, True)

        @block.sync
        def _(sp):
            def load_w(g):
                rows = lambda w, n: w.rearrange("(k p) n -> p k n", p=P)[:, :, bass.ds(g * n, n)]
                at = 0
                for w, n in ((w_selk, GK), (w_wink, GK), (w_selv, GV), (w_winv, GV)):
                    sp.dma_start(RAW[:, :, at:at + n], rows(w, n)).then_inc(w_in, 16)
                    at += n

            def load_dq(g):
                sp.dma_start(DQ[:, 0:GV], w_dqn[:, bass.ds(g * GV, GV)]).then_inc(dq_in, 16)
                sp.dma_start(DQ[:, GV:GK], w_dqr[:, bass.ds(g * 2 * GV, 2 * GV)]).then_inc(dq_in, 16)
                sp.dma_start(DK[:, 0:GV], w_dkn[:, bass.ds(g * GV, GV)]).then_inc(dq_in, 16)
                sp.dma_start(DK[:, GV:], w_dv[:, bass.ds(g * GV, GV)]).then_inc(dq_in, 16)
            load_w(0)
            load_dq(0)
            for dst, src in ((I[:], ident), (ROPE_T[:], rope), (CAUSAL[:], causal)):
                sp.dma_start(dst, src).then_inc(const_in, 16)

            def body(g, last):
                if not last:
                    sp.wait_ge(w_lo_done, g + 1)
                    load_w(g + 1)
                    sp.wait_ge(vv_done, B * (g + 1))
                    load_dq(g + 1)
            rounds(sp, body)

        @block.gpsimd
        def _(g_):
            g_.memset(V3[:], 1.0).then_inc(ones_set, 1)
            for b in range(B):
                g_.tensor_copy(T4[:, b, K1_, :, NOPE:], KRT[:, b:b + 1, :].broadcast_to([P, G4, ROPE])).then_inc(kr_set, 1)

            def body(g, last):
                for b in range(B):
                    g_.wait_ge(s_maxed, B * g + b + 1)
                    g_.tensor_tensor(S[:, b % 2], S[:, b % 2], mx[:, b % 2].unsqueeze(2).broadcast_to([P, 12, P]), ALU.subtract
                                     ).then_inc(s_shifted, 1)
            rounds(g_, body)

        @block.scalar
        def _(a):
            def split(n):
                a.wait_ge(w_in, 64 * n)
                a.copy(flat(W_hi[:]), flat(RAW[:])).then_inc(w_hi_done, 1)
            split(1)
            a.wait_ge(ones_set, 1)

            def body(g, last):
                for b in range(B):
                    a.wait_ge(ks_done, B * g + b + 1)
                    a.copy(T4[:, b, KS_].rearrange("p h d -> p (h d)"), bank(b % 2, GK)).then_inc(ks_copied, 1)
                    a.wait_ge(kw_done, B * g + b + 1)
                    a.copy(T4[:, b, KW_].rearrange("p h d -> p (h d)"), bank(2 + b % 2, GK)).then_inc(kw_copied, 1)
                    a.wait_ge(vv_done, B * g + b + 1)
                    vb = bank(4 + b % 2)
                    for n, at in ((1, 0), (2, GV), (0, 3 * GV)):
                        a.copy(V3[:, b, n, :, 0:VH], heads(vb[:, at:at + GV], G4)).then_inc(vv_copied, 1)
                    a.copy(T4[:, b, K1_, :, 0:NOPE], heads(vb[:, 2 * GV:3 * GV], G4)).then_inc(vv_copied, 1)
                if not last:
                    split(g + 2)
                for k in STEPS:
                    for u in RING:
                        if copier(u) == "a" and ((u[0] == "turn" and u[1] == k) or (u[0] == "p" and u[1] == k - LAGB)):
                            ring_copy(a, a.copy, g, u)
                    if 1 <= k <= B:
                        b = k - 1
                        a.wait_ge(s_shifted, B * g + b + 1)
                        a.activation(flat(S[:, b % 2]), flat(S[:, b % 2]), ACT.Exp, scale=QK ** -0.5).then_inc(s_expd, 1)
            rounds(a, body)

        @block.vector
        def _(v):
            def split(n):
                v.wait_ge(w_hi_done, n)
                v.tensor_tensor(flat(W_lo[:]), flat(RAW[:]), flat(W_hi[:]).bitcast(F32), ALU.subtract).then_inc(w_lo_done, 1)
            v.wait_ge(const_in, 48)
            split(1)

            def body(g, last):
                c = Chain(v, vchain, g, 4 * B)
                link = c.link
                for b in range(B):
                    v.wait_ge(q_done, B * g + b + 1)
                    v.tensor_copy(T4[:, b, Q_, :, 0:NOPE], heads(bank(6 + b % 2, GV), G4)).then_inc(q_copied, 1)
                    v.tensor_copy(T4[:, b, Q_, :, NOPE:], heads(bank(6 + b % 2, GK)[:, GV:], G4)).then_inc(q_copied, 1)
                    v.wait_ge(q_copied, 2 * (B * g + b + 1))
                    v.wait_ge(kw_copied, B * g + b + 1)
                    x_ = T4[:, b, KS_:Q_ + 1].rearrange("p t h d -> p (t h) d")[:, :, NOPE:]
                    H_ = ROPE // 2
                    v.tensor_tensor(R[:, 0], x_, ROPE_T[:, 0:1, :].broadcast_to([P, 12, ROPE]), ALU.mult)
                    link(v.tensor_tensor(R[:, 1], x_, ROPE_T[:, 1:2, :].broadcast_to([P, 12, ROPE]), ALU.mult))
                    v.tensor_tensor(x_[:, :, 0:H_], R[:, 0, :, 0:H_], R[:, 1, :, H_:], ALU.add)
                    v.tensor_tensor(x_[:, :, H_:], R[:, 0, :, H_:], R[:, 1, :, 0:H_], ALU.add).then_inc(roped, 1)
                if not last:
                    split(g + 2)
                for k in STEPS:
                    if k < B:
                        ring_copy(v, v.tensor_copy, g, ("turn", k, KS_))
                        b = k
                        v.wait_ge(s_done, B * g + b + 1)
                        v.tensor_tensor(S[:, b % 2].rearrange("p (a i) f -> p a (i f)", a=4),
                                        ps[:, 0:4 * 512].rearrange("p (a f) -> p a f", a=4)[:, :, 0:3 * P],
                                        flat(CAUSAL[:]).unsqueeze(1).broadcast_to([P, 4, 3 * P]), ALU.add).then_inc(s_read, 1)
                        v.wait_ge(s_read, B * g + b + 1)
                        v.tensor_reduce(mx[:, b % 2], S[:, b % 2], AX.X, ALU.max).then_inc(s_maxed, 1)
                    if k >= LAGB:
                        b = k - LAGB
                        v.wait_ge(pv_done, B * g + b + 1)
                        o12 = bank(7, 12 * (VH + 1)).rearrange("p (n d) -> p n d", n=12)
                        link(v.reciprocal(rec[:], o12[:, :, VH]))
                        r4 = rec[:].rearrange("p (h i) -> p h i", i=3)
                        link(v.tensor_tensor(r4, r4, GATE[:, b:b + 1, :].broadcast_to([P, 4, 3]), ALU.mult))
                        v.tensor_tensor(ON[:], o12[:, :, 0:VH], rec[:].unsqueeze(2).broadcast_to([P, 12, VH]), ALU.mult).then_inc(o_read, 1)
                        v.wait_ge(o_read, B * g + b + 1)
                        link(v.tensor_reduce(O2[:, b, bass.ds(g * GV, GV)].rearrange("p (h d) -> p h d", h=G4),
                                             ON[:].rearrange("p (h i) d -> p h d i", i=3), AX.X, ALU.add))
                c.end()
            rounds(v, body)

        @block.tensor
        def _(t):
            t.wait_ge(const_in, 48)
            t.wait_ge(kr_set, B)

            def body(g, last):
                t.wait_ge(w_lo_done, g + 1)
                t.wait_ge(dq_in, 64 * (g + 1))
                for b in range(B):
                    tok = slice(b * P, (b + 1) * P)

                    def dense(out, w0, w1):
                        n = 0
                        for k in range(KC):
                            for x_, w in ((XT_lo, W_hi), (XT_hi, W_lo), (XT_hi, W_hi)):
                                mm = t.matmul(out, x_[:, k, tok], w[:, k, w0:w1], start=n == 0, stop=n == 3 * KC - 1)
                                n += 1
                        return mm
                    if b >= 2:
                        t.wait_ge(ks_copied, B * g + b - 1)
                    dense(bank(b % 2, GK), 0, GK).then_inc(ks_done, 1)
                    if b >= 2:
                        t.wait_ge(q_copied, 2 * (B * g + b - 1))
                    t.matmul(bank(6 + b % 2, GK), NQT[:, tok], DQ[:], start=True, stop=True).then_inc(q_done, 1)
                    if b >= 2:
                        t.wait_ge(kw_copied, B * g + b - 1)
                    dense(bank(2 + b % 2, GK), GK, 2 * GK).then_inc(kw_done, 1)
                    if b >= 2:
                        t.wait_ge(vv_copied, 4 * (B * g + b - 1))
                    dense(bank(4 + b % 2, 2 * GV), 2 * GK, NW)
                    t.matmul(bank(4 + b % 2)[:, 2 * GV:], CKT[:, tok], DK[:], start=True, stop=True).then_inc(vv_done, 1)
                t.wait_ge(vv_copied, 4 * B * (g + 1))
                t.wait_ge(roped, B * (g + 1))
                for k in STEPS:
                    if k < B:
                        for T in range(4):
                            u = ("turn", k, T)
                            ring_free(g, u)
                            for j in range(G4):
                                mm = t.transpose(bank(4 + index[u] % 3, 512, QK)[:, j * P:(j + 1) * P], T4[:, k, T, j, :], I[:])
                            mm.then_inc(ring_done, 1)
                    if k >= LAGB:
                        b = k - LAGB
                        t.wait_ge(s_expd, B * g + b + 1)
                        for n in range(3):
                            u = ("p", b, n)
                            ring_free(g, u)
                            for j in range(4):
                                mm = t.transpose(bank(4 + index[u] % 3)[:, j * P:(j + 1) * P], S[:, b % 2, 4 * n + j, :], I[:])
                            mm.then_inc(ring_done, 1)
                    if k < B:
                        copied(t, g, ("turn", k, KS_))
                        copied(t, g, ("turn", k, Q_))
                        if k:
                            t.wait_ge(s_read, B * g + k)
                        for j in range(G4):
                            mm = t.matmul(bank(j, 3 * P), QT[:, k % 2, j, :], K3T[:, k % 2, j].rearrange("p a f -> p (a f)"),
                                          start=True, stop=True)
                        mm.then_inc(s_done, 1)
                    if k >= LAGB:
                        b = k - LAGB
                        copied(t, g, ("p", b, 2))
                        if b:
                            t.wait_ge(o_read, B * g + b)
                        for n in range(12):
                            mm = t.matmul(bank(7)[:, n * (VH + 1):(n + 1) * (VH + 1)], PT[:, n, :], V3[:, b, n % 3, n // 3, :],
                                          start=n == 0, stop=True, skip_group_check=True)
                        mm.then_inc(pv_done, 1)
                t.wait_ge(s_read, B * (g + 1))
                t.wait_ge(o_read, B * (g + 1))

            def ring_free(g, u):
                n = index[u]
                if n >= 3:
                    copied(t, g, RING[n - 3])
            rounds(t, body)


def stage_project(nc, x1_d, x2_d, w_proj, ident, ROWS, XT_hi, XT_lo):
    with ExitStack() as ctx:
        sb = lambda n, s, d=F32: ctx.enter_context(nc.sbuf_tensor("p_" + n, s, d))
        I = sb("ident", [P, P])
        W_raw = sb("w_raw", [P, KC, D])
        W_hi = sb("w_hi", [P, KC, D], F32R)
        W_lo = sb("w_lo", [P, KC, D], F32R)
        OT_hi = sb("ot_hi", [P, 2, D], F32R)
        OT_lo = sb("ot_lo", [P, 2, D], F32R)
        X1 = sb("x1", [P, B, D])
        X2 = sb("x2", [P, 2, D])
        stats = sb("stats", [P, 6])
        col = sb("col", [P, 8])
        ps = ctx.enter_context(nc.psum_tensor("p_ps", [P, 8 * 512], F32))
        bank = lambda n: ps[:, n * 512:(n + 1) * 512]
        sem = lambda n: ctx.enter_context(nc.semaphore("p_" + n))
        ident_in, w_in, w_hi_done, w_lo_done, vchain = (sem(n) for n in ("ident_in", "w_in", "w_hi_done", "w_lo_done", "vchain"))
        x1_in = [sem(f"x1_in{b}") for b in range(B)]
        x2_out = [sem("x2_out0"), sem("x2_out1")]
        o_turned, ot_hi, ot_lo, y_done, x2_done, normed, x_turned, xt_hi, xt_lo = (sem(n) for n in
            ("o_turned", "ot_hi_done", "ot_lo_done", "y_done", "x2_done", "normed", "x_turned", "xt_hi", "xt_lo"))
        block = ctx.enter_context(nc.Block())
        STEPS = range(B + 2)

        @block.sync
        def _(sp):
            sp.dma_start(I[:], ident).then_inc(ident_in, 16)
            sp.dma_start(W_raw[:], w_proj.rearrange("(k p) n -> p k n", p=P)).then_inc(w_in, 16)
            for b in range(B):
                sp.dma_start(X1[:, b], x1_d[b]).then_inc(x1_in[b], 16)
            for b in range(B):
                sp.wait_ge(x2_done, b + 1)
                sp.dma_start(x2_d[b], X2[:, b % 2]).then_inc(x2_out[b % 2], 16)
            for par in range(2):
                sp.wait_ge(x2_out[par], 16 * B // 2)

        @block.scalar
        def _(a):
            a.wait_ge(w_in, 16)
            a.copy(flat(W_hi[:]), flat(W_raw[:])).then_inc(w_hi_done, 1)
            for k in STEPS:
                if k < B:
                    a.wait_ge(o_turned, k + 1)
                    if k >= 2:
                        a.wait_ge(y_done, k - 1)
                    a.copy(OT_hi[:, k % 2], bank(k % 2)).then_inc(ot_hi, 1)
                if k >= 2:
                    b = k - 2
                    a.wait_ge(x_turned, b + 1)
                    a.copy(XT_hi[:, :, b * P:(b + 1) * P], bank(4 + b % 2).rearrange("p (k f) -> p k f", k=KC)).then_inc(xt_hi, 1)

        @block.vector
        def _(v):
            c = Chain(v, vchain, 0, 0)
            v.wait_ge(w_hi_done, 1)
            v.tensor_tensor(flat(W_lo[:]), flat(W_raw[:]), flat(W_hi[:]).bitcast(F32), ALU.subtract).then_inc(w_lo_done, 1)
            for k in STEPS:
                if k < B:
                    v.wait_ge(ot_hi, k + 1)
                    v.tensor_tensor(OT_lo[:, k % 2], bank(k % 2), OT_hi[:, k % 2].bitcast(F32), ALU.subtract).then_inc(ot_lo, 1)
                if 0 <= k - 1 < B:
                    b = k - 1
                    v.wait_ge(y_done, b + 1)
                    v.wait_ge(x1_in[b], 16)
                    if b >= 2:
                        v.wait_ge(x2_out[b % 2], 16 * (b // 2))
                    v.tensor_tensor(X2[:, b % 2], bank(2 + b % 2), X1[:, b], ALU.add).then_inc(x2_done, 1)
                    v.wait_ge(x2_done, b + 1)
                    layernorm_(v, c, ROWS[:, b], X2[:, b % 2], stats[:], col[:]).then_inc(normed, 1)
                if k >= 2:
                    b = k - 2
                    v.wait_ge(xt_hi, b + 1)
                    s_ = slice(b * P, (b + 1) * P)
                    v.tensor_tensor(XT_lo[:, :, s_], bank(4 + b % 2).rearrange("p (k f) -> p k f", k=KC), XT_hi[:, :, s_].bitcast(F32),
                                    ALU.subtract).then_inc(xt_lo, 1)
            v.wait_ge(xt_lo, B)

        @block.tensor
        def _(t):
            t.wait_ge(ident_in, 16)

            def turn(n, b):
                for j in range(KC):
                    mm = t.transpose(bank(n)[:, j * P:(j + 1) * P], ROWS[:, b, j * P:(j + 1) * P], I[:])
                return mm
            for k in STEPS:
                if k < B:
                    if k >= 2:
                        t.wait_ge(ot_lo, k - 1)
                    turn(k % 2, k).then_inc(o_turned, 1)
                if 0 <= k - 1 < B:
                    b = k - 1
                    if b == 0:
                        t.wait_ge(w_lo_done, 1)
                    if b >= 2:
                        t.wait_ge(x2_done, b - 1)
                    t.wait_ge(ot_lo, b + 1)
                    n = 0
                    for j in range(KC):
                        for o, w in ((OT_lo, W_hi), (OT_hi, W_lo), (OT_hi, W_hi)):
                            mm = t.matmul(bank(2 + b % 2), o[:, b % 2, j * P:(j + 1) * P], w[:, j, :], start=n == 0, stop=n == 11)
                            n += 1
                    mm.then_inc(y_done, 1)
                if k >= 2:
                    b = k - 2
                    if b >= 2:
                        t.wait_ge(xt_lo, b - 1)
                    t.wait_ge(normed, b + 1)
                    turn(4 + b % 2, b).then_inc(x_turned, 1)


HF = D // H
DC = D // 4
HID = 1024
GROUPS_E, EPG = 2, 4
E_ALL = GROUPS_E * EPG


def rms_scale(v, c, y, out, weight, stats, col):
    moments(v, c, col[:, 0:2], y, stats, col[:, 5:6])
    c.link(v.scalar_tensor_tensor(out=col[:, 2:3], in0=col[:, 0:1], scalar=col[:, 0:1], in1=col[:, 1:2], op0=ALU.mult, op1=ALU.add))
    c.link(v.tensor_scalar(col[:, 2:3], col[:, 2:3], RMS_EPS, None, ALU.add))
    rsqrt_cols(v, c, col[:, 3:4], col[:, 2:3], col[:, 4:5])
    return v.scalar_tensor_tensor(out=out, in0=y, scalar=col[:, 3:4], in1=weight, op0=ALU.mult, op1=ALU.mult)


def stage_ffn_attend(nc, wts, tables, ROWS, XT_hi, XT_lo, W8):
    wq, wk_c, wv_c, wk, wv, wo, wg, we, g_bias, e_bias, norm1 = wts
    ident, rope_t, earlier = tables
    with ExitStack() as ctx:
        sb = lambda n, s, d=F32: ctx.enter_context(nc.sbuf_tensor("g_" + n, s, d))
        HALF = 512
        NL = GROUPS_E + E_ALL
        I = sb("ident", [P, P])
        ROPE_T = sb("rope", [P, 2, P])
        EARLIER = sb("earlier", [P, EPG, EPG])
        BIAS = sb("bias", [P, NL])
        N1 = sb("n1", [P, D])
        WG = sb("wg", [P, KC, NL])
        RAW = sb("raw", [P, KC, D])
        WQ_hi = sb("wq_hi", [P, KC, D], F32R)
        WQ_lo = sb("wq_lo", [P, KC, D], F32R)
        WS_hi = sb("ws_hi", [P, KC, D], F32R)
        WS_lo = sb("ws_lo", [P, KC, D], F32R)
        WC_raw = sb("wc_raw", [P, KC, 2 * DC])
        WC_hi = sb("wc_hi", [P, KC, 2 * DC], F32R)
        WC_lo = sb("wc_lo", [P, KC, 2 * DC], F32R)
        WK = sb("wk", [P, 2, D])
        WV = sb("wv", [P, D])
        CT = sb("ct", [P, 2, TOK])
        QT = sb("qt", [P, KC, TOK])
        KT_ = sb("kt", [P, KC, TOK])
        V = sb("v", [P, B, D])
        PT = sb("pt", [P, H, P])
        R = flat(PT[:]).rearrange("p (r s f) -> p r s f", r=2, s=2)
        S = (CT[:].rearrange("p a (h f) -> p (a h) f", f=P), RAW[:].rearrange("p k (h f) -> p (k h) f", f=P))
        mx = sb("mx", [P, 2, H])
        sm = sb("sm", [P, 2, H])
        O = sb("o", [P, D])
        OT_hi = sb("ot_hi", [P, D], F32R)
        OT_lo = sb("ot_lo", [P, D], F32R)
        stats = sb("stats", [P, 6])
        col = sb("col", [P, 8])
        G = sb("g", [P, 56])
        RK = sb("rk", [P, 2, EPG, EPG])
        ps = ctx.enter_context(nc.psum_tensor("g_ps", [P, 8 * 512], F32))
        bank = lambda n, w=512: ps[:, n * 512:n * 512 + w]
        names = """const_in wc_in wq_in wkv_in wo_in wc_hi_done wc_lo_done wq_hi_done wq_lo_done swapped k_swapped vchain
            c_done ct_copied two_done multiplied roped v_done v_copied
            s_done maxed s_expd p_turned pt_copied pv_done normed o_turned ot_hi ot_lo y_done y_read xf_done f_turned xt_hi xt_lo
            logits_done g_shifted g_expd""".split()
        sems = {n: ctx.enter_context(nc.semaphore("g_" + n)) for n in names}
        (const_in, wc_in, wq_in, wkv_in, wo_in, wc_hi_done, wc_lo_done, wq_hi_done, wq_lo_done, swapped, k_swapped, vchain,
         c_done, ct_copied, two_done, multiplied, roped, v_done, v_copied,
         s_done, maxed, s_expd, p_turned, pt_copied, pv_done, normed, o_turned, ot_hi, ot_lo, y_done, y_read, xf_done, f_turned, xt_hi,
         xt_lo, logits_done, g_shifted, g_expd) = (sems[n] for n in names)
        block = ctx.enter_context(nc.Block())
        UNITS = [(w, c, t) for w in ("q", "k") for c in range(KC) for t in range(2)]
        NU = len(UNITS)
        STEPS = range(B + 4)
        at = lambda k: 0 <= k < B
        NC = 8

        @block.sync
        def _(sp):
            rows = lambda w: w.rearrange("(k p) n -> p k n", p=P)
            sp.dma_start(WC_raw[:, :, 0:DC], rows(wk_c)).then_inc(wc_in, 16)
            sp.dma_start(WC_raw[:, :, DC:], rows(wv_c)).then_inc(wc_in, 16)
            sp.dma_start(RAW[:], rows(wq)).then_inc(wq_in, 16)
            sp.dma_start(WK[:, 0], wk).then_inc(wkv_in, 16)
            sp.dma_start(WV[:], wv).then_inc(wkv_in, 16)
            pieces = ((I[:], ident), (ROPE_T[:], rope_t), (EARLIER[:], earlier.partition_broadcast(P)),
                      (BIAS[:, 0:GROUPS_E], g_bias.partition_broadcast(P)), (BIAS[:, GROUPS_E:], e_bias.partition_broadcast(P)),
                      (N1[:], norm1.partition_broadcast(P)), (WG[:, :, 0:GROUPS_E], rows(wg)), (WG[:, :, GROUPS_E:], rows(we)))
            assert len(pieces) == NC
            for dst, src in pieces:
                sp.dma_start(dst, src).then_inc(const_in, 16)
            sp.wait_ge(wq_lo_done, 1)
            sp.dma_start(RAW[:], rows(wo)).then_inc(wo_in, 16)

        @block.gpsimd
        def _(g):
            g.wait_ge(wkv_in, 32)
            for n in range(2):
                g.tensor_copy(WK[:, 1, n::2], WK[:, 0, 1 - n::2]).then_inc(k_swapped, 1)
            for u, (w, c, t) in enumerate(UNITS):
                g.wait_ge(multiplied, 2 * (u + 1))
                dst = (QT if w == "q" else KT_)[:, c, t * HALF:(t + 1) * HALF]
                g.tensor_tensor(dst, R[:, u % 2, 0], R[:, u % 2, 1], ALU.add).then_inc(roped, 1)

        @block.scalar
        def _(a):
            a.wait_ge(wc_in, 32)
            a.copy(flat(WC_hi[:]), flat(WC_raw[:])).then_inc(wc_hi_done, 1)
            a.wait_ge(wq_in, 16)
            a.copy(flat(WQ_hi[:]), flat(RAW[:])).then_inc(wq_hi_done, 1)
            for n in range(4):
                a.wait_ge(c_done, n + 1)
                a.copy(CT[:, n // 2, n % 2 * HALF:(n % 2 + 1) * HALF], bank(n)).then_inc(ct_copied, 1)
            for b in range(B):
                a.wait_ge(v_done, b + 1)
                a.copy(V[:, b], bank(b % 4)).then_inc(v_copied, 1)
            a.wait_ge(wo_in, 16)
            a.copy(flat(WQ_hi[:]), flat(RAW[:])).then_inc(wq_hi_done, 1)
            for k in STEPS:
                if at(k - 2):
                    b = k - 2
                    a.wait_ge(o_turned, b + 1)
                    if b:
                        a.wait_ge(y_done, b)
                    a.copy(OT_hi[:], bank(4)).then_inc(ot_hi, 1)
                if at(k - 1):
                    b = k - 1
                    for n in range(4):
                        a.wait_ge(p_turned, 4 * b + n + 1)
                        if b:
                            a.wait_ge(pv_done, b)
                        a.copy(flat(PT[:, 4 * n:4 * n + 4]), bank(5 - n % 2)).then_inc(pt_copied, 1)
                if at(k):
                    a.wait_ge(maxed, 2 * k + 2)
                    for h in range(H):
                        a.activation(S[k % 2][:, h], ps[:, h * P:(h + 1) * P], ACT.Exp, scale=HF ** -0.5,
                                     bias=mx[:, k % 2, h:h + 1]).then_inc(s_expd, 1)
                if at(k - 3):
                    b = k - 3
                    a.wait_ge(f_turned, b + 1)
                    a.copy(XT_hi[:, :, b * P:(b + 1) * P], bank(5).rearrange("p (k f) -> p k f", k=KC)).then_inc(xt_hi, 1)
                if at(k - 4):
                    a.wait_ge(g_shifted, k - 3)
                    a.activation(G[:, 18:24], G[:, 12:18], ACT.Exp).then_inc(g_expd, 1)

        def route(v, link, b):
            v.wait_ge(logits_done, b + 1)
            link(v.tensor_tensor(G[:, 0:NL], bank(7, NL), BIAS[:], ALU.add))
            link(v.tensor_reduce(G[:, 10:11], G[:, 0:2], AX.X, ALU.max))
            link(v.tensor_scalar(G[:, 12:14], G[:, 0:2], G[:, 10:11], None, ALU.subtract))
            link(v.tensor_tensor(G[:, 25:26], G[:, 1:2], G[:, 0:1], ALU.is_gt))
            link(v.tensor_scalar(G[:, 24:25], G[:, 25:26], -1.0, 1.0, ALU.mult, ALU.add))
            link(v.tensor_scalar(G[:, 26:30], G[:, 2:6], G[:, 24:25], None, ALU.mult))
            link(v.scalar_tensor_tensor(out=G[:, 26:30], in0=G[:, 6:10], scalar=G[:, 25:26], in1=G[:, 26:30], op0=ALU.mult, op1=ALU.add))
            link(v.tensor_reduce(G[:, 11:12], G[:, 26:30], AX.X, ALU.max))
            v.tensor_scalar(G[:, 14:18], G[:, 26:30], G[:, 11:12], None, ALU.subtract).then_inc(g_shifted, 1)
            v.wait_ge(g_expd, b + 1)
            link(v.tensor_reduce(G[:, 30:31], G[:, 18:20], AX.X, ALU.add))
            link(v.tensor_reduce(G[:, 31:32], G[:, 20:24], AX.X, ALU.add))
            link(v.reciprocal(G[:, 32:34], G[:, 30:32]))
            link(v.tensor_scalar(G[:, 36:40], G[:, 20:24], G[:, 33:34], G[:, 32:33], ALU.mult, ALU.mult))
            pj = G[:, 36:40].unsqueeze(1).broadcast_to([P, EPG, EPG])
            pi = G[:, 36:40].unsqueeze(2).broadcast_to([P, EPG, EPG])
            link(v.tensor_tensor(RK[:, 0], pj, pi, ALU.is_gt))
            link(v.tensor_tensor(RK[:, 1], pj, pi, ALU.is_equal))
            link(v.tensor_tensor(RK[:, 1], RK[:, 1], EARLIER[:], ALU.mult))
            link(v.tensor_tensor(RK[:, 0], RK[:, 0], RK[:, 1], ALU.add))
            link(v.tensor_reduce(G[:, 40:44], RK[:, 0], AX.X, ALU.add))
            link(v.tensor_scalar(G[:, 44:48], G[:, 40:44], 1.5, None, ALU.is_lt))
            link(v.tensor_tensor(G[:, 44:48], G[:, 44:48], G[:, 36:40], ALU.mult))
            link(v.tensor_scalar(W8[:, b, 0:EPG], G[:, 44:48], G[:, 24:25], None, ALU.mult))
            link(v.tensor_scalar(W8[:, b, EPG:], G[:, 44:48], G[:, 25:26], None, ALU.mult))

        @block.vector
        def _(v):
            c = Chain(v, vchain, 0, 0)
            link = c.link
            v.wait_ge(wc_hi_done, 1)
            v.tensor_tensor(flat(WC_lo[:]), flat(WC_raw[:]), flat(WC_hi[:]).bitcast(F32), ALU.subtract).then_inc(wc_lo_done, 1)
            v.wait_ge(wq_hi_done, 1)
            v.tensor_tensor(flat(WQ_lo[:]), flat(RAW[:]), flat(WQ_hi[:]).bitcast(F32), ALU.subtract).then_inc(wq_lo_done, 1)
            v.wait_ge(wq_lo_done, 1)
            for dst, src in ((WS_hi, WQ_hi), (WS_lo, WQ_lo)):
                for n in range(2):
                    v.tensor_copy(dst[:, :, n::2], src[:, :, 1 - n::2]).then_inc(swapped, 1)
            v.wait_ge(const_in, 16 * NC)
            for u in range(NU):
                v.wait_ge(two_done, u + 1)
                if u >= 2:
                    v.wait_ge(roped, u - 1)
                for s in range(2):
                    v.tensor_tensor(R[:, u % 2, s].rearrange("p (b f) -> p b f", f=P),
                                    bank(4 + 2 * (u % 2) + s).rearrange("p (b f) -> p b f", f=P),
                                    ROPE_T[:, s:s + 1].broadcast_to([P, HALF // P, P]), ALU.mult).then_inc(multiplied, 1)
            v.wait_ge(wq_hi_done, 2)
            v.tensor_tensor(flat(WQ_lo[:]), flat(RAW[:]), flat(WQ_hi[:]).bitcast(F32), ALU.subtract).then_inc(wq_lo_done, 1)
            for k in STEPS:
                if at(k):
                    v.wait_ge(s_done, k + 1)
                    v.tensor_reduce(mx[:, k % 2], ps[:, 0:4 * 512].rearrange("p (h f) -> p h f", f=P), AX.X, ALU.max).then_inc(maxed, 1)
                    v.wait_ge(maxed, 2 * k + 1)
                    v.tensor_scalar(mx[:, k % 2], mx[:, k % 2], -HF ** -0.5, None, ALU.mult).then_inc(maxed, 1)
                if at(k - 2):
                    b = k - 2
                    v.wait_ge(ot_hi, b + 1)
                    v.tensor_tensor(OT_lo[:], bank(4), OT_hi[:].bitcast(F32), ALU.subtract).then_inc(ot_lo, 1)
                    v.wait_ge(y_done, b + 1)
                    v.tensor_tensor(ROWS[:, b], bank(7), ROWS[:, b], ALU.add).then_inc(y_read, 1)
                    v.wait_ge(y_read, b + 1)
                    rms_scale(v, c, ROWS[:, b], ROWS[:, b], N1[:], stats[:], col[:]).then_inc(xf_done, 1)
                if at(k - 1):
                    b = k - 1
                    v.wait_ge(s_expd, H * (b + 1))
                    link(v.tensor_reduce(sm[:, 0], S[b % 2], AX.X, ALU.add))
                    link(v.reciprocal(sm[:, 1], sm[:, 0]))
                    v.wait_ge(pv_done, b + 1)
                    if b:
                        v.wait_ge(o_turned, b)
                    by_head = lambda ap: ap.rearrange("p (c j d) -> p c j d", c=4, j=4)
                    v.tensor_tensor(by_head(O[:]), by_head(bank(6)), sm[:, 1].rearrange("p (j c) -> p c j", j=4).unsqueeze(3).broadcast_to([P, 4, 4, HF]),
                                    ALU.mult).then_inc(normed, 1)
                if at(k - 3):
                    b = k - 3
                    s_ = slice(b * P, (b + 1) * P)
                    v.wait_ge(xt_hi, b + 1)
                    v.tensor_tensor(XT_lo[:, :, s_], bank(5).rearrange("p (k f) -> p k f", k=KC), XT_hi[:, :, s_].bitcast(F32),
                                    ALU.subtract).then_inc(xt_lo, 1)
                if at(k - 4):
                    route(v, link, k - 4)

        @block.tensor
        def _(t_):
            def exact(out, pairs):
                n, steps = 0, 3 * len(pairs)
                for (x_hi, x_lo), (w_hi, w_lo) in pairs:
                    for l, r in ((x_lo, w_hi), (x_hi, w_lo), (x_hi, w_hi)):
                        mm = t_.matmul(out, l, r, start=n == 0, stop=n == steps - 1)
                        n += 1
                return mm
            half = lambda t: slice(t * HALF, (t + 1) * HALF)
            t_.wait_ge(wc_lo_done, 1)
            for n in range(4):
                f_ = slice(n // 2 * DC, (n // 2 + 1) * DC)
                exact(bank(n), [((WC_hi[:, k, f_], WC_lo[:, k, f_]), (XT_hi[:, k, half(n % 2)], XT_lo[:, k, half(n % 2)]))
                                for k in range(KC)]).then_inc(c_done, 1)
            for u, (w, c, t) in enumerate(UNITS):
                if u == 0:
                    t_.wait_ge(swapped, 4)
                if w == "k" and c == 0 and t == 0:
                    t_.wait_ge(k_swapped, 2)
                    t_.wait_ge(ct_copied, 4)
                if u >= 2:
                    t_.wait_ge(multiplied, 2 * (u - 1))
                f_ = slice(c * P, (c + 1) * P)
                for s in range(2):
                    out = bank(4 + 2 * (u % 2) + s)
                    if w == "q":
                        hi, lo = ((WQ_hi, WQ_lo), (WS_hi, WS_lo))[s]
                        mm = exact(out, [((hi[:, k, f_], lo[:, k, f_]), (XT_hi[:, k, half(t)], XT_lo[:, k, half(t)])) for k in range(KC)])
                    else:
                        mm = t_.matmul(out, WK[:, s, f_], CT[:, 0, half(t)], start=True, stop=True)
                mm.then_inc(two_done, 1)
            for b in range(B):
                if b >= 4:
                    t_.wait_ge(v_copied, b - 3)
                t_.matmul(bank(b % 4), CT[:, 1, b * P:(b + 1) * P], WV[:], start=True, stop=True).then_inc(v_done, 1)
            t_.wait_ge(v_copied, B)
            t_.wait_ge(roped, NU)

            def turn(out, src):
                for j in range(KC):
                    mm = t_.transpose(out[:, j * P:(j + 1) * P], src[:, j * P:(j + 1) * P], I[:])
                return mm
            for k in STEPS:
                if at(k):
                    if k:
                        t_.wait_ge(s_expd, H * k)
                    for h in range(H):
                        q_ = slice(h % 4 * HF, (h % 4 + 1) * HF)
                        mm = t_.matmul(bank(h % 4)[:, h // 4 * P:(h // 4 + 1) * P], QT[q_, h // 4, k * P:(k + 1) * P],
                                       KT_[q_, h // 4, k * P:(k + 1) * P], start=True, stop=True)
                    mm.then_inc(s_done, 1)
                if at(k - 2):
                    b = k - 2
                    t_.wait_ge(pt_copied, 4 * (b + 1))
                    t_.wait_ge(normed, b + 1)
                    turn(bank(4), O[:]).then_inc(o_turned, 1)
                if at(k - 1):
                    b = k - 1
                    for n in range(4):
                        if n == 0 and b >= 3:
                            t_.wait_ge(xt_lo, b - 2)
                        elif n == 1 and b >= 1:
                            t_.wait_ge(ot_lo, b)
                        elif n >= 2:
                            t_.wait_ge(pt_copied, 4 * b + n - 1)
                        turn(bank(5 - n % 2), flat(S[b % 2][:, 4 * n:4 * n + 4])).then_inc(p_turned, 1)
                if at(k - 2):
                    b = k - 2
                    if b == 0:
                        t_.wait_ge(wq_lo_done, 2)
                    if b >= 3:
                        t_.wait_ge(g_shifted, b - 2)
                    t_.wait_ge(ot_lo, b + 1)
                    exact(bank(7), [((OT_hi[:, j * P:(j + 1) * P], OT_lo[:, j * P:(j + 1) * P]), (WQ_hi[:, j], WQ_lo[:, j]))
                                    for j in range(KC)]).then_inc(y_done, 1)
                if at(k - 1):
                    b = k - 1
                    t_.wait_ge(pt_copied, 4 * (b + 1))
                    if b:
                        t_.wait_ge(normed, b)
                    for n in range(H):
                        h = n % 4 * 4 + n // 4
                        mm = t_.matmul(bank(6)[:, h * HF:(h + 1) * HF], PT[:, n, :], V[:, b, h * HF:(h + 1) * HF],
                                       start=n == 0, stop=True, skip_group_check=True)
                    mm.then_inc(pv_done, 1)
                if at(k - 3):
                    b = k - 3
                    t_.wait_ge(pt_copied, 4 * min(b + 3, B) - 1)
                    t_.wait_ge(xf_done, b + 1)
                    if b:
                        t_.wait_ge(xt_lo, b)
                    turn(bank(5), ROWS[:, b]).then_inc(f_turned, 1)
                if at(k - 4):
                    b = k - 4
                    t_.wait_ge(xt_lo, b + 1)
                    t_.wait_ge(y_read, min(b + 3, B))
                    if b:
                        t_.wait_ge(g_shifted, b)
                    for j in range(KC):
                        for n, xt in enumerate((XT_lo, XT_hi)):
                            mm = t_.matmul(bank(7, NL), xt[:, j, b * P:(b + 1) * P].bitcast(F32), WG[:, j, :],
                                           start=j == 0 and n == 0, stop=j == KC - 1 and n == 1)
                    mm.then_inc(logits_done, 1)


def stage_dense(nc, x2_d, wts, norm2, ROWS, XT_hi, XT_lo, W8, out):
    w_in, w_out, w1, w2 = wts
    with ExitStack() as ctx:
        sb = lambda n, s, d=F32: ctx.enter_context(nc.sbuf_tensor("d_" + n, s, d))
        sem = lambda n: ctx.enter_context(nc.semaphore("d_" + n))
        HK = HID // P
        PW = 2 * D
        GP = 4
        TH = TOK // 512
        RAW = sb("raw", [P, GP, PW])
        W_hi = sb("w_hi", [P, 2, GP, PW], F32R)
        W_lo = sb("w_lo", [P, 2, GP, PW], F32R)
        HT_hi = sb("ht_hi", [P, HK, TOK], F32R)
        HT_lo = sb("ht_lo", [P, HK, TOK], F32R)
        SG = sb("sg", [P, 2, 512])
        HS = sb("hs", [P, 2, 512])
        W8i = sb("w8i", [P, B, 2])
        N2 = sb("n2", [P, D])
        X2 = sb("x2", [P, 2, D])
        OUT = HS
        ZERO = sb("zero", [P, 1])
        zeroed = sem("zeroed")
        stats = sb("stats", [P, 6])
        col = sb("col", [P, 8])
        ps = ctx.enter_context(nc.psum_tensor("d_ps", [P, 8 * 512], F32))
        bank = lambda n: ps[:, n * 512:(n + 1) * 512]
        raw_in = [sem(f"raw_in{q}") for q in range(GP)]
        w_hi_done, w_lo_done = sem("w_hi_done"), sem("w_lo_done")
        a_done, b_done, silu_done, h_done, h_hi, h_lo = (sem(n) for n in ("a_done", "b_done", "silu_done", "h_done", "h_hi", "h_lo"))
        out_done, added = sem("out_done"), sem("added")
        n2_in, w8i_done, vchain, final = sem("n2_in"), sem("w8i_done"), sem("vchain"), sem("final")
        x2_in, stored = [sem("x2_in0"), sem("x2_in1")], [sem("stored0"), sem("stored1")]
        block = ctx.enter_context(nc.Block())
        A_, B_ = 0, 1

        def region_free(eng, G, q):
            if isinstance(G, int) and G in (1, 3, 4):
                eng.wait_ge(b_done, TH * (GP * {1: 0, 3: 1, 4: 2}[G] + q + 1))
            elif isinstance(G, int) and G == 5:
                eng.wait_ge(out_done, B)
            elif isinstance(G, int) and G == 6:
                eng.wait_ge(b_done, 2 * TH * HK)
            elif not isinstance(G, int) or G > 6:
                eng.wait_ge(out_done, B * (G - 5))

        @block.sync
        def _(sp):
            def piece(src, G, q):
                if not isinstance(G, int) or G > 0:
                    sp.wait_ge(w_lo_done, GP * (G - 1) + q + 1)
                sp.dma_start(RAW[:, q].rearrange("p (k f) -> p k f", k=src.shape[1]), src).then_inc(raw_in[q], 16)

            def hidden_group(w, G, j):
                rows = w.rearrange("(k p) n -> p k n", p=P)
                for q in range(GP):
                    if G > 0:
                        sp.wait_ge(w_lo_done, GP * (G - 1) + q + 1)
                    dst = RAW[:, q].rearrange("p (s k f) -> p s k f", s=2, k=KC)
                    for s in range(2):
                        at = s * HID + (j + q) * P
                        sp.dma_start(dst[:, s], rows[:, :, at:at + P]).then_inc(raw_in[q], 16)

            def out_group(w, G):
                rows = w.rearrange("(k p) n -> p k n", p=P)
                for q in range(GP):
                    piece(rows[:, 2 * q:2 * q + 2, :], G, q)
            hidden_group(w_in, 0, 0)
            hidden_group(w_in, 1, GP)
            sp.dma_start(N2[:], norm2.partition_broadcast(P)).then_inc(n2_in, 16)
            for par in range(2):
                sp.dma_start(X2[:, par], x2_d[par]).then_inc(x2_in[par], 16)
            out_group(w_out, 2)
            hidden_group(w1, 3, 0)
            hidden_group(w1, 4, GP)
            with sp.Fori(0, E_ALL) as e:
                out_group(w2[bass.ds(e, 1)].rearrange("o k n -> (o k) n"), e + 5)
            for b in range(B):
                sp.wait_ge(final, b + 1)
                sp.dma_start(out[b], OUT[:, b % 2]).then_inc(stored[b % 2], 16)
                if b + 2 < B:
                    sp.dma_start(X2[:, b % 2], x2_d[b + 2]).then_inc(x2_in[b % 2], 16)
            for par in range(2):
                sp.wait_ge(stored[par], 16 * B // 2)

        def raw_value(G):
            if isinstance(G, int):
                return 16 * sum(1 if g == 2 or g >= 5 else 2 for g in range(G + 1))
            return 16 * (G + 5)

        @block.gpsimd
        def _(g):
            g.memset(ZERO[:], 0.0).then_inc(zeroed, 1)
            g.wait_ge(zeroed, 1)

            def split(G, r):
                for q in range(GP):
                    g.wait_ge(raw_in[q], raw_value(G))
                    region_free(g, G, q)
                    g.tensor_tensor(W_hi[:, r, q], RAW[:, q], ZERO[:].broadcast_to([P, PW]), ALU.add).then_inc(w_hi_done, 1)
                    g.wait_ge(w_hi_done, GP * G + q + 1)
                    g.tensor_tensor(W_lo[:, r, q], RAW[:, q], W_hi[:, r, q].bitcast(F32), ALU.subtract).then_inc(w_lo_done, 1)
            for G, r in enumerate((A_, A_, B_, A_, A_, B_, A_)):
                split(G, r)
            with g.Fori(1, E_ALL // 2) as i:
                for r in (B_, A_):
                    split(2 * i + 5 + (r == A_), r)

        def hidden_tiles(eng, body):
            def branch(n0):
                with eng.Fori(0, 2) as i:
                    for q in range(GP):
                        for t in range(TH):
                            body(i, q, t, n0 + 2 * GP * i + TH * q + t)
            return branch

        @block.scalar
        def _(a):
            def tile(i, q, t, n):
                a.wait_ge(a_done, n + 1)
                a.activation(SG[:, t], bank(2 * t), ACT.Silu).then_inc(silu_done, 1)
                a.wait_ge(h_done, n + 1)
                a.copy(HT_hi[:, bass.ds(GP * i + q, 1), t * 512:(t + 1) * 512].rearrange("p o f -> p (o f)"), HS[:, t]).then_inc(h_hi, 1)
            branch = hidden_tiles(a, tile)
            branch(0)
            branch(2 * HK)

        @block.vector
        def _(v):
            def tile(i, q, t, n):
                v.wait_ge(b_done, n + 1)
                v.wait_ge(silu_done, n + 1)
                v.tensor_tensor(HS[:, t], SG[:, t], bank(2 * t + 1), ALU.mult).then_inc(h_done, 1)
                v.wait_ge(h_hi, n + 1)
                h_ = (slice(None), bass.ds(GP * i + q, 1), slice(t * 512, (t + 1) * 512))
                v.tensor_tensor(HT_lo[h_].rearrange("p o f -> p (o f)"), HS[:, t], HT_hi[h_].bitcast(F32).rearrange("p o f -> p (o f)"),
                                ALU.subtract).then_inc(h_lo, 1)
            branch = hidden_tiles(v, tile)
            branch(0)
            for b in range(B):
                v.wait_ge(out_done, b + 1)
                v.tensor_tensor(ROWS[:, b], bank(4 + b % 4), ROWS[:, b], ALU.add).then_inc(added, 1)
            branch(2 * HK)

            def expert(i, s, last):
                u = 2 * i + s + 1
                for b in range(B):
                    v.wait_ge(out_done, B * u + b + 1)
                    v.wait_ge(added, B * (u - 1) + b + 1)
                    v.scalar_tensor_tensor(out=ROWS[:, b], in0=bank(4 + b % 4), scalar=W8i[:, b, s:s + 1], in1=ROWS[:, b],
                                           op0=ALU.mult, op1=ALU.add).then_inc(added, 1)
                    if last:
                        v.wait_ge(added, B * u + b + 1)
                        c.link(rms_scale(v, c, ROWS[:, b], ROWS[:, b], N2[:], stats[:], col[:]))
                        v.wait_ge(x2_in[b % 2], 16 * (b // 2 + 1))
                        if b >= 2:
                            v.wait_ge(stored[b % 2], 16 * (b // 2))
                        v.tensor_tensor(OUT[:, b % 2], ROWS[:, b], X2[:, b % 2], ALU.add).then_inc(final, 1)

            def weights_of(i):
                v.wait_ge(added, B * (2 * i + 1))
                v.tensor_copy(W8i[:], W8[:, :, bass.ds(2 * i, 2)]).then_inc(w8i_done, 1)
                v.wait_ge(w8i_done, i + 1)
            c = Chain(v, vchain, 0, 0)
            v.wait_ge(n2_in, 16)
            with v.Fori(0, E_ALL // 2 - 1) as i:
                weights_of(i)
                expert(i, 0, False)
                expert(i, 1, False)
            i = E_ALL // 2 - 1
            weights_of(i)
            expert(i, 0, False)
            expert(i, 1, True)

        @block.tensor
        def _(t_):
            def branch(n0, G0):
                def turn(i, first):
                    for q in range(GP):
                        t_.wait_ge(w_lo_done, GP * (G0 + i) + q + 1)
                        for t in range(TH):
                            n = n0 + 2 * GP * i + TH * q + t
                            if not first or TH * q + t >= 2:
                                t_.wait_ge(h_done, n - 1)
                            for s in range(2):
                                m = 0
                                for k in range(KC):
                                    at = slice((s * KC + k) * P, (s * KC + k + 1) * P)
                                    for w, x_ in ((W_lo, XT_hi), (W_hi, XT_lo), (W_hi, XT_hi)):
                                        mm = t_.matmul(bank(2 * t + s), w[:, A_, q, at], x_[:, k, t * 512:(t + 1) * 512],
                                                       start=m == 0, stop=m == 3 * KC - 1)
                                        m += 1
                                mm.then_inc((a_done, b_done)[s], 1)
                if n0 == 0:
                    turn(0, True)
                    turn(1, False)
                else:
                    with t_.Fori(0, 2) as i:
                        turn(i, False)

            def unit(u, G, r):
                t_.wait_ge(w_lo_done, GP * (G + 1))
                for b in range(B):
                    if b >= 4 or not isinstance(u, int) or u > 0:
                        t_.wait_ge(added, B * u + b - 3)
                    m = 0
                    for k in range(HK):
                        for h, w in ((HT_lo, W_hi), (HT_hi, W_lo), (HT_hi, W_hi)):
                            mm = t_.matmul(bank(4 + b % 4), h[:, k, b * P:(b + 1) * P], w[:, r, k // 2, (k % 2) * D:(k % 2 + 1) * D],
                                           start=m == 0, stop=m == 3 * HK - 1)
                            m += 1
                    mm.then_inc(out_done, 1)
            branch(0, 0)
            t_.wait_ge(h_lo, TH * HK)
            unit(0, 2, B_)
            branch(TH * HK, 3)
            t_.wait_ge(h_lo, 2 * TH * HK)
            with t_.Fori(0, E_ALL // 2) as i:
                unit(2 * i + 1, 2 * i + 5, B_)
                unit(2 * i + 2, 2 * i + 6, A_)


def clear_semaphores(nc):
    nums = sorted(nc.released_uncleared_semaphores)
    with nc.Block() as block:
        @block.gpsimd
        def _(g):
            g.sem_clear(range(nums[0], nums[-1] + 1))


def program(nc, x, ctx_t, mask, ident, rope, causal, rope_t, earlier, wq, wkv, front, attend, w_proj, ffn, dense, norm2, out):
    scratch = lambda n, s: nc.dram_tensor(n, s, F32, kind="Internal").ap()
    q_hi = scratch("q_hi_scratch", (PAIRS, P, TOK))
    q_lo = scratch("q_lo_scratch", (PAIRS, P, TOK))
    o_part = scratch("o_part_scratch", (NIT, VW, GRP, GW))
    x1 = scratch("x1_scratch", (B, P, D))
    x2 = scratch("x2_scratch", (B, P, D))
    with ExitStack() as ctx:
        sb = lambda n, s, d=F32: ctx.enter_context(nc.sbuf_tensor(n, s, d))
        WKV = sb("wkv_hi", [P, KC, 2 * INNER], F32R), sb("wkv_lo", [P, KC, 2 * INNER], F32R)
        C = sb("c_hi", [P, 2, KC, BLK], F32R), sb("c_lo", [P, 2, KC, BLK], F32R)
        RAW = sb("raw", [P, 2, KC, BLK])
        stage_queries(nc, x, wq, wkv, ctx_t, ident, q_hi, q_lo, WKV, C, RAW)
        stage_cross(nc, ctx_t, mask, q_hi, q_lo, o_part, WKV, C, RAW)
    clear_semaphores(nc)
    with ExitStack() as ctx:
        sb = lambda n, s, d=F32: ctx.enter_context(nc.sbuf_tensor(n, s, d))
        ROWS = sb("rows", [P, B, D])
        XT_hi = sb("xt_hi", [P, KC, TOK], F32R)
        XT_lo = sb("xt_lo", [P, KC, TOK], F32R)
        W8 = sb("w8", [P, B, E_ALL])
        with ExitStack() as inner:
            sb = lambda n, s, d=F32: inner.enter_context(nc.sbuf_tensor(n, s, d))
            keep = (XT_hi, XT_lo, sb("nqt", [QL, TOK]), sb("ckt", [KVL, TOK]), sb("krt", [P, B, ROPE]), sb("gate", [P, B, 3]))
            stage_front(nc, x, o_part, x1, front, (ident, rope), keep)
            stage_attend(nc, attend, (ident, rope, causal), keep, ROWS)
        stage_project(nc, x1, x2, w_proj, ident, ROWS, XT_hi, XT_lo)
        stage_ffn_attend(nc, ffn, (ident, rope_t, earlier), ROWS, XT_hi, XT_lo, W8)
        stage_dense(nc, x2, dense, norm2, ROWS, XT_hi, XT_lo, W8, out)


FRONT = ["L0_xattn_Wo", "L0_xattn_bo"] + ["L0_attn_" + n for n in ("w_cq", "g_qnorm", "w_ckv", "g_kvnorm", "w_krope", "w_gate")]
ATTEND = ["L0_attn_" + n for n in ("w_dq_nope", "w_dq_rope", "w_dk_nope", "w_dv", "w_selk", "w_selv", "w_wink", "w_winv")]
FFN = ["L0_ffn_" + n for n in ("Wq", "Wk_c", "Wv_c", "Wk", "Wv", "Wo", "Wg_gate", "We_gate", "group_bias", "expert_bias", "norm1_w")]
DENSE = ["L0_ffn_" + n for n in ("W_shared_in", "W_shared_out", "W1_shared", "W2_experts")]


def tables():
    angle = np.outer(np.arange(P), 10000.0 ** (-np.arange(0, ROPE, 2) / ROPE))
    cos, sin = np.cos(angle), np.sin(angle)
    rope = np.stack([np.concatenate([cos, cos], 1), np.concatenate([sin, -sin], 1)], 1)
    angle = np.outer(np.arange(P), 10000.0 ** (-np.arange(0, HF, 2) / HF))
    cos, sin = np.cos(angle), np.sin(angle)
    pairs = lambda a, b: np.tile(np.stack([a, b], 2).reshape(P, HF).T, (P // HF, 1))
    rope_t = np.stack([pairs(cos, cos), pairs(-sin, sin)], 1)
    causal = np.zeros((P, 3, P))
    causal[:, 0] = causal[:, 2] = np.triu(np.full((P, P), NEG), 1)
    f = lambda a: np.ascontiguousarray(a, np.float32)
    return {"ident": f(np.eye(P)), "rope": f(rope), "causal": f(causal), "rope_t": f(rope_t), "earlier": f(np.tril(np.ones((EPG, EPG)), -1))}


def kernel(**inputs):
    import concourse.bacc as bacc
    from concourse.bass_utils import run_bass_kernel_spmd

    nc = bacc.Bacc("TRN2", target_bir_lowering=False, num_devices=1)
    ctx = np.asarray(inputs["ctx_1024"]).reshape(B * M // BLK, BLK, KC, P)
    mask = np.asarray(inputs["mask_BxS2_bk1"]).reshape(B, M // P, P)
    arrays = {
        "x": np.asarray(inputs["x"]),
        "ctx_t": ctx.transpose(0, 3, 2, 1),
        "mask": np.ascontiguousarray(mask.transpose(2, 0, 1)).reshape(P, P),
        **tables(),
        **{n: np.asarray(inputs[n]) for n in ["L0_xattn_Wq", "L0_xattn_Wkv", *FRONT, *ATTEND, "L0_attn_w_proj", *FFN, *DENSE, "L0_ffn_norm2_w"]},
    }
    arrays = {"in_" + n: np.ascontiguousarray(a) for n, a in arrays.items()}
    ap = {n[3:]: nc.dram_tensor(n, a.shape, mybir.dt.from_np(a.dtype), kind="ExternalInput").ap() for n, a in arrays.items()}
    out = nc.dram_tensor("out", (B, P, D), F32, kind="ExternalOutput").ap()
    program(nc, *(ap[n] for n in ("x", "ctx_t", "mask", "ident", "rope", "causal", "rope_t", "earlier", "L0_xattn_Wq", "L0_xattn_Wkv")),
            [ap[n] for n in FRONT], [ap[n] for n in ATTEND], ap["L0_attn_w_proj"], [ap[n] for n in FFN], [ap[n] for n in DENSE], ap["L0_ffn_norm2_w"], out)
    r = run_bass_kernel_spmd(nc, [arrays], core_ids=[0])
    return r.results[0]["out"]
```

```python
from contextlib import ExitStack

import numpy as np
import concourse.bass as bass
from concourse import mybir

F32 = mybir.dt.float32
F32R = mybir.dt.float32r
I32 = mybir.dt.int32
U8 = mybir.dt.uint8
ALU = mybir.AluOpType
ACT = mybir.ActivationFunctionType
AX = mybir.AxisListType

P = 128
B = 8
D = 512
KC = D // P
TOK = B * P
M = 2048
H = 16
DH = 64
INNER = H * DH
PAIRS = H // 2
BLK = 512
BPI = 2
NIT = B * M // (BLK * BPI)
KT = BLK // P
GRP = 4
SLOTS = GRP * KT
SPI = SLOTS * BPI
LAG = 2
VW = DH + 1
GW = 4 * P
LN_EPS = 1e-5
CLIP = 5.0
EXP_HI, EXP_LO = float(np.exp(CLIP)), float(np.exp(-CLIP))


RSQRT_GUESS = 0x5F3759DF

NOPE, ROPE, VH = 32, 64, 32
QK = NOPE + ROPE
QL, KVL = 96, 32
NEG = -3.0e38
RMS_EPS = 1e-6


class Chain:

    def __init__(self, eng, sem, i, length):
        self.eng, self.sem, self.i, self.length, self.n = eng, sem, i, length, 0

    def link(self, ins):
        self.n += 1
        ins.then_inc(self.sem, 1)
        self.eng.wait_ge(self.sem, self.i * self.length + self.n)

    def end(self):
        assert self.n == self.length, self.n


def rsqrt_cols(v, c, y, x, tmp):
    c.link(v.tensor_scalar(tmp.bitcast(I32), x.bitcast(I32), 1, None, ALU.arith_shift_right))
    c.link(v.tensor_scalar(y.bitcast(I32), tmp.bitcast(I32), -1, RSQRT_GUESS, ALU.mult, ALU.add))
    for n in range(3):
        c.link(v.tensor_tensor(tmp, y, y, ALU.mult))
        c.link(v.tensor_tensor(tmp, tmp, x, ALU.mult))
        c.link(v.tensor_scalar(tmp, tmp, -0.5, 1.5, ALU.mult, ALU.add))
        c.link(v.tensor_tensor(y, y, tmp, ALU.mult))


def moments(v, c, out, x, stats, carry):
    c.link(v.bn_stats(stats, x))
    v.tensor_copy(carry, stats[:, 0:1])
    c.link(v.bn_aggr(out, stats))


def layernorm_(v, c, out, x, stats, col):
    moments(v, c, col[:, 0:2], x, stats, col[:, 5:6])
    c.link(v.tensor_scalar(col[:, 2:3], col[:, 1:2], LN_EPS, None, ALU.add))
    rsqrt_cols(v, c, col[:, 3:4], col[:, 2:3], col[:, 4:5])
    return v.tensor_scalar(out, x, col[:, 0:1], col[:, 3:4], ALU.subtract, ALU.mult)


def heads(ap, h):
    return ap.rearrange("p (h d) -> p h d", h=h)


def flat(ap):
    return ap.rearrange("p k f -> p (k f)")


def stage_queries(nc, x, wq, wkv, ctx_t, ident, q_hi_d, q_lo_d, WKV, C, RAW):
    (W_hi, W_lo), (C_hi, C_lo) = WKV, C
    with ExitStack() as ctx:
        sb = lambda n, s, d=F32: ctx.enter_context(nc.sbuf_tensor("qa_" + n, s, d))
        sem = lambda n: ctx.enter_context(nc.semaphore("qa_" + n))
        QR = 3
        I = sb("ident", [P, P])
        WQ_hi = sb("wq_hi", [P, KC, INNER], F32R)
        WQ_lo = sb("wq_lo", [P, KC, INNER], F32R)
        X = sb("x", [P, B, D])
        XT_hi = sb("xt_hi", [P, KC, TOK], F32R)
        XT_lo = sb("xt_lo", [P, KC, TOK], F32R)
        stats = sb("stats", [P, 6])
        mom = sb("mom", [P, B, 2])
        rs = sb("rs", [P, 3, B])
        QH = sb("qh", [P, QR, 512], F32R)
        QL_ = sb("ql", [P, QR, 512], F32R)
        ps_t = ctx.enter_context(nc.psum_tensor("qa_pst", [P, 2, 512], F32))
        ps_q = ctx.enter_context(nc.psum_tensor("qa_psq", [P, 2, 512], F32))
        ident_in, raw_in, x_in = sem("ident_in"), [sem("raw_in0"), sem("raw_in1")], [sem(f"x_in{b}") for b in range(B)]
        hi_split, lo_split = sem("hi_split"), sem("lo_split")
        vchain, normed, turned, xt_hi, xt_lo = sem("vchain"), sem("normed"), sem("turned"), sem("xt_hi_done"), sem("xt_lo_done")
        q_done, hi_done, lo_done, q_out = sem("q_done"), sem("hi_done"), sem("lo_done"), [sem(f"out{n}") for n in range(QR)]
        GROUPS = [(c, t) for t in range(2) for c in range(PAIRS)]
        NQ = len(GROUPS)
        block = ctx.enter_context(nc.Block())
        HB = B // 2
        piece_of = lambda w, n: flat(w[:, 2 * n:2 * n + 2])
        PIECES = [tuple(piece_of(w, n) for w in (WQ_hi, WQ_lo)) for n in range(2)]
        PIECES += [(W_hi[:, k], W_lo[:, k]) for k in range(KC)]
        PIECES += [tuple(flat(c[:, n]) for c in (C_hi, C_lo)) for n in range(2)]
        raw = lambda n: flat(RAW[:, n % 2])

        @block.sync
        def _(sp):
            def load(n):
                if n >= 2:
                    sp.wait_ge(lo_split, n - 1)
                if n < 2:
                    dst = RAW[:, n].rearrange("p k f -> p (k f)").rearrange("p (k f) -> p k f", k=2)
                    sp.dma_start(dst, wq.rearrange("(k p) n -> p k n", p=P)[:, 2 * n:2 * n + 2]).then_inc(raw_in[n % 2], 16)
                elif n < 2 + KC:
                    sp.dma_start(raw(n), wkv[(n - 2) * P:(n - 1) * P, :]).then_inc(raw_in[n % 2], 16)
                else:
                    sp.dma_start(RAW[:, n % 2], ctx_t[n - 2 - KC]).then_inc(raw_in[n % 2], 16)

            def store(n):
                c, t = GROUPS[n]
                sp.wait_ge(lo_done, n + 1)
                for q_d, part in ((q_hi_d, QH), (q_lo_d, QL_)):
                    sp.dma_start(q_d[c, :, t * 512:(t + 1) * 512], part[:, n % QR, :].bitcast(F32)).then_inc(q_out[n % QR], 16)
            sp.dma_start(I[:], ident).then_inc(ident_in, 16)
            for b in range(HB):
                sp.dma_start(X[:, b, :], x[b]).then_inc(x_in[b], 16)
            load(0)
            load(1)
            for b in range(HB, B):
                sp.dma_start(X[:, b, :], x[b]).then_inc(x_in[b], 16)
            for n in range(2, 6):
                load(n)
            store(0)
            store(1)
            load(6)
            store(2)
            store(3)
            load(7)
            for n in range(4, NQ):
                store(n)
            for n in range(QR):
                sp.wait_ge(q_out[n], 32 * len(range(n, NQ, QR)))

        @block.gpsimd
        def _(g):
            for n, (hi, lo) in enumerate(PIECES):
                g.wait_ge(hi_split, n + 1)
                g.tensor_tensor(lo, raw(n), hi.bitcast(F32), ALU.subtract).then_inc(lo_split, 1)

        @block.vector
        def _(v):
            c = Chain(v, vchain, 0, 0)
            for hb in range(2):
                bs = range(hb * HB, (hb + 1) * HB)
                for b in bs:
                    v.wait_ge(x_in[b], 16)
                    moments(v, c, mom[:, b], X[:, b], stats[:], rs[:, 2, 0:1])
                s_ = slice(hb * HB, (hb + 1) * HB)
                c.link(v.tensor_scalar(rs[:, 0, s_], mom[:, s_, 1], LN_EPS, None, ALU.add))
                rsqrt_cols(v, c, rs[:, 1, s_], rs[:, 0, s_], rs[:, 2, s_])
                for b in bs:
                    v.tensor_scalar(X[:, b], X[:, b], mom[:, b, 0:1], rs[:, 1, b:b + 1], ALU.subtract, ALU.mult).then_inc(normed, 1)
                for b in bs:
                    v.wait_ge(xt_hi, b + 1)
                    t_ = slice(b * P, (b + 1) * P)
                    v.tensor_tensor(XT_lo[:, :, t_], ps_t[:, b % 2].rearrange("p (k f) -> p k f", k=KC), XT_hi[:, :, t_].bitcast(F32),
                                    ALU.subtract).then_inc(xt_lo, 1)
            for n in range(NQ):
                v.wait_ge(hi_done, n + 1)
                v.tensor_tensor(QL_[:, n % QR, :], ps_q[:, n % 2, :], QH[:, n % QR, :].bitcast(F32), ALU.subtract).then_inc(lo_done, 1)

        @block.scalar
        def _(a):
            def split(n):
                a.wait_ge(raw_in[n % 2], 16 * (n // 2 + 1))
                a.copy(PIECES[n][0], raw(n)).then_inc(hi_split, 1)

            def turned_hi(b):
                a.wait_ge(turned, b + 1)
                a.copy(XT_hi[:, :, b * P:(b + 1) * P], ps_t[:, b % 2].rearrange("p (k f) -> p k f", k=KC)).then_inc(xt_hi, 1)
            split(0)
            split(1)
            for b in range(B):
                turned_hi(b)
            split(2)
            split(3)
            for n in range(NQ):
                a.wait_ge(q_done, n + 1)
                if n >= QR:
                    a.wait_ge(q_out[n % QR], 32 * (n // QR))
                a.copy(QH[:, n % QR, :], ps_q[:, n % 2, :]).then_inc(hi_done, 1)
                if n in (0, 2, 4, 6):
                    split(4 + n // 2)

        @block.tensor
        def _(t_):
            t_.wait_ge(ident_in, 16)
            for b in range(B):
                t_.wait_ge(normed, b + 1)
                if b >= 2:
                    t_.wait_ge(xt_lo, b - 1)
                for k in range(KC):
                    mm = t_.transpose(ps_t[:, b % 2, k * P:(k + 1) * P], X[:, b, k * P:(k + 1) * P], I[:])
                mm.then_inc(turned, 1)
            t_.wait_ge(lo_split, 2)
            t_.wait_ge(xt_lo, B)
            for n, (c, t) in enumerate(GROUPS):
                if n >= 2:
                    t_.wait_ge(lo_done, n - 1)
                m = 0
                for k in range(KC):
                    for w, x_ in ((WQ_lo, XT_hi), (WQ_hi, XT_lo), (WQ_hi, XT_hi)):
                        mm = t_.matmul(ps_q[:, n % 2, :], w[:, k, c * P:(c + 1) * P], x_[:, k, t * 512:(t + 1) * 512],
                                       start=m == 0, stop=m == 3 * KC - 1)
                        m += 1
                mm.then_inc(q_done, 1)


def stage_cross(nc, ctx_t, mask, q_hi_d, q_lo_d, o_part, WKV, C, RAW):
    (W_hi, W_lo), (C_hi, C_lo) = WKV, C
    with ExitStack() as ctx:
        sb = lambda n, s, d=F32: ctx.enter_context(nc.sbuf_tensor(n, s, d))
        sem = lambda n: ctx.enter_context(nc.semaphore(n))
        K_hi = sb("k_hi", [P, PAIRS, BLK], F32R)
        K_lo = sb("k_lo", [P, PAIRS, BLK], F32R)
        V_hi = sb("v_hi", [P, KT, H, VW], F32R)
        V_lo = sb("v_lo", [P, KT, H, VW], F32R)
        Q_hi = sb("q_hi", [P, PAIRS, 2 * P], F32R)
        Q_lo = sb("q_lo", [P, PAIRS, 2 * P], F32R)
        E = sb("e", [P, 2, 512])
        E_hi = sb("e_hi", [P, 2, 512], F32R)
        E_lo = sb("e_lo", [P, 2, 512], F32R)
        O_sb = sb("o_sb", [VW, GW])
        mask_u8 = sb("mask_u8", [P, P], U8)
        top = sb("top", [P, P])
        topi = sb("topi", [P, SPI // GRP])
        ps_s = ctx.enter_context(nc.psum_tensor("ps_s", [P, 2, 512], F32))
        ps_p = ctx.enter_context(nc.psum_tensor("ps_p", [P, 2, 512], F32))
        ps_o = ctx.enter_context(nc.psum_tensor("ps_o", [P, GRP, 512], F32))
        mask_in = sem("mask_in")
        raw_in = [sem("raw_in0"), sem("raw_in1")]
        q_in = [sem(f"q_in{g}") for g in range(GRP)]
        zeroed, ones_set = sem("zeroed"), sem("ones_set")
        top_done, topi_done = sem("top_done"), sem("topi_done")
        chi_done, clo_done = sem("chi_done"), sem("clo_done")
        proj_done = sem("proj_done")
        kv_hi, kv_lo = sem("kv_hi"), sem("kv_lo")
        scored, expd, clipped = sem("scored"), sem("expd"), sem("clipped")
        e_hi, e_lo = sem("e_hi_done"), sem("e_lo_done")
        pv_done = sem("pv_done")
        o_copied, o_out = sem("o_copied"), sem("o_out")
        block = ctx.enter_context(nc.Block())

        K, V = "K", "V"
        AHEAD = [(K, c) for c in range(6)] + [(V, 0, t) for t in range(KT)]
        IN_SLOT = {0: (K, 6, 0), 1: (K, 7, 0), 2: (V, 1, 0, 0), 3: (V, 1, 1, 0), 6: (V, 1, 2, 0), 7: (V, 1, 3, 0),
                   4: (K, 0, 1), 5: (K, 1, 1), 8: (K, 2, 1), 9: (K, 3, 1), 12: (K, 4, 1), 13: (K, 5, 1),
                   10: (V, 0, 0, 1), 11: (V, 0, 1, 1), 14: (V, 0, 2, 1), 15: (V, 0, 3, 1)}
        NA = len(AHEAD)
        SPLIT_SLOT = 10

        def group_of(s):
            g = IN_SLOT[s % SLOTS]
            return g[:-1], (s // SLOTS + g[-1]) % 2

        def has_group(s, last):
            return not (last and s >= SLOTS and IN_SLOT[s % SLOTS][-1])

        def before(s, last):
            return sum(has_group(x, last) for x in range(s))

        def has_split(s, last):
            return not last and SPLIT_SLOT <= s % SLOTS < SPLIT_SLOT + KC

        def over_iterations(eng, body):
            body(0, True, False)
            with eng.Fori(1, NIT - 1) as i:
                body(i, False, False)
            body(NIT - 1, False, True)

        @block.sync
        def _(sp):
            sp.dma_start(mask_u8[:], mask).then_inc(mask_in, 16)

            def queries(i, g):
                b0 = (i // 2) * P
                for par, (dst, src) in enumerate(((Q_hi, q_hi_d), (Q_lo, q_lo_d))):
                    for hh in range(2):
                        sp.dma_start(dst[hh * DH:(hh + 1) * DH, 2 * g:2 * g + 2, hh * P:(hh + 1) * P].bitcast(F32),
                                     src[2 * g:2 * g + 2, hh * DH:(hh + 1) * DH, bass.ds(b0, P)].rearrange("c p t -> p c t")
                                     ).then_inc(q_in[g], 16)
            sp.wait_ge(zeroed, 2)
            for g in range(GRP):
                queries(0, g)

            def body(i, first, last):
                for s in range(SPI):
                    S = i * SPI + s
                    blk, r = divmod(s, SLOTS)
                    if r == 0 and not last:
                        if not first:
                            sp.wait_ge(clo_done, KC * (2 * i + blk - 1))
                        nxt = 2 * i + blk + 2
                        sp.dma_start(RAW[:, blk], ctx_t[bass.ds(nxt, 1)].rearrange("o p k f -> (o p) k f")).then_inc(raw_in[blk], 16)
                    if not last and s >= SLOTS and r % KT == KT - 1:
                        sp.wait_ge(scored, S + 1)
                        queries(i + 1, r // KT)
                    g = (s - SLOTS - KT - LAG + 1)
                    if (g >= 0 and g % KT == 0 and g // KT < GRP - 1) or (s == LAG - 1 and not first):
                        gg = GRP - 1 if s < SLOTS else g // KT
                        ii = i - 1 if s < SLOTS else i
                        sp.wait_ge(o_copied, GRP * ii + gg + 1)
                        sp.dma_start(o_part[bass.ds(ii, 1), :, gg].rearrange("o p f -> (o p) f"), O_sb[:]).then_inc(o_out, 16)
            over_iterations(sp, body)
            sp.wait_ge(o_copied, GRP * NIT)
            sp.dma_start(o_part[NIT - 1, :, GRP - 1], O_sb[:]).then_inc(o_out, 16)
            sp.wait_ge(o_out, 16 * GRP * NIT)

        @block.gpsimd
        def _(g):
            for Q in (Q_hi, Q_lo):
                g.memset(Q[:].bitcast(F32), 0.0).then_inc(zeroed, 1)

            def body(i, first, last):
                for s in range(SPI):
                    S = i * SPI + s
                    if has_split(s, last):
                        blk, k = s // SLOTS, s % SLOTS - SPLIT_SLOT
                        g.wait_ge(chi_done, KC * (2 * i + blk) + k + 1)
                        g.tensor_tensor(C_lo[:, blk, k, :], RAW[:, blk, k, :], C_hi[:, blk, k, :].bitcast(F32),
                                        ALU.subtract).then_inc(clo_done, 1)
                    g.wait_ge(e_hi, S + 1)
                    g.tensor_tensor(E_lo[:, s % 2, :], E[:, s % 2, :], E_hi[:, s % 2, :].bitcast(F32), ALU.subtract
                                    ).then_inc(e_lo, 1)
            over_iterations(g, body)

        def kv_slice(hi, kind):
            if kind[0] == K:
                return (K_hi if hi else K_lo)[:, kind[1], :]
            return (V_hi if hi else V_lo)[:, kind[2], 8 * kind[1]:8 * kind[1] + 8, 0:DH]

        def ps_view(G, kind):
            out = ps_p[:, G % 2, :]
            return out if kind[0] == K else out.rearrange("p (h d) -> p h d", d=DH)

        @block.scalar
        def _(a):
            def evac_hi(par, kind, value):
                a.wait_ge(proj_done, value)
                a.copy(kv_slice(True, kind), ps_view(par, kind)).then_inc(kv_hi, 1)

            for G, kind in enumerate(AHEAD):
                evac_hi(G, kind, G + 1)

            def body(i, first, last):
                for s in range(SPI):
                    S = i * SPI + s
                    if s and has_group(s - 1, last):
                        n = before(s, last)
                        evac_hi(n - 1, group_of(s - 1)[0], NA + i * SPI + n)
                    a.wait_ge(scored, S + 1)
                    if not (first and s < 2):
                        a.wait_ge(e_lo, S - 1)
                    a.activation(E[:, s % 2, :], ps_s[:, s % 2, :], ACT.Exp, scale=DH ** -0.5).then_inc(expd, 1)
                    if has_split(s, last):
                        blk, k = s // SLOTS, s % SLOTS - SPLIT_SLOT
                        if k == 0:
                            a.wait_ge(raw_in[blk], 16 * (i + 1))
                            a.wait_ge(proj_done, NA + S - 2)
                        a.copy(C_hi[:, blk, k, :], RAW[:, blk, k, :]).then_inc(chi_done, 1)
                    g = s - SLOTS - KT - LAG + 1
                    if g >= 0 and g % KT == 0 and g // KT < GRP - 1:
                        copy_out(g // KT, i, S)
                    if s == LAG - 1 and not first:
                        copy_out(GRP - 1, i - 1, S)
                if not last:
                    evac_hi(SPI - 1, group_of(SPI - 1)[0], NA + S + 1)

            def copy_out(gg, i, S):
                a.wait_ge(pv_done, S - LAG + 1)
                n = GRP * i + gg
                if not isinstance(n, int) or n > 0:
                    a.wait_ge(o_out, 16 * n)
                a.copy(O_sb[:], ps_o[0:VW, gg, 0:GW]).then_inc(o_copied, 1)
            over_iterations(a, body)
            copy_out(GRP - 1, NIT - 1, SPI * NIT + LAG - 1)

        @block.vector
        def _(v):
            v.memset(V_hi[:, :, :, DH:VW].bitcast(F32), 1.0).then_inc(ones_set, 1)
            v.memset(V_lo[:, :, :, DH:VW].bitcast(F32), 0.0).then_inc(ones_set, 1)
            v.wait_ge(mask_in, 16)
            v.tensor_scalar(top[:], mask_u8[:], EXP_HI - EXP_LO, EXP_LO, ALU.mult, ALU.add).then_inc(top_done, 1)
            v.wait_ge(top_done, 1)

            def evac_lo(par, kind, value):
                v.wait_ge(kv_hi, value)
                v.tensor_tensor(kv_slice(False, kind), ps_view(par, kind), kv_slice(True, kind).bitcast(F32),
                                ALU.subtract).then_inc(kv_lo, 1)
            for G, kind in enumerate(AHEAD):
                evac_lo(G, kind, G + 1)

            def body(i, first, last):
                n0 = i * (SPI // GRP)
                for s in range(SPI):
                    S = i * SPI + s
                    if s == 0:
                        v.tensor_copy(topi[:], top[:, bass.ds(n0, SPI // GRP)]).then_inc(topi_done, 1)
                        v.wait_ge(topi_done, i + 1)
                    if s and has_group(s - 1, last):
                        n = before(s, last)
                        evac_lo(n - 1, group_of(s - 1)[0], NA + i * SPI + n)
                    kt = (s // SLOTS) * KT + s % KT
                    v.wait_ge(expd, S + 1)
                    v.tensor_scalar(E[:, s % 2, :], E[:, s % 2, :], topi[:, kt:kt + 1], EXP_LO, ALU.min, ALU.max
                                    ).then_inc(clipped, 1)
                    if not (first and s < LAG):
                        v.wait_ge(pv_done, S - 1)
                    v.wait_ge(clipped, S + 1)
                    v.tensor_copy(E_hi[:, s % 2, :], E[:, s % 2, :]).then_inc(e_hi, 1)
                if not last:
                    evac_lo(SPI - 1, group_of(SPI - 1)[0], NA + S + 1)
            over_iterations(v, body)

        @block.tensor
        def _(t):
            def project(kind, cb, par):
                n = 0
                for k in range(KC):
                    for w, c in ((W_lo, C_hi), (W_hi, C_lo), (W_hi, C_hi)):
                        if kind[0] == K:
                            lhs, rhs = w[:, k, kind[1] * P:(kind[1] + 1) * P], c[:, cb, k, :]
                        else:
                            lhs = c[:, cb, k, kind[2] * P:(kind[2] + 1) * P]
                            rhs = w[:, k, INNER + kind[1] * 512:INNER + (kind[1] + 1) * 512]
                        mm = t.matmul(ps_p[:, par % 2, :], lhs, rhs, start=n == 0, stop=n == 3 * KC - 1)
                        n += 1
                mm.then_inc(proj_done, 1)

            def values(s, value):
                s = s % SPI
                g, kt = s % SLOTS // KT, s % KT
                t.wait_ge(e_lo, value)
                for j in range(4):
                    h = 4 * g + j
                    for n, (e, vv) in enumerate(((E_lo, V_hi), (E_hi, V_lo), (E_hi, V_hi))):
                        mm = t.matmul(ps_o[0:VW, g, j * P:(j + 1) * P], vv[:, kt, h, :], e[:, s % 2, j * P:(j + 1) * P],
                                      start=(s < SLOTS and kt == 0 and j == 0 and n == 0),
                                      stop=(s >= SLOTS and kt == KT - 1 and n == 2), skip_group_check=True)
                mm.then_inc(pv_done, 1)

            for G, kind in enumerate(AHEAD):
                if G >= 2:
                    t.wait_ge(kv_lo, G - 1)
                project(kind, 0, G)
            t.wait_ge(ones_set, 2)
            t.wait_ge(zeroed, 2)

            def body(i, first, last):
                for s in range(SPI):
                    S = i * SPI + s
                    g, kt = s % SLOTS // KT, s % KT
                    t.wait_ge(kv_lo, NA + i * SPI + (before(s - 1, last) if s else -1))
                    if s < SLOTS and kt == 0:
                        t.wait_ge(q_in[g], 64 * (i + 1))
                    if not (first and s < 2):
                        t.wait_ge(expd, S - 1)
                    for pr in range(2):
                        c = 2 * g + pr
                        for n, (k_, q_) in enumerate(((K_lo, Q_hi), (K_hi, Q_lo), (K_hi, Q_hi))):
                            mm = t.matmul(ps_s[:, s % 2, pr * 256:(pr + 1) * 256], k_[:, c, kt * P:(kt + 1) * P],
                                          q_[:, c, :], start=n == 0, stop=n == 2)
                    mm.then_inc(scored, 1)
                    if has_group(s, last):
                        kind, cb = group_of(s)
                        if s % SLOTS == 4 and not (first and s < SLOTS):
                            t.wait_ge(clo_done, KC * (2 * i + s // SLOTS))
                        project(kind, cb, before(s, last))
                    if not (first and s < LAG):
                        u = s - LAG
                        if s % SPI >= LAG and u < SLOTS and u % KT == 0:
                            if not first:
                                t.wait_ge(o_copied, GRP * (i - 1) + u // KT + 1)
                        values(u, S - LAG + 1)

            over_iterations(t, body)
            for s in range(SPI - LAG, SPI):
                values(s, SPI * (NIT - 1) + s + 1)


OV = DH + 1


G4 = 4
NR = H // G4
GK, GV = G4 * QK, G4 * VH
NW = 2 * GK + 2 * GV


def round_weights(wts, RAW, g):
    at, out = 0, []
    for w, n in zip(wts, (GK, GK, GV, GV)):
        out.append((RAW[:, :, at:at + n], w.rearrange("(k p) n -> p k n", p=P)[:, :, bass.ds(g * n, n)]))
        at += n
    return out


def stage_front(nc, x, o_part, x1_d, wts, tables, keep, ROWS, prefetch):
    wo, bo, w_cq, g_q, w_ckv, g_kv, w_kr, w_gate = wts
    ident, rope = tables
    XT_hi, XT_lo, NQT, CKT, KRT, GATE = keep
    with ExitStack() as ctx:
        sb = lambda n, s, d=F32: ctx.enter_context(nc.sbuf_tensor("t_" + n, s, d))
        I = sb("ident", [P, P])
        ROPE_T = sb("rope", [P, 2, ROPE])
        MEAN = sb("mean", [P, P])
        BO = sb("bo", [P, D])
        GQ = sb("gq", [P, QL + KVL])
        WO_raw = sb("wo_raw", [P, INNER // P, D])
        WO_hi = sb("wo_hi", [P, INNER // P, D], F32R)
        WO_lo = sb("wo_lo", [P, INNER // P, D], F32R)
        NS = QL + KVL + ROPE + 3
        WS = sb("ws", [P, KC, NS])
        OP = sb("op", [OV, 2, 2, H * P])
        OS = sb("os", [OV, 2, H * P])
        X = sb("x", [P, 2, D])
        REC = sb("rec", [P, 4, 4])
        X1, XN = ROWS[:, 0:2], ROWS[:, 2:4]
        ON = ROWS[:, 4:8].rearrange("p (a b) f -> p a (b f)", a=2).rearrange("p a (h d) -> p a h d", h=H)
        OT_hi = sb("ot_hi", [P, INNER], F32R)
        OT_lo = sb("ot_lo", [P, INNER], F32R)
        stats = sb("stats", [P, 6])
        col = sb("col", [P, 8])
        S3 = sb("s3", [P, B, NS])
        ms = sb("ms", [P, 3, 2 * B])
        NQ = sb("nq", [P, B, QL + KVL])
        KR = sb("kr", [P, 2, B, ROPE])
        gs = sb("gs", [P, 3, B, 3])
        ps = ctx.enter_context(nc.psum_tensor("t_ps", [P, 8 * 512], F32))
        bank = lambda n, w=512, rows=P: ps[0:rows, n * 512:n * 512 + w]
        sems = {}

        def done(n):
            if n not in sems:
                sems[n] = ctx.enter_context(nc.semaphore("t_" + n))
            return sems[n]
        names = """const_in wo_in wo_split_hi wo_split_lo vchain setup summed x_biased o_turned on_done on_turned ot_hi ot_lo
            xo_done x1_done x_normed x_turned xt_hi xt_lo s3_done s3_copied nq_done nq_turned ck_turned nqt_copied
            gate_done gate_shifted gate_expd kr_done""".split()
        (const_in, wo_in, wo_split_hi, wo_split_lo, vchain, setup, summed, x_biased, o_turned, on_done, on_turned, ot_hi, ot_lo,
         xo_done, x1_done, x_normed, x_turned, xt_hi, xt_lo, s3_done, s3_copied, nq_done, nq_turned, ck_turned, nqt_copied,
         gate_done, gate_shifted, gate_expd, kr_done) = (done(n) for n in names)
        loaded, x_in = [done("loaded0"), done("loaded1")], [done("x_in0"), done("x_in1")]
        ident_in, bo_in, prefetched = done("ident_in"), done("bo_in"), done("prefetched")
        x1_out = [done("x1_out0"), done("x1_out1")]
        block = ctx.enter_context(nc.Block())
        rows = lambda w: w.rearrange("(k p) n -> p k n", p=P)
        NC = 7
        STEPS = range(B + 3)

        @block.sync
        def _(sp):
            def load_parts(b):
                for h in range(2):
                    sp.dma_start(OP[:, b % 2, h, :], o_part[2 * b + h].rearrange("p g f -> p (g f)")).then_inc(loaded[b % 2], 16)

            def load_x(b):
                sp.dma_start(X[:, b % 2, :], x[b]).then_inc(x_in[b % 2], 16)
            sp.dma_start(I[:], ident).then_inc(ident_in, 16)
            load_parts(0)
            sp.dma_start(BO[:], bo.partition_broadcast(P)).then_inc(bo_in, 16)
            load_x(0)
            sp.dma_start(WO_raw[:], rows(wo)).then_inc(wo_in, 16)
            load_parts(1)
            load_x(1)
            pieces = ((ROPE_T[:], rope),
                      (GQ[:, 0:QL], g_q.partition_broadcast(P)), (GQ[:, QL:], g_kv.partition_broadcast(P)),
                      (WS[:, :, 0:QL], rows(w_cq)), (WS[:, :, QL:QL + KVL], rows(w_ckv)),
                      (WS[:, :, QL + KVL:NS - 3], rows(w_kr)), (WS[:, :, NS - 3:NS], rows(w_gate)))
            for dst, src in pieces:
                sp.dma_start(dst, src).then_inc(const_in, 16)
            for dst, src in prefetch:
                sp.dma_start(dst, src).then_inc(prefetched, 16)
            for b in range(2, B):
                sp.wait_ge(summed, b - 1)
                load_parts(b)
                sp.wait_ge(x1_done, b - 1)
                load_x(b)
                sp.dma_start(x1_d[b - 2], X1[:, b % 2, :]).then_inc(x1_out[b % 2], 16)
            for b in range(B - 2, B):
                sp.wait_ge(x1_done, b + 1)
                sp.dma_start(x1_d[b], X1[:, b % 2, :]).then_inc(x1_out[b % 2], 16)
            sp.wait_ge(prefetched, 16 * len(prefetch))
            for par in range(2):
                sp.wait_ge(x1_out[par], 16 * B // 2)

        @block.gpsimd
        def _(g):
            g.memset(MEAN[:], 1.0 / P).then_inc(setup, 1)
            for b in range(B):
                par = b % 2
                g.wait_ge(loaded[par], 32 * (b // 2 + 1))
                if b >= 2:
                    g.wait_ge(o_turned, b - 1)
                g.tensor_tensor(OS[:, par, :], OP[:, par, 0, :], OP[:, par, 1, :], ALU.add).then_inc(summed, 1)
                if b == 0:
                    g.wait_ge(bo_in, 16)
                g.wait_ge(x_in[par], 16 * (b // 2 + 1))
                g.tensor_tensor(X[:, par, :], X[:, par, :], BO[:], ALU.add).then_inc(x_biased, 1)

        @block.scalar
        def _(a):
            a.wait_ge(wo_in, 16)
            for j in range(4):
                a.copy(flat(WO_hi[:, 2 * j:2 * j + 2]), flat(WO_raw[:, 2 * j:2 * j + 2])).then_inc(wo_split_hi, 1)
            for k in STEPS:
                if 0 <= k - 2 < B:
                    b = k - 2
                    a.wait_ge(x_turned, b + 1)
                    a.copy(XT_hi[:, :, b * P:(b + 1) * P], bank(7).rearrange("p (k f) -> p k f", k=KC)).then_inc(xt_hi, 1)
                if k < B:
                    a.wait_ge(on_turned, k + 1)
                    a.copy(OT_hi[:], ps[:, 4 * 512:6 * 512]).then_inc(ot_hi, 1)
            a.wait_ge(gate_shifted, 1)
            a.activation(gs[:, 1], gs[:, 0], ACT.Exp).then_inc(gate_expd, 1)

        @block.vector
        def _(v):
            c = Chain(v, vchain, 0, 0)
            link = c.link
            for k in STEPS:
                if k < B:
                    v.wait_ge(o_turned, k + 1)
                    o4 = ps[:, 0:4 * 512].rearrange("p (a f) -> p a f", a=4)[:, :, 0:4 * OV].rearrange("p a (h d) -> p a h d", d=OV)
                    link(v.reciprocal(REC[:], o4[:, :, :, DH]))
                    if k >= 2:
                        v.wait_ge(on_turned, k - 1)
                    v.tensor_tensor(ON[:, k % 2].rearrange("p (a h) d -> p a h d", a=4), o4[:, :, :, 0:DH],
                                    REC[:].unsqueeze(3).broadcast_to([P, 4, 4, DH]), ALU.mult).then_inc(on_done, 1)
                if k == 0:
                    for j in range(4):
                        v.wait_ge(wo_split_hi, j + 1)
                        v.tensor_tensor(flat(WO_lo[:, 2 * j:2 * j + 2]), flat(WO_raw[:, 2 * j:2 * j + 2]),
                                        flat(WO_hi[:, 2 * j:2 * j + 2]).bitcast(F32), ALU.subtract).then_inc(wo_split_lo, 1)
                if 0 <= k - 1 < B:
                    b = k - 1
                    par = b % 2
                    v.wait_ge(xo_done, b + 1)
                    v.wait_ge(x_biased, b + 1)
                    if b >= 2:
                        v.wait_ge(x1_out[par], 16 * (b // 2))
                    v.tensor_tensor(X1[:, par], bank(6), X[:, par], ALU.add).then_inc(x1_done, 1)
                    v.wait_ge(x1_done, b + 1)
                    if b >= 2:
                        v.wait_ge(x_turned, b - 1)
                    layernorm_(v, c, XN[:, par], X1[:, par], stats[:], col[:]).then_inc(x_normed, 1)
                if 0 <= k - 2 < B:
                    b = k - 2
                    v.wait_ge(xt_hi, b + 1)
                    s_ = slice(b * P, (b + 1) * P)
                    v.tensor_tensor(XT_lo[:, :, s_], bank(7).rearrange("p (k f) -> p k f", k=KC), XT_hi[:, :, s_].bitcast(F32),
                                    ALU.subtract).then_inc(xt_lo, 1)
                if k < B:
                    v.wait_ge(ot_hi, k + 1)
                    v.tensor_tensor(OT_lo[:], ps[:, 4 * 512:6 * 512], OT_hi[:].bitcast(F32), ALU.subtract).then_inc(ot_lo, 1)
                if 0 <= k - 3 < B:
                    v.wait_ge(s3_done, k - 2)
                    v.tensor_copy(S3[:, k - 3], bank(0, NS)).then_inc(s3_copied, 1)
            v.wait_ge(const_in, 16 * NC)
            v.wait_ge(s3_copied, B)
            ranks = S3[:, :, 0:QL + KVL]
            link(v.tensor_tensor(NQ[:], ranks, ranks, ALU.mult))
            for r, s_ in enumerate((slice(0, QL), slice(QL, QL + KVL))):
                sums = ms[:, 0, r * B:(r + 1) * B]
                link(v.tensor_reduce(sums, NQ[:, :, s_], AX.X, ALU.add))
                link(v.tensor_scalar(sums, sums, 1.0 / (s_.stop - s_.start), RMS_EPS, ALU.mult, ALU.add))
            rsqrt_cols(v, c, ms[:, 1], ms[:, 0], ms[:, 2])
            for r, s_ in enumerate((slice(0, QL), slice(QL, QL + KVL))):
                w = s_.stop - s_.start
                link(v.tensor_tensor(NQ[:, :, s_], S3[:, :, s_], ms[:, 1, r * B:(r + 1) * B].unsqueeze(2).broadcast_to([P, B, w]), ALU.mult))
                v.tensor_tensor(NQ[:, :, s_], NQ[:, :, s_], GQ[:, s_].unsqueeze(1).broadcast_to([P, B, w]), ALU.mult).then_inc(nq_done, 1)
            v.wait_ge(gate_done, 1)
            link(v.tensor_reduce(ms[:, 0, 0:B], bank(1, 3 * B).rearrange("p (b g) -> p b g", b=B), AX.X, ALU.max))
            v.tensor_tensor(gs[:, 0], bank(1, 3 * B).rearrange("p (b g) -> p b g", b=B), ms[:, 0, 0:B].unsqueeze(2).broadcast_to([P, B, 3]),
                            ALU.subtract).then_inc(gate_shifted, 1)
            kr = S3[:, :, QL + KVL:NS - 3]
            R = ROPE // 2
            link(v.tensor_scalar(kr, kr, 1.0 / H, None, ALU.mult))
            link(v.tensor_tensor(KR[:, 0], kr, ROPE_T[:, 0:1, :].broadcast_to([P, B, ROPE]), ALU.mult))
            link(v.tensor_tensor(KR[:, 1], kr, ROPE_T[:, 1:2, :].broadcast_to([P, B, ROPE]), ALU.mult))
            v.tensor_tensor(KRT[:, :, 0:R], KR[:, 0, :, 0:R], KR[:, 1, :, R:], ALU.add).then_inc(kr_done, 1)
            v.tensor_tensor(KRT[:, :, R:], KR[:, 0, :, R:], KR[:, 1, :, 0:R], ALU.add).then_inc(kr_done, 1)
            v.wait_ge(gate_expd, 1)
            link(v.tensor_reduce(ms[:, 0, B:2 * B], gs[:, 1], AX.X, ALU.add))
            link(v.reciprocal(ms[:, 0, B:2 * B], ms[:, 0, B:2 * B]))
            v.tensor_tensor(GATE[:], gs[:, 1], ms[:, 0, B:2 * B].unsqueeze(2).broadcast_to([P, B, 3]), ALU.mult)
            for n in range(2):
                v.wait_ge((nq_turned, ck_turned)[n], 1)
                dst, w = ((NQT, QL), (CKT, KVL))[n]
                v.tensor_copy(dst[:], ps[0:w, (2 + 2 * n) * 512:(4 + 2 * n) * 512]).then_inc(nqt_copied, 1)
            v.wait_ge(nqt_copied, 2)

        @block.tensor
        def _(t):
            t.wait_ge(ident_in, 16)
            for k in STEPS:
                if k < B:
                    t.wait_ge(summed, k + 1)
                    if k >= 1:
                        t.wait_ge(on_done, k)
                    if k - 4 >= 0:
                        t.wait_ge(s3_copied, k - 3)
                    for h in range(H):
                        o = bank(h // 4)[:, (h % 4) * OV:(h % 4 + 1) * OV]
                        mm = t.transpose(o, OS[:, k % 2, h * P:(h + 1) * P], I[0:OV, 0:OV])
                    mm.then_inc(o_turned, 1)
                if 0 <= k - 1 < B:
                    b = k - 1
                    if b == 0:
                        t.wait_ge(wo_split_lo, 4)
                    t.wait_ge(ot_lo, b + 1)
                    if b:
                        t.wait_ge(x1_done, b)
                    n = 0
                    for kk in range(INNER // P):
                        for o, w in ((OT_lo, WO_hi), (OT_hi, WO_lo), (OT_hi, WO_hi)):
                            mm = t.matmul(bank(6), o[:, kk * P:(kk + 1) * P], w[:, kk, :], start=n == 0, stop=n == 23)
                            n += 1
                    mm.then_inc(xo_done, 1)
                if 0 <= k - 2 < B:
                    b = k - 2
                    t.wait_ge(x_normed, b + 1)
                    if b:
                        t.wait_ge(xt_lo, b)
                    for kk in range(KC):
                        mm = t.transpose(bank(7)[:, kk * P:(kk + 1) * P], XN[:, b % 2, kk * P:(kk + 1) * P], I[:])
                    mm.then_inc(x_turned, 1)
                if k < B:
                    t.wait_ge(on_done, k + 1)
                    if k:
                        t.wait_ge(ot_lo, k)
                    for j in range(8):
                        mm = t.transpose(ps[:, 4 * 512 + j * P:4 * 512 + (j + 1) * P],
                                         ON[:, k % 2].rearrange("p h d -> p (h d)")[:, j * P:(j + 1) * P], I[:])
                    mm.then_inc(on_turned, 1)
                if 0 <= k - 3 < B:
                    b = k - 3
                    if b == 0:
                        t.wait_ge(const_in, 16 * NC)
                        t.wait_ge(setup, 1)
                    t.wait_ge(xt_lo, b + 1)
                    t.wait_ge(on_done, min(k + 1, B))
                    if b:
                        t.wait_ge(s3_copied, b)
                    for kk in range(KC):
                        for n, xt in enumerate((XT_lo, XT_hi)):
                            mm = t.matmul(bank(0, NS), xt[:, kk, b * P:(b + 1) * P].bitcast(F32), WS[:, kk, :],
                                          start=kk == 0 and n == 0, stop=kk == KC - 1 and n == 1)
                    mm.then_inc(s3_done, 1)
            t.wait_ge(s3_copied, B)
            t.matmul(bank(1, 3 * B), MEAN[:], S3[:, :, NS - 3:NS], start=True, stop=True).then_inc(gate_done, 1)
            for n, (o, s_, w) in enumerate(((2, slice(0, QL), QL), (4, slice(QL, QL + KVL), KVL))):
                t.wait_ge(nq_done, n + 1)
                for b in range(B):
                    mm = t.transpose(ps[0:w, o * 512 + b * P:o * 512 + (b + 1) * P], NQ[:, b, s_], I[:])
                mm.then_inc((nq_turned, ck_turned)[n], 1)


def stage_attend(nc, wts, tables, keep, O2, RAW):
    w_dqn, w_dqr, w_dkn, w_dv, w_selk, w_selv, w_wink, w_winv = wts
    ident, rope, causal = tables
    XT_hi, XT_lo, NQT, CKT, KRT, GATE = keep
    with ExitStack() as ctx:
        sb = lambda n, s, d=F32: ctx.enter_context(nc.sbuf_tensor("a_" + n, s, d))
        PARTS = ((0, GK), (GK, 2 * GK), (2 * GK, NW))
        I = sb("ident", [P, P])
        ROPE_T = sb("rope", [P, 2, ROPE])
        CAUSAL = sb("causal", [P, 3, P])
        W_hi = sb("w_hi", [P, KC, NW], F32R)
        W_lo = sb("w_lo", [P, KC, NW], F32R)
        DQK = sb("dqk", [P, GK])
        DQ, DK = DQK[0:QL, :], DQK[QL:QL + KVL, 0:2 * GV]
        K1_, KS_, KW_, Q_ = range(4)
        T4 = sb("t4", [P, B, 4, G4, QK])
        V3 = sb("v3", [P, B, 3, G4, VH])
        QT = sb("qt", [QK, 2, G4, P])
        K3T = sb("k3t", [QK, 2, G4, 3, P])
        S = sb("s", [P, 3, 12, P])
        PT = sb("pt", [P, 12, P])
        R = flat(PT[:]).rearrange("p (a n d) -> p a n d", a=2, n=12)
        mx = sb("mx", [P, 2, 12])
        rec = sb("rec", [P, 2, 12])
        ps = ctx.enter_context(nc.psum_tensor("a_ps", [P, 8 * 512], F32))
        bank = lambda n, w=512, rows=P: ps[0:rows, n * 512:n * 512 + w]
        sem = lambda n: ctx.enter_context(nc.semaphore("a_" + n))
        const_in, w_in, dq_in, w_hi_done, w_lo_done, kr_set = (sem(n) for n in
            ("const_in", "w_in", "dq_in", "w_hi_done", "w_lo_done", "kr_set"))
        vchain = sem("vchain")
        ks_done, kw_done, vv_done, q_done = sem("ks_done"), sem("kw_done"), sem("vv_done"), sem("q_done")
        ks_copied, kw_copied, vv_copied, q_copied, roped = sem("ks_copied"), sem("kw_copied"), sem("vv_copied"), sem("q_copied"), sem("roped")
        ring_done, ring_copied = sem("ring_done"), sem("ring_copied")
        s_done, s_read, s_maxed, s_shifted, s_expd, rec_done, s_scaled, pv_done, o_read = (sem(n) for n in
            ("s_done", "s_read", "s_maxed", "s_shifted", "s_expd", "rec_done", "s_scaled", "pv_done", "o_read"))
        block = ctx.enter_context(nc.Block())
        LAGB = 3
        STEPS = range(B + LAGB)
        RING = [u for k in STEPS for u in ([("turn", k, T) for T in range(4)] if k < B else []) +
                ([("p", k - LAGB, n) for n in range(3)] if k >= LAGB else [])]
        index = {u: n for n, u in enumerate(RING)}

        def copied(eng, g, u):
            eng.wait_ge(ring_copied, len(RING) * g + index[u] + 1)

        def ring_copy(a, g, u):
            kind, b, n = u
            src = bank(4 + index[u] % 3)
            a.wait_ge(ring_done, len(RING) * g + index[u] + 1)
            if kind == "p":
                if b > 0:
                    a.wait_ge(pv_done, B * g + b)
                a.copy(flat(PT[:, 4 * n:4 * n + 4]), src).then_inc(ring_copied, 1)
            else:
                dst = QT[:, b % 2] if n == Q_ else K3T[:, b % 2, :, n, :]
                a.copy(dst, src[0:QK].rearrange("p (h f) -> p h f", h=G4)).then_inc(ring_copied, 1)

        def rounds(eng, body):
            body(0, True, False)
            with eng.Fori(1, NR - 1) as g:
                body(g, False, False)
            body(NR - 1, False, True)

        @block.sync
        def _(sp):
            def load_w(g):
                for dst, src in round_weights((w_selk, w_wink, w_selv, w_winv), RAW, g):
                    sp.dma_start(dst, src).then_inc(w_in, 16)

            def load_dq(g):
                sp.dma_start(DQ[:, 0:GV], w_dqn[:, bass.ds(g * GV, GV)]).then_inc(dq_in, 16)
                sp.dma_start(DQ[:, GV:GK], w_dqr[:, bass.ds(g * 2 * GV, 2 * GV)]).then_inc(dq_in, 16)
                sp.dma_start(DK[:, 0:GV], w_dkn[:, bass.ds(g * GV, GV)]).then_inc(dq_in, 16)
                sp.dma_start(DK[:, GV:], w_dv[:, bass.ds(g * GV, GV)]).then_inc(dq_in, 16)
            load_dq(0)
            for dst, src in ((I[:], ident), (ROPE_T[:], rope), (CAUSAL[:], causal)):
                sp.dma_start(dst, src).then_inc(const_in, 16)

            def body(g, first, last):
                if not last:
                    sp.wait_ge(w_lo_done, 3 * (g + 1))
                    load_w(g + 1)
                    sp.wait_ge(vv_done, B * (g + 1))
                    load_dq(g + 1)
            rounds(sp, body)

        @block.gpsimd
        def _(g_):
            for b in range(B):
                g_.tensor_copy(T4[:, b, K1_, :, NOPE:], KRT[:, b:b + 1, :].broadcast_to([P, G4, ROPE])).then_inc(kr_set, 1)

            def body(g, first, last):
                each = lambda t: t.unsqueeze(2).broadcast_to([P, 12, P])
                for k in range(B + 2):
                    if k >= 2:
                        b = k - 2
                        g_.wait_ge(rec_done, B * g + b + 1)
                        g_.tensor_tensor(S[:, b % 3], S[:, b % 3], each(rec[:, b % 2]), ALU.mult).then_inc(s_scaled, 1)
                    if k < B:
                        g_.wait_ge(s_maxed, B * g + k + 1)
                        g_.tensor_tensor(S[:, k % 3], S[:, k % 3], each(mx[:, k % 2]), ALU.subtract).then_inc(s_shifted, 1)
            rounds(g_, body)

        @block.scalar
        def _(a):
            def split(n):
                if not isinstance(n, int) or n > 1:
                    a.wait_ge(w_in, 64 * (n - 1))
                for c0, c1 in PARTS:
                    a.copy(W_hi[:, :, c0:c1], RAW[:, :, c0:c1]).then_inc(w_hi_done, 1)
            split(1)

            def copy_keys(g, b):
                a.wait_ge(ks_done, B * g + b + 1)
                a.copy(T4[:, b, KS_].rearrange("p h d -> p (h d)"), bank(b % 2, GK)).then_inc(ks_copied, 1)
                a.wait_ge(kw_done, B * g + b + 1)
                a.copy(T4[:, b, KW_].rearrange("p h d -> p (h d)"), bank(2 + b % 2, GK)).then_inc(kw_copied, 1)

            def body(g, first, last):
                for b in range(B):
                    if first or b >= LAGB:
                        copy_keys(g, b)
                    a.wait_ge(vv_done, B * g + b + 1)
                    vb = bank(4 + b % 2)
                    for n, at in ((1, 0), (2, GV), (0, 3 * GV)):
                        a.copy(V3[:, b, n], heads(vb[:, at:at + GV], G4)).then_inc(vv_copied, 1)
                    a.copy(T4[:, b, K1_, :, 0:NOPE], heads(vb[:, 2 * GV:3 * GV], G4)).then_inc(vv_copied, 1)
                if not last:
                    split(g + 2)
                for k in STEPS:
                    for u in RING:
                        if u[1] == (k if u[0] == "turn" else k - LAGB):
                            ring_copy(a, g, u)
                    if 1 <= k <= B:
                        b = k - 1
                        a.wait_ge(s_shifted, B * g + b + 1)
                        a.activation(flat(S[:, b % 3]), flat(S[:, b % 3]), ACT.Exp, scale=QK ** -0.5).then_inc(s_expd, 1)
                    if k >= B and not last:
                        copy_keys(g + 1, k - B)
            rounds(a, body)

        @block.vector
        def _(v):
            def split(n):
                for m, (c0, c1) in enumerate(PARTS):
                    v.wait_ge(w_hi_done, 3 * (n - 1) + m + 1)
                    v.tensor_tensor(W_lo[:, :, c0:c1], RAW[:, :, c0:c1], W_hi[:, :, c0:c1].bitcast(F32), ALU.subtract
                                    ).then_inc(w_lo_done, 1)
            split(1)
            v.wait_ge(const_in, 48)

            def body(g, first, last):
                c = Chain(v, vchain, g, 3 * B)
                link = c.link
                for b in range(B):
                    v.wait_ge(q_done, B * g + b + 1)
                    v.tensor_copy(T4[:, b, Q_, :, 0:NOPE], heads(bank(6 + b % 2, GV), G4)).then_inc(q_copied, 1)
                    v.tensor_copy(T4[:, b, Q_, :, NOPE:], heads(bank(6 + b % 2, GK)[:, GV:], G4)).then_inc(q_copied, 1)
                    v.wait_ge(q_copied, 2 * (B * g + b + 1))
                    v.wait_ge(kw_copied, B * g + b + 1)
                    x_ = T4[:, b, KS_:Q_ + 1].rearrange("p t h d -> p (t h) d")[:, :, NOPE:]
                    H_ = ROPE // 2
                    v.tensor_tensor(R[:, 0], x_, ROPE_T[:, 0:1, :].broadcast_to([P, 12, ROPE]), ALU.mult)
                    link(v.tensor_tensor(R[:, 1], x_, ROPE_T[:, 1:2, :].broadcast_to([P, 12, ROPE]), ALU.mult))
                    v.tensor_tensor(x_[:, :, 0:H_], R[:, 0, :, 0:H_], R[:, 1, :, H_:], ALU.add)
                    v.tensor_tensor(x_[:, :, H_:], R[:, 0, :, H_:], R[:, 1, :, 0:H_], ALU.add).then_inc(roped, 1)
                if not last:
                    split(g + 2)
                for k in STEPS:
                    if 0 <= k - 2 < B:
                        b = k - 2
                        v.wait_ge(s_expd, B * g + b + 1)
                        link(v.tensor_reduce(rec[:, b % 2], S[:, b % 3], AX.X, ALU.add))
                        link(v.reciprocal(rec[:, b % 2], rec[:, b % 2]))
                        r4 = rec[:, b % 2].rearrange("p (h i) -> p h i", i=3)
                        v.tensor_tensor(r4, r4, GATE[:, b:b + 1, :].broadcast_to([P, 4, 3]), ALU.mult).then_inc(rec_done, 1)
                    if k < B:
                        b = k
                        v.wait_ge(s_done, B * g + b + 1)
                        v.tensor_tensor(S[:, b % 3].rearrange("p (a i) f -> p a (i f)", a=4),
                                        ps[:, 0:4 * 512].rearrange("p (a f) -> p a f", a=4)[:, :, 0:3 * P],
                                        flat(CAUSAL[:]).unsqueeze(1).broadcast_to([P, 4, 3 * P]), ALU.add).then_inc(s_read, 1)
                        v.wait_ge(s_read, B * g + b + 1)
                        v.tensor_reduce(mx[:, b % 2], S[:, b % 3], AX.X, ALU.max).then_inc(s_maxed, 1)
                    if k >= LAGB:
                        b = k - LAGB
                        v.wait_ge(pv_done, B * g + b + 1)
                        v.tensor_copy(O2[:, b, bass.ds(g * P, P)], bank(7, P)).then_inc(o_read, 1)
                c.end()
            rounds(v, body)

        @block.tensor
        def _(t):

            def dense(out, b, w0, w1):
                n = 0
                for k in range(KC):
                    for x_, w in ((XT_lo, W_hi), (XT_hi, W_lo), (XT_hi, W_hi)):
                        mm = t.matmul(out, x_[:, k, b * P:(b + 1) * P], w[:, k, w0:w1], start=n == 0, stop=n == 3 * KC - 1)
                        n += 1
                return mm

            def keys(g, b):
                if b >= 2:
                    t.wait_ge(ks_copied, B * g + b - 1)
                if isinstance(g, int) and g == 0 and b == 0:
                    t.wait_ge(w_lo_done, 1)
                dense(bank(b % 2, GK), b, 0, GK).then_inc(ks_done, 1)
                if isinstance(g, int) and g == 0 and b == 0:
                    t.wait_ge(w_lo_done, 2)
                if b >= 2:
                    t.wait_ge(kw_copied, B * g + b - 1)
                dense(bank(2 + b % 2, GK), b, GK, 2 * GK).then_inc(kw_done, 1)

            def body(g, first, last):
                for b in range(B):
                    tok = slice(b * P, (b + 1) * P)
                    if first or b >= LAGB:
                        keys(g, b)
                    if b == 0:
                        t.wait_ge(dq_in, 64 * (g + 1))
                    if b >= 2:
                        t.wait_ge(q_copied, 2 * (B * g + b - 1))
                    t.matmul(bank(6 + b % 2, GK), NQT[:, tok], DQ[:], start=True, stop=True).then_inc(q_done, 1)
                    if b >= 2:
                        t.wait_ge(vv_copied, 4 * (B * g + b - 1))
                    if b == 0:
                        t.wait_ge(w_lo_done, 3 * (g + 1))
                    dense(bank(4 + b % 2, 2 * GV), b, 2 * GK, NW)
                    t.matmul(bank(4 + b % 2)[:, 2 * GV:], CKT[:, tok], DK[:], start=True, stop=True).then_inc(vv_done, 1)
                t.wait_ge(vv_copied, 4 * B * (g + 1))
                t.wait_ge(roped, B * (g + 1))
                if first:
                    t.wait_ge(const_in, 48)
                    t.wait_ge(kr_set, B)
                for k in STEPS:
                    if k < B:
                        for T in range(4):
                            u = ("turn", k, T)
                            ring_free(g, u)
                            for j in range(G4):
                                mm = t.transpose(bank(4 + index[u] % 3, 512, QK)[:, j * P:(j + 1) * P], T4[:, k, T, j, :], I[:])
                            mm.then_inc(ring_done, 1)
                    if k >= LAGB:
                        b = k - LAGB
                        t.wait_ge(s_scaled, B * g + b + 1)
                        for n in range(3):
                            u = ("p", b, n)
                            ring_free(g, u)
                            for j in range(4):
                                mm = t.transpose(bank(4 + index[u] % 3)[:, j * P:(j + 1) * P], S[:, b % 3, 4 * n + j, :], I[:])
                            mm.then_inc(ring_done, 1)
                    if k < B:
                        copied(t, g, ("turn", k, Q_))
                        if k:
                            t.wait_ge(s_read, B * g + k)
                        for j in range(G4):
                            mm = t.matmul(bank(j, 3 * P), QT[:, k % 2, j, :], K3T[:, k % 2, j].rearrange("p a f -> p (a f)"),
                                          start=True, stop=True)
                        mm.then_inc(s_done, 1)
                    if k >= LAGB:
                        b = k - LAGB
                        copied(t, g, ("p", b, 2))
                        if b:
                            t.wait_ge(o_read, B * g + b)
                        for n in range(12):
                            j, i = divmod(n, 3)
                            mm = t.matmul(bank(7, P)[j * VH:(j + 1) * VH], V3[:, b, i, j, :], PT[:, n, :],
                                          start=i == 0, stop=i == 2, skip_group_check=True)
                        mm.then_inc(pv_done, 1)
                    if k >= B and not last:
                        if k == B:
                            t.wait_ge(w_lo_done, 3 * (g + 2))
                            t.wait_ge(s_read, B * (g + 1))
                        keys(g + 1, k - B)
                t.wait_ge(s_read, B * (g + 1))
                t.wait_ge(o_read, B * (g + 1))

            def ring_free(g, u):
                n = index[u]
                if n >= 3:
                    copied(t, g, RING[n - 3])
            rounds(t, body)


def stage_project(nc, x1_d, x2_d, w_proj, ident, ROWS, XT_hi, XT_lo):
    with ExitStack() as ctx:
        sb = lambda n, s, d=F32: ctx.enter_context(nc.sbuf_tensor("p_" + n, s, d))
        I = sb("ident", [P, P])
        W_raw = sb("w_raw", [P, KC, D])
        W_hi = sb("w_hi", [P, KC, D], F32R)
        W_lo = sb("w_lo", [P, KC, D], F32R)
        OT_hi = sb("ot_hi", [P, 4, D], F32R)
        OT_lo = sb("ot_lo", [P, 4, D], F32R)
        X1 = sb("x1", [P, B, D])
        X2 = sb("x2", [P, 4, D])
        stats = sb("stats", [P, 6])
        mom = sb("mom", [P, B, 2])
        rs = sb("rs", [P, 3, 2])
        ps = ctx.enter_context(nc.psum_tensor("p_ps", [P, 8 * 512], F32))
        bank = lambda n: ps[:, n * 512:(n + 1) * 512]
        sem = lambda n: ctx.enter_context(nc.semaphore("p_" + n))
        ident_in, w_in, w_hi_done, w_lo_done, vchain = (sem(n) for n in ("ident_in", "w_in", "w_hi_done", "w_lo_done", "vchain"))
        x1_in = [sem(f"x1_in{b}") for b in range(B)]
        x2_out = [sem(f"x2_out{n}") for n in range(4)]
        ot_hi, ot_lo, y_done, x2_done, normed, x_turned, xt_hi, xt_lo = (sem(n) for n in
            ("ot_hi_done", "ot_lo_done", "y_done", "x2_done", "normed", "x_turned", "xt_hi", "xt_lo"))
        block = ctx.enter_context(nc.Block())
        HB = B // 2
        STEPS = range(HB + 2)
        pair = lambda k: range(2 * k, 2 * k + 2) if 0 <= k < HB else ()

        @block.sync
        def _(sp):
            sp.dma_start(I[:], ident).then_inc(ident_in, 16)
            sp.dma_start(W_raw[:], w_proj.rearrange("(k p) n -> p k n", p=P)).then_inc(w_in, 16)
            for b in range(B):
                sp.dma_start(X1[:, b], x1_d[b]).then_inc(x1_in[b], 16)
            for b in range(B):
                sp.wait_ge(x2_done, b + 1)
                sp.dma_start(x2_d[b], X2[:, b % 4]).then_inc(x2_out[b % 4], 16)
            for n in range(4):
                sp.wait_ge(x2_out[n], 16 * B // 4)

        @block.scalar
        def _(a):
            a.wait_ge(w_in, 16)
            a.copy(flat(W_hi[:]), flat(W_raw[:])).then_inc(w_hi_done, 1)
            for k in STEPS:
                for b in pair(k):
                    if b >= 4:
                        a.wait_ge(y_done, b - 3)
                    a.copy(OT_hi[:, b % 4], ROWS[:, b]).then_inc(ot_hi, 1)
                for b in pair(k - 2):
                    a.wait_ge(x_turned, b + 1)
                    a.copy(XT_hi[:, :, b * P:(b + 1) * P], bank(6 + b % 2).rearrange("p (k f) -> p k f", k=KC)).then_inc(xt_hi, 1)

        @block.vector
        def _(v):
            c = Chain(v, vchain, 0, 0)
            v.wait_ge(w_hi_done, 1)
            v.tensor_tensor(flat(W_lo[:]), flat(W_raw[:]), flat(W_hi[:]).bitcast(F32), ALU.subtract).then_inc(w_lo_done, 1)
            for k in STEPS:
                for b in pair(k):
                    v.wait_ge(ot_hi, b + 1)
                    v.tensor_tensor(OT_lo[:, b % 4], ROWS[:, b], OT_hi[:, b % 4].bitcast(F32), ALU.subtract).then_inc(ot_lo, 1)
                for b in pair(k - 1):
                    v.wait_ge(y_done, b + 1)
                    v.wait_ge(x1_in[b], 16)
                    if b >= 4:
                        v.wait_ge(x2_out[b % 4], 16 * (b // 4))
                    v.tensor_tensor(X2[:, b % 4], bank(2 + b % 4), X1[:, b], ALU.add).then_inc(x2_done, 1)
                    v.wait_ge(x2_done, b + 1)
                    moments(v, c, mom[:, b], X2[:, b % 4], stats[:], rs[:, 2, 0:1])
                if pair(k - 1):
                    s_ = slice(2 * (k - 1), 2 * k)
                    c.link(v.tensor_scalar(rs[:, 0], mom[:, s_, 1], LN_EPS, None, ALU.add))
                    rsqrt_cols(v, c, rs[:, 1], rs[:, 0], rs[:, 2])
                for b in pair(k - 1):
                    v.tensor_scalar(ROWS[:, b], X2[:, b % 4], mom[:, b, 0:1], rs[:, 1, b % 2:b % 2 + 1], ALU.subtract, ALU.mult
                                    ).then_inc(normed, 1)
                for b in pair(k - 2):
                    v.wait_ge(xt_hi, b + 1)
                    s_ = slice(b * P, (b + 1) * P)
                    v.tensor_tensor(XT_lo[:, :, s_], bank(6 + b % 2).rearrange("p (k f) -> p k f", k=KC), XT_hi[:, :, s_].bitcast(F32),
                                    ALU.subtract).then_inc(xt_lo, 1)
            v.wait_ge(xt_lo, B)

        @block.tensor
        def _(t):
            t.wait_ge(ident_in, 16)

            def turn(n, b):
                for j in range(KC):
                    mm = t.transpose(bank(n)[:, j * P:(j + 1) * P], ROWS[:, b, j * P:(j + 1) * P], I[:])
                return mm
            for k in STEPS:
                for b in pair(k - 1):
                    if b == 0:
                        t.wait_ge(w_lo_done, 1)
                    if b >= 4:
                        t.wait_ge(x2_done, b - 3)
                    t.wait_ge(ot_lo, b + 1)
                    n = 0
                    for j in range(KC):
                        for o, w in ((OT_lo, W_hi), (OT_hi, W_lo), (OT_hi, W_hi)):
                            mm = t.matmul(bank(2 + b % 4), o[:, b % 4, j * P:(j + 1) * P], w[:, j, :], start=n == 0, stop=n == 11)
                            n += 1
                    mm.then_inc(y_done, 1)
                for b in pair(k - 2):
                    if b >= 2:
                        t.wait_ge(xt_lo, b - 1)
                    t.wait_ge(normed, b + 1)
                    turn(6 + b % 2, b).then_inc(x_turned, 1)


HF = D // H
DC = D // 4
HID = 1024
GROUPS_E, EPG = 2, 4
E_ALL = GROUPS_E * EPG


def rms_scale(v, c, y, out, weight, stats, col):
    moments(v, c, col[:, 0:2], y, stats, col[:, 5:6])
    c.link(v.scalar_tensor_tensor(out=col[:, 2:3], in0=col[:, 0:1], scalar=col[:, 0:1], in1=col[:, 1:2], op0=ALU.mult, op1=ALU.add))
    c.link(v.tensor_scalar(col[:, 2:3], col[:, 2:3], RMS_EPS, None, ALU.add))
    rsqrt_cols(v, c, col[:, 3:4], col[:, 2:3], col[:, 4:5])
    return v.scalar_tensor_tensor(out=out, in0=y, scalar=col[:, 3:4], in1=weight, op0=ALU.mult, op1=ALU.mult)


def stage_ffn_attend(nc, wts, tables, ROWS, XT_hi, XT_lo, W8, prefetch):
    wq, wk_c, wv_c, wk, wv, wo, wg, we, g_bias, e_bias, norm1 = wts
    ident, rope_t, earlier = tables
    with ExitStack() as ctx:
        sb = lambda n, s, d=F32: ctx.enter_context(nc.sbuf_tensor("g_" + n, s, d))
        HALF = 512
        NL = GROUPS_E + E_ALL
        I = sb("ident", [P, P])
        ROPE_T = sb("rope", [P, 2, P])
        EARLIER = sb("earlier", [P, EPG, EPG])
        BIAS = sb("bias", [P, NL])
        N1 = sb("n1", [P, D])
        WG = sb("wg", [P, KC, NL])
        WG_hi = sb("wg_hi", [P, KC, NL], F32R)
        WG_lo = sb("wg_lo", [P, KC, NL], F32R)
        RAW = sb("raw", [P, KC, D])
        WQ_hi = sb("wq_hi", [P, KC, D], F32R)
        WQ_lo = sb("wq_lo", [P, KC, D], F32R)
        WS_hi = sb("ws_hi", [P, KC, D], F32R)
        WS_lo = sb("ws_lo", [P, KC, D], F32R)
        WC_raw = sb("wc_raw", [P, KC, 2 * DC])
        WC_hi = sb("wc_hi", [P, KC, 2 * DC], F32R)
        WC_lo = sb("wc_lo", [P, KC, 2 * DC], F32R)
        WK = sb("wk", [P, 2, D])
        WV = sb("wv", [P, D])
        CT = sb("ct", [P, 2, TOK])
        QT = sb("qt", [P, KC, TOK])
        KT_ = sb("kt", [P, KC, TOK])
        V = sb("v", [P, B, D])
        PT = sb("pt", [P, H, P])
        R = flat(PT[:]).rearrange("p (r s f) -> p r s f", r=2, s=2)
        S = (sb("s", [P, H, P])[:], RAW[:].rearrange("p k (h f) -> p (k h) f", f=P), CT[:].rearrange("p a (h f) -> p (a h) f", f=P))
        mx = sb("mx", [P, 2, H])
        sm = sb("sm", [P, 2, H])
        OT_hi = sb("ot_hi", [P, D], F32R)
        OT_lo = sb("ot_lo", [P, D], F32R)
        stats = sb("stats", [P, 6])
        col = sb("col", [P, 8])
        LT = sb("lt", [NL, TOK])
        LG = sb("lg", [P, NL, B])
        RK = flat(PT[:])[:, 0:2 * EPG * EPG * B].rearrange("p (a i j b) -> p a i j b", a=2, i=EPG, j=EPG)
        G = flat(PT[:])[:, 2 * EPG * EPG * B:][:, 0:30 * B].rearrange("p (n b) -> p n b", b=B)
        SS = flat(WC_raw[:]).rearrange("p (h f) -> p h f", h=H)
        ps = ctx.enter_context(nc.psum_tensor("g_ps", [P, 8 * 512], F32))
        bank = lambda n, w=512: ps[:, n * 512:n * 512 + w]
        names = """const_in wc_in wq_in wkv_in wo_in wc_hi_done wc_lo_done wq_hi_done wq_lo_done swapped k_swapped vchain
            c_done ct_copied two_done multiplied roped v_done v_copied
            s_done maxed s_expd p_turned pt_copied pv_done scaled ot_hi ot_lo y_done y_read xf_done f_turned xt_hi xt_lo
            logits_done lt_copied logits_turned logits_read wg_hi_done wg_lo_done halved summed rec_done prefetched g_shifted g_expd""".split()
        sems = {n: ctx.enter_context(nc.semaphore("g_" + n)) for n in names}
        (const_in, wc_in, wq_in, wkv_in, wo_in, wc_hi_done, wc_lo_done, wq_hi_done, wq_lo_done, swapped, k_swapped, vchain,
         c_done, ct_copied, two_done, multiplied, roped, v_done, v_copied,
         s_done, maxed, s_expd, p_turned, pt_copied, pv_done, scaled, ot_hi, ot_lo, y_done, y_read, xf_done, f_turned, xt_hi,
         xt_lo, logits_done, lt_copied, logits_turned, logits_read, wg_hi_done, wg_lo_done, halved, summed, rec_done, prefetched, g_shifted, g_expd) = (sems[n] for n in names)
        block = ctx.enter_context(nc.Block())
        UNITS = [(w, c, t) for w in ("q", "k") for c in range(KC) for t in range(2)]
        NU = len(UNITS)
        STEPS = range(B + 5)
        at = lambda k: 0 <= k < B
        VALUES = {0: range(0, 4), 1: range(4, 8)}
        NC = 8

        @block.sync
        def _(sp):
            rows = lambda w: w.rearrange("(k p) n -> p k n", p=P)
            sp.dma_start(WC_raw[:, :, 0:DC], rows(wk_c)).then_inc(wc_in, 16)
            sp.dma_start(WC_raw[:, :, DC:], rows(wv_c)).then_inc(wc_in, 16)
            sp.dma_start(RAW[:], rows(wq)).then_inc(wq_in, 16)
            sp.dma_start(WK[:, 0], wk).then_inc(wkv_in, 16)
            sp.dma_start(WV[:], wv).then_inc(wkv_in, 16)
            pieces = ((I[:], ident), (ROPE_T[:], rope_t), (EARLIER[:], earlier.partition_broadcast(P)),
                      (BIAS[:, 0:GROUPS_E], g_bias.partition_broadcast(P)), (BIAS[:, GROUPS_E:], e_bias.partition_broadcast(P)),
                      (N1[:], norm1.partition_broadcast(P)), (WG[:, :, 0:GROUPS_E], rows(wg)), (WG[:, :, GROUPS_E:], rows(we)))
            assert len(pieces) == NC
            for dst, src in pieces:
                sp.dma_start(dst, src).then_inc(const_in, 16)
            for dst, src in prefetch:
                sp.dma_start(dst, src).then_inc(prefetched, 16)
            sp.wait_ge(wq_lo_done, 1)
            sp.dma_start(RAW[:], rows(wo)).then_inc(wo_in, 16)
            if prefetch:
                sp.wait_ge(prefetched, 16 * len(prefetch))

        @block.gpsimd
        def _(g):
            g.wait_ge(wkv_in, 32)
            for n in range(2):
                g.tensor_copy(WK[:, 1, n::2], WK[:, 0, 1 - n::2]).then_inc(k_swapped, 1)
            for u, (w, c, t) in enumerate(UNITS):
                g.wait_ge(multiplied, 2 * (u + 1))
                dst = (QT if w == "q" else KT_)[:, c, t * HALF:(t + 1) * HALF]
                g.tensor_tensor(dst, R[:, u % 2, 0], R[:, u % 2, 1], ALU.add).then_inc(roped, 1)
            g.wait_ge(wq_hi_done, 2)
            g.tensor_tensor(flat(WQ_lo[:]), flat(RAW[:]), flat(WQ_hi[:]).bitcast(F32), ALU.subtract).then_inc(wq_lo_done, 1)
            for b in range(B):
                w_ = S[b % 3]
                g.wait_ge(s_expd, H * (b + 1))
                if b:
                    g.wait_ge(summed, b)
                g.tensor_tensor(SS[:], w_[:, :, 0:P // 2], w_[:, :, P // 2:], ALU.add).then_inc(halved, 1)
                g.wait_ge(halved, 2 * b + 1)
                g.tensor_tensor(SS[:, :, 0:P // 4], SS[:, :, 0:P // 4], SS[:, :, P // 4:], ALU.add).then_inc(halved, 1)
                g.wait_ge(rec_done, b + 1)
                g.tensor_tensor(w_, w_, sm[:, b % 2].unsqueeze(2).broadcast_to([P, H, P]), ALU.mult).then_inc(scaled, 1)

        @block.scalar
        def _(a):
            a.wait_ge(wc_in, 32)
            a.copy(flat(WC_hi[:]), flat(WC_raw[:])).then_inc(wc_hi_done, 1)
            a.wait_ge(wq_in, 16)
            a.copy(flat(WQ_hi[:]), flat(RAW[:])).then_inc(wq_hi_done, 1)
            for n in range(4):
                a.wait_ge(c_done, n + 1)
                a.copy(CT[:, n // 2, n % 2 * HALF:(n % 2 + 1) * HALF], bank(n)).then_inc(ct_copied, 1)
            a.wait_ge(const_in, 16 * NC)
            a.copy(flat(WG_hi[:]), flat(WG[:])).then_inc(wg_hi_done, 1)
            a.wait_ge(wo_in, 16)
            a.wait_ge(two_done, NU)
            a.copy(flat(WQ_hi[:]), flat(RAW[:])).then_inc(wq_hi_done, 1)
            for k in STEPS:
                if at(k - 2):
                    b = k - 2
                    for n in range(4):
                        a.wait_ge(p_turned, 4 * b + n + 1)
                        if b:
                            a.wait_ge(pv_done, b)
                        a.copy(flat(PT[:, 4 * n:4 * n + 4]), bank(5 - n % 2)).then_inc(pt_copied, 1)
                if at(k):
                    a.wait_ge(maxed, 2 * k + 2)
                    if k == 1:
                        a.wait_ge(wq_lo_done, 2)
                    if k >= 3:
                        a.wait_ge(p_turned, 4 * (k - 2))
                    for h in range(H):
                        a.activation(S[k % 3][:, h], ps[:, h * P:(h + 1) * P], ACT.Exp, scale=HF ** -0.5,
                                     bias=mx[:, k % 2, h:h + 1]).then_inc(s_expd, 1)
                for b in VALUES.get(k, ()):
                    a.wait_ge(v_done, b + 1)
                    a.copy(V[:, b], bank(4 + b % 4)).then_inc(v_copied, 1)
                if at(k - 2):
                    b = k - 2
                    a.wait_ge(pv_done, b + 1)
                    if b:
                        a.wait_ge(y_done, b)
                    a.copy(OT_hi[:], bank(6)).then_inc(ot_hi, 1)
                if at(k - 5):
                    b = k - 5
                    a.wait_ge(f_turned, b + 1)
                    a.copy(XT_hi[:, :, b * P:(b + 1) * P], bank(5).rearrange("p (k f) -> p k f", k=KC)).then_inc(xt_hi, 1)
            for t in range(2):
                a.wait_ge(logits_done, t + 1)
                a.copy(LT[:, t * HALF:(t + 1) * HALF], bank(t)[0:NL]).then_inc(lt_copied, 1)
            a.wait_ge(g_shifted, 1)
            a.activation(G[:, 14:20, :], G[:, 4:10, :], ACT.Exp).then_inc(g_expd, 1)

        def route(v, link):
            L = lambda a, n=1: LG[:, a:a + n, :]
            each = lambda ap, n: ap.broadcast_to([P, n, B])
            T = lambda a, n=1: G[:, a:a + n, :]
            gmax, sel0, sel1, emax = T(0), T(1), T(2), T(3)
            d, e, ex, rs, p_, cnt = T(4, 6), T(10, EPG), T(14, 6), T(20, 2), T(22, EPG), T(26, EPG)
            over = lambda ap: ap.rearrange("p n b -> p b n")
            link(v.tensor_tensor(gmax, L(0), L(1), ALU.max))
            link(v.tensor_tensor(d[:, 0:2], L(0, 2), each(gmax, 2), ALU.subtract))
            link(v.tensor_tensor(sel1, L(1), L(0), ALU.is_gt))
            link(v.tensor_scalar(sel0, sel1, -1.0, 1.0, ALU.mult, ALU.add))
            link(v.tensor_tensor(e, L(GROUPS_E, EPG), each(sel0, EPG), ALU.mult))
            link(v.tensor_tensor(p_, L(GROUPS_E + EPG, EPG), each(sel1, EPG), ALU.mult))
            link(v.tensor_tensor(e, e, p_, ALU.add))
            link(v.tensor_reduce(emax[:, 0], over(e), AX.X, ALU.max))
            v.tensor_tensor(d[:, 2:6], e, each(emax, EPG), ALU.subtract).then_inc(g_shifted, 1)
            v.wait_ge(g_expd, 1)
            link(v.tensor_reduce(rs[:, 0], over(ex[:, 0:2]), AX.X, ALU.add))
            link(v.tensor_reduce(rs[:, 1], over(ex[:, 2:6]), AX.X, ALU.add))
            link(v.reciprocal(rs, rs))
            link(v.tensor_tensor(p_, ex[:, 2:6], each(rs[:, 1:2], EPG), ALU.mult))
            link(v.tensor_tensor(p_, p_, each(rs[:, 0:1], EPG), ALU.mult))
            pj, pi = (p_.unsqueeze(n).broadcast_to([P, EPG, EPG, B]) for n in (1, 2))
            link(v.tensor_tensor(RK[:, 0], pj, pi, ALU.is_gt))
            link(v.tensor_tensor(RK[:, 1], pj, pi, ALU.is_equal))
            link(v.tensor_tensor(RK[:, 1], RK[:, 1], EARLIER[:].unsqueeze(3).broadcast_to([P, EPG, EPG, B]), ALU.mult))
            link(v.tensor_tensor(RK[:, 0], RK[:, 0], RK[:, 1], ALU.add))
            link(v.tensor_reduce(cnt, RK[:, 0].rearrange("p i j b -> p i b j"), AX.X, ALU.add))
            link(v.tensor_scalar(cnt, cnt, 1.5, None, ALU.is_lt))
            link(v.tensor_tensor(cnt, cnt, p_, ALU.mult))
            for n, sel in enumerate((sel0, sel1)):
                link(v.tensor_tensor(W8[:, :, EPG * n:EPG * (n + 1)].rearrange("p b e -> p e b"), cnt, each(sel, EPG), ALU.mult))

        @block.vector
        def _(v):
            c = Chain(v, vchain, 0, 0)
            link = c.link
            v.wait_ge(wc_hi_done, 1)
            v.tensor_tensor(flat(WC_lo[:]), flat(WC_raw[:]), flat(WC_hi[:]).bitcast(F32), ALU.subtract).then_inc(wc_lo_done, 1)
            v.wait_ge(wq_hi_done, 1)
            v.tensor_tensor(flat(WQ_lo[:]), flat(RAW[:]), flat(WQ_hi[:]).bitcast(F32), ALU.subtract).then_inc(wq_lo_done, 1)
            v.wait_ge(wq_lo_done, 1)
            for dst, src in ((WS_hi, WQ_hi), (WS_lo, WQ_lo)):
                for n in range(2):
                    v.tensor_copy(dst[:, :, n::2], src[:, :, 1 - n::2]).then_inc(swapped, 1)
            v.wait_ge(const_in, 16 * NC)
            v.wait_ge(wg_hi_done, 1)
            v.tensor_tensor(flat(WG_lo[:]), flat(WG[:]), flat(WG_hi[:]).bitcast(F32), ALU.subtract).then_inc(wg_lo_done, 1)
            for u in range(NU):
                v.wait_ge(two_done, u + 1)
                if u >= 2:
                    v.wait_ge(roped, u - 1)
                for s in range(2):
                    v.tensor_tensor(R[:, u % 2, s].rearrange("p (b f) -> p b f", f=P),
                                    bank(4 + 2 * (u % 2) + s).rearrange("p (b f) -> p b f", f=P),
                                    ROPE_T[:, s:s + 1].broadcast_to([P, HALF // P, P]), ALU.mult).then_inc(multiplied, 1)
            for k in STEPS:
                if at(k):
                    v.wait_ge(s_done, k + 1)
                    v.tensor_reduce(mx[:, k % 2], ps[:, 0:4 * 512].rearrange("p (h f) -> p h f", f=P), AX.X, ALU.max).then_inc(maxed, 1)
                    v.wait_ge(maxed, 2 * k + 1)
                    v.tensor_scalar(mx[:, k % 2], mx[:, k % 2], -HF ** -0.5, None, ALU.mult).then_inc(maxed, 1)
                if at(k - 1):
                    b = k - 1
                    v.wait_ge(halved, 2 * (b + 1))
                    v.tensor_reduce(sm[:, b % 2], SS[:, :, 0:P // 4], AX.X, ALU.add).then_inc(summed, 1)
                    v.wait_ge(summed, b + 1)
                    v.reciprocal(sm[:, b % 2], sm[:, b % 2]).then_inc(rec_done, 1)
                if at(k - 4):
                    b = k - 4
                    v.wait_ge(y_read, b + 1)
                    rms_scale(v, c, ROWS[:, b], ROWS[:, b], N1[:], stats[:], col[:]).then_inc(xf_done, 1)
                if at(k - 2):
                    v.wait_ge(ot_hi, k - 1)
                    v.tensor_tensor(OT_lo[:], bank(6), OT_hi[:].bitcast(F32), ALU.subtract).then_inc(ot_lo, 1)
                if at(k - 3):
                    b = k - 3
                    v.wait_ge(y_done, b + 1)
                    v.tensor_tensor(ROWS[:, b], bank(7), ROWS[:, b], ALU.add).then_inc(y_read, 1)
                if at(k - 5):
                    b = k - 5
                    s_ = slice(b * P, (b + 1) * P)
                    v.wait_ge(xt_hi, b + 1)
                    v.tensor_tensor(XT_lo[:, :, s_], bank(5).rearrange("p (k f) -> p k f", k=KC), XT_hi[:, :, s_].bitcast(F32),
                                    ALU.subtract).then_inc(xt_lo, 1)
            v.wait_ge(logits_turned, 1)
            v.tensor_tensor(LG[:], bank(2, NL * B).rearrange("p (b n) -> p n b", b=B), BIAS[:].unsqueeze(2).broadcast_to([P, NL, B]),
                            ALU.add).then_inc(logits_read, 1)
            v.wait_ge(logits_read, 1)
            route(v, link)

        @block.tensor
        def _(t_):
            def exact(out, pairs):
                n, steps = 0, 3 * len(pairs)
                for (x_hi, x_lo), (w_hi, w_lo) in pairs:
                    for l, r in ((x_lo, w_hi), (x_hi, w_lo), (x_hi, w_hi)):
                        mm = t_.matmul(out, l, r, start=n == 0, stop=n == steps - 1)
                        n += 1
                return mm
            half = lambda t: slice(t * HALF, (t + 1) * HALF)
            t_.wait_ge(wc_lo_done, 1)
            for n in range(4):
                f_ = slice(n // 2 * DC, (n // 2 + 1) * DC)
                exact(bank(n), [((WC_hi[:, k, f_], WC_lo[:, k, f_]), (XT_hi[:, k, half(n % 2)], XT_lo[:, k, half(n % 2)]))
                                for k in range(KC)]).then_inc(c_done, 1)
            for u, (w, c, t) in enumerate(UNITS):
                if u == 0:
                    t_.wait_ge(swapped, 4)
                if w == "k" and c == 0 and t == 0:
                    t_.wait_ge(k_swapped, 2)
                    t_.wait_ge(ct_copied, 4)
                if u >= 2:
                    t_.wait_ge(multiplied, 2 * (u - 1))
                f_ = slice(c * P, (c + 1) * P)
                for s in range(2):
                    out = bank(4 + 2 * (u % 2) + s)
                    if w == "q":
                        hi, lo = ((WQ_hi, WQ_lo), (WS_hi, WS_lo))[s]
                        mm = exact(out, [((hi[:, k, f_], lo[:, k, f_]), (XT_hi[:, k, half(t)], XT_lo[:, k, half(t)])) for k in range(KC)])
                    else:
                        mm = t_.matmul(out, WK[:, s, f_], CT[:, 0, half(t)], start=True, stop=True)
                mm.then_inc(two_done, 1)
            t_.wait_ge(roped, NU)

            def turn(out, src):
                for j in range(KC):
                    mm = t_.transpose(out[:, j * P:(j + 1) * P], src[:, j * P:(j + 1) * P], I[:])
                return mm
            def turn_weights(b, n):
                if n == 0:
                    t_.wait_ge(scaled, b + 1)
                    t_.wait_ge(v_copied, B)
                    if b >= 4:
                        t_.wait_ge(xt_lo, b - 3)
                if 4 * b + n >= 2:
                    t_.wait_ge(pt_copied, 4 * b + n - 1)
                turn(bank(5 - n % 2), flat(S[b % 3][:, 4 * n:4 * n + 4])).then_inc(p_turned, 1)
            for k in STEPS:
                if at(k - 2):
                    turn_weights(k - 2, 0)
                    turn_weights(k - 2, 1)
                if at(k):
                    if k:
                        t_.wait_ge(s_expd, H * k)
                    for h in range(H):
                        q_ = slice(h % 4 * HF, (h % 4 + 1) * HF)
                        mm = t_.matmul(bank(h % 4)[:, h // 4 * P:(h // 4 + 1) * P], QT[q_, h // 4, k * P:(k + 1) * P],
                                       KT_[q_, h // 4, k * P:(k + 1) * P], start=True, stop=True)
                    mm.then_inc(s_done, 1)
                if k in VALUES:
                    t_.wait_ge(multiplied, 2 * NU)
                    for b in VALUES[k]:
                        if b >= 4:
                            t_.wait_ge(v_copied, b - 3)
                        t_.matmul(bank(4 + b % 4), CT[:, 1, b * P:(b + 1) * P], WV[:], start=True, stop=True).then_inc(v_done, 1)
                if at(k - 2):
                    b = k - 2
                    turn_weights(b, 2)
                    turn_weights(b, 3)
                    t_.wait_ge(pt_copied, 4 * (b + 1))
                    if b:
                        t_.wait_ge(ot_lo, b)
                    for n in range(H):
                        h = n % 4 * 4 + n // 4
                        q_ = slice(h % 4 * HF, (h % 4 + 1) * HF)
                        mm = t_.matmul(bank(6)[q_, h // 4 * P:(h // 4 + 1) * P], V[:, b, h * HF:(h + 1) * HF], PT[:, n, :],
                                       start=True, stop=True)
                    mm.then_inc(pv_done, 1)
                if at(k - 3):
                    b = k - 3
                    if b == 0:
                        t_.wait_ge(wq_lo_done, 2)
                    if b:
                        t_.wait_ge(y_read, b)
                    t_.wait_ge(ot_lo, b + 1)
                    exact(bank(7), [((OT_hi[:, j * P:(j + 1) * P], OT_lo[:, j * P:(j + 1) * P]), (WQ_hi[:, j], WQ_lo[:, j]))
                                    for j in range(KC)]).then_inc(y_done, 1)
                if at(k - 5):
                    b = k - 5
                    t_.wait_ge(pt_copied, 4 * min(b + 4, B) - 1)
                    t_.wait_ge(xf_done, b + 1)
                    if b:
                        t_.wait_ge(xt_lo, b)
                    turn(bank(5), ROWS[:, b]).then_inc(f_turned, 1)
            t_.wait_ge(xt_lo, B)
            t_.wait_ge(wg_lo_done, 1)
            for t in range(2):
                exact(bank(t)[0:NL], [((WG_hi[:, j], WG_lo[:, j]), (XT_hi[:, j, half(t)], XT_lo[:, j, half(t)])) for j in range(KC)]
                      ).then_inc(logits_done, 1)
            t_.wait_ge(lt_copied, 2)
            for b in range(B):
                mm = t_.transpose(bank(2)[:, b * NL:(b + 1) * NL], LT[:, b * P:(b + 1) * P], I[0:NL, 0:NL])
            mm.then_inc(logits_turned, 1)


GP = 4


def hidden_piece(w, RAW, j, q):
    dst = RAW[:, q].rearrange("p (s k f) -> p s k f", s=2, k=KC)
    rows = w.rearrange("(k p) n -> p k n", p=P)
    return [(dst[:, s], rows[:, :, s * HID + j * P:s * HID + (j + 1) * P]) for s in range(2)]


def stage_dense(nc, x2_d, wts, norm2, ROWS, XT_hi, XT_lo, W8, RAW, out):
    w_in, w_out, w1, w2 = wts
    with ExitStack() as ctx:
        sb = lambda n, s, d=F32: ctx.enter_context(nc.sbuf_tensor("d_" + n, s, d))
        sem = lambda n: ctx.enter_context(nc.semaphore("d_" + n))
        HK = HID // P
        PW = 2 * D
        TH = TOK // 512
        W_hi = sb("w_hi", [P, 2, GP, PW], F32R)
        W_lo = sb("w_lo", [P, 2, GP, PW], F32R)
        HT_hi = sb("ht_hi", [P, HK, TOK], F32R)
        HT_lo = sb("ht_lo", [P, HK, TOK], F32R)
        SG = sb("sg", [P, 2, 512])
        HS = sb("hs", [P, 2, 512])
        W8i = sb("w8i", [P, B, 2])
        N2 = sb("n2", [P, D])
        X2 = sb("x2", [P, 2, D])
        OUT = HS
        ZERO = sb("zero", [P, 1])
        zeroed = sem("zeroed")
        stats = sb("stats", [P, 6])
        col = sb("col", [P, 8])
        ps = ctx.enter_context(nc.psum_tensor("d_ps", [P, 8 * 512], F32))
        bank = lambda n: ps[:, n * 512:(n + 1) * 512]
        raw_in = [sem(f"raw_in{q}") for q in range(GP)]
        w_hi_done, w_lo_done = sem("w_hi_done"), sem("w_lo_done")
        a_done, b_done, silu_done, h_done, h_hi, h_lo = (sem(n) for n in ("a_done", "b_done", "silu_done", "h_done", "h_hi", "h_lo"))
        out_done, added = sem("out_done"), sem("added")
        n2_in, w8i_done, vchain, final = sem("n2_in"), sem("w8i_done"), sem("vchain"), sem("final")
        x2_in, stored = [sem("x2_in0"), sem("x2_in1")], [sem("stored0"), sem("stored1")]
        block = ctx.enter_context(nc.Block())
        A_, B_ = 0, 1

        def region_free(eng, G, q):
            if isinstance(G, int) and G in (1, 3, 4):
                eng.wait_ge(b_done, TH * (GP * {1: 0, 3: 1, 4: 2}[G] + q + 1))
            elif isinstance(G, int) and G == 5:
                eng.wait_ge(out_done, B)
            elif isinstance(G, int) and G == 6:
                eng.wait_ge(b_done, 2 * TH * HK)
            elif not isinstance(G, int) or G > 6:
                eng.wait_ge(out_done, B * (G - 5))

        @block.sync
        def _(sp):
            def piece(src, G, q):
                sp.wait_ge(w_lo_done, GP * (G - 1) + q + 1)
                sp.dma_start(RAW[:, q].rearrange("p (k f) -> p k f", k=src.shape[1]), src).then_inc(raw_in[q], 16)

            def hidden_group(w, G, j):
                for q in range(GP):
                    sp.wait_ge(w_lo_done, GP * (G - 1) + q + 1)
                    for dst, src in hidden_piece(w, RAW, j + q, q):
                        sp.dma_start(dst, src).then_inc(raw_in[q], 16)

            def out_group(w, G):
                rows = w.rearrange("(k p) n -> p k n", p=P)
                for q in range(GP):
                    piece(rows[:, 2 * q:2 * q + 2, :], G, q)
            hidden_group(w_in, 1, GP)
            sp.dma_start(N2[:], norm2.partition_broadcast(P)).then_inc(n2_in, 16)
            for par in range(2):
                sp.dma_start(X2[:, par], x2_d[par]).then_inc(x2_in[par], 16)
            out_group(w_out, 2)
            hidden_group(w1, 3, 0)
            hidden_group(w1, 4, GP)
            with sp.Fori(0, E_ALL) as e:
                out_group(w2[bass.ds(e, 1)].rearrange("o k n -> (o k) n"), e + 5)
            for b in range(B):
                sp.wait_ge(final, b + 1)
                sp.dma_start(out[b], OUT[:, b % 2]).then_inc(stored[b % 2], 16)
                if b + 2 < B:
                    sp.dma_start(X2[:, b % 2], x2_d[b + 2]).then_inc(x2_in[b % 2], 16)
            for par in range(2):
                sp.wait_ge(stored[par], 16 * B // 2)

        def raw_value(G):
            if isinstance(G, int):
                return 16 * sum(1 if g == 2 or g >= 5 else 2 for g in range(1, G + 1))
            return 16 * (G + 3)

        @block.gpsimd
        def _(g):
            g.memset(ZERO[:], 0.0).then_inc(zeroed, 1)
            g.wait_ge(zeroed, 1)

            def split(G, r):
                for q in range(GP):
                    g.wait_ge(raw_in[q], raw_value(G))
                    region_free(g, G, q)
                    g.tensor_tensor(W_hi[:, r, q], RAW[:, q], ZERO[:].broadcast_to([P, PW]), ALU.add).then_inc(w_hi_done, 1)
                    g.wait_ge(w_hi_done, GP * G + q + 1)
                    g.tensor_tensor(W_lo[:, r, q], RAW[:, q], W_hi[:, r, q].bitcast(F32), ALU.subtract).then_inc(w_lo_done, 1)
            g.wait_ge(w_lo_done, GP)
            for G, r in enumerate((A_, B_, A_, A_, B_, A_), 1):
                split(G, r)
            with g.Fori(1, E_ALL // 2) as i:
                for r in (B_, A_):
                    split(2 * i + 5 + (r == A_), r)

        def hidden_tiles(eng, body):
            def branch(n0):
                with eng.Fori(0, 2) as i:
                    for q in range(GP):
                        for t in range(TH):
                            body(i, q, t, n0 + 2 * GP * i + TH * q + t)
            return branch

        @block.scalar
        def _(a):
            def tile(i, q, t, n):
                a.wait_ge(a_done, n + 1)
                a.activation(SG[:, t], bank(2 * t), ACT.Silu).then_inc(silu_done, 1)
                a.wait_ge(h_done, n + 1)
                a.copy(HT_hi[:, bass.ds(GP * i + q, 1), t * 512:(t + 1) * 512].rearrange("p o f -> p (o f)"), HS[:, t]).then_inc(h_hi, 1)
            for q in range(GP):
                a.copy(W_hi[:, A_, q], RAW[:, q]).then_inc(w_hi_done, 1)
            branch = hidden_tiles(a, tile)
            branch(0)
            branch(2 * HK)

        @block.vector
        def _(v):
            def tile(i, q, t, n):
                v.wait_ge(b_done, n + 1)
                v.wait_ge(silu_done, n + 1)
                v.tensor_tensor(HS[:, t], SG[:, t], bank(2 * t + 1), ALU.mult).then_inc(h_done, 1)
                v.wait_ge(h_hi, n + 1)
                h_ = (slice(None), bass.ds(GP * i + q, 1), slice(t * 512, (t + 1) * 512))
                v.tensor_tensor(HT_lo[h_].rearrange("p o f -> p (o f)"), HS[:, t], HT_hi[h_].bitcast(F32).rearrange("p o f -> p (o f)"),
                                ALU.subtract).then_inc(h_lo, 1)
            for q in range(GP):
                v.wait_ge(w_hi_done, q + 1)
                v.tensor_tensor(W_lo[:, A_, q], RAW[:, q], W_hi[:, A_, q].bitcast(F32), ALU.subtract).then_inc(w_lo_done, 1)
            branch = hidden_tiles(v, tile)
            branch(0)
            for b in range(B):
                v.wait_ge(out_done, b + 1)
                v.tensor_tensor(ROWS[:, b], bank(4 + b % 4), ROWS[:, b], ALU.add).then_inc(added, 1)
            branch(2 * HK)

            def expert(i, s, last):
                u = 2 * i + s + 1
                for b in range(B):
                    v.wait_ge(out_done, B * u + b + 1)
                    v.wait_ge(added, B * (u - 1) + b + 1)
                    v.scalar_tensor_tensor(out=ROWS[:, b], in0=bank(4 + b % 4), scalar=W8i[:, b, s:s + 1], in1=ROWS[:, b],
                                           op0=ALU.mult, op1=ALU.add).then_inc(added, 1)
                    if last:
                        v.wait_ge(added, B * u + b + 1)
                        c.link(rms_scale(v, c, ROWS[:, b], ROWS[:, b], N2[:], stats[:], col[:]))
                        v.wait_ge(x2_in[b % 2], 16 * (b // 2 + 1))
                        if b >= 2:
                            v.wait_ge(stored[b % 2], 16 * (b // 2))
                        v.tensor_tensor(OUT[:, b % 2], ROWS[:, b], X2[:, b % 2], ALU.add).then_inc(final, 1)

            def weights_of(i):
                v.wait_ge(added, B * (2 * i + 1))
                v.tensor_copy(W8i[:], W8[:, :, bass.ds(2 * i, 2)]).then_inc(w8i_done, 1)
                v.wait_ge(w8i_done, i + 1)
            c = Chain(v, vchain, 0, 0)
            v.wait_ge(n2_in, 16)
            with v.Fori(0, E_ALL // 2 - 1) as i:
                weights_of(i)
                expert(i, 0, False)
                expert(i, 1, False)
            i = E_ALL // 2 - 1
            weights_of(i)
            expert(i, 0, False)
            expert(i, 1, True)

        @block.tensor
        def _(t_):
            def branch(n0, G0):
                def turn(i, first):
                    for q in range(GP):
                        t_.wait_ge(w_lo_done, GP * (G0 + i) + q + 1)
                        for t in range(TH):
                            n = n0 + 2 * GP * i + TH * q + t
                            if not first or TH * q + t >= 2:
                                t_.wait_ge(h_done, n - 1)
                            for s in range(2):
                                m = 0
                                for k in range(KC):
                                    at = slice((s * KC + k) * P, (s * KC + k + 1) * P)
                                    for w, x_ in ((W_lo, XT_hi), (W_hi, XT_lo), (W_hi, XT_hi)):
                                        mm = t_.matmul(bank(2 * t + s), w[:, A_, q, at], x_[:, k, t * 512:(t + 1) * 512],
                                                       start=m == 0, stop=m == 3 * KC - 1)
                                        m += 1
                                mm.then_inc((a_done, b_done)[s], 1)
                if n0 == 0:
                    turn(0, True)
                    turn(1, False)
                else:
                    with t_.Fori(0, 2) as i:
                        turn(i, False)

            def unit(u, G, r):
                t_.wait_ge(w_lo_done, GP * (G + 1))
                for b in range(B):
                    if b >= 4 or not isinstance(u, int) or u > 0:
                        t_.wait_ge(added, B * u + b - 3)
                    m = 0
                    for k in range(HK):
                        for h, w in ((HT_lo, W_hi), (HT_hi, W_lo), (HT_hi, W_hi)):
                            mm = t_.matmul(bank(4 + b % 4), h[:, k, b * P:(b + 1) * P], w[:, r, k // 2, (k % 2) * D:(k % 2 + 1) * D],
                                           start=m == 0, stop=m == 3 * HK - 1)
                            m += 1
                    mm.then_inc(out_done, 1)
            branch(0, 0)
            t_.wait_ge(h_lo, TH * HK)
            unit(0, 2, B_)
            branch(TH * HK, 3)
            t_.wait_ge(h_lo, 2 * TH * HK)
            with t_.Fori(0, E_ALL // 2) as i:
                unit(2 * i + 1, 2 * i + 5, B_)
                unit(2 * i + 2, 2 * i + 6, A_)


def clear_semaphores(nc):
    nums = sorted(nc.released_uncleared_semaphores)
    with nc.Block() as block:
        @block.gpsimd
        def _(g):
            g.sem_clear(range(nums[0], nums[-1] + 1))


def program(nc, x, ctx_t, mask, ident, rope, causal, rope_t, earlier, wq, wkv, front, attend, w_proj, ffn, dense, norm2, out):
    scratch = lambda n, s: nc.dram_tensor(n, s, F32, kind="Internal").ap()
    q_hi = scratch("q_hi_scratch", (PAIRS, P, TOK))
    q_lo = scratch("q_lo_scratch", (PAIRS, P, TOK))
    o_part = scratch("o_part_scratch", (NIT, VW, GRP, GW))
    x1 = scratch("x1_scratch", (B, P, D))
    x2 = scratch("x2_scratch", (B, P, D))
    with ExitStack() as ctx:
        sb = lambda n, s, d=F32: ctx.enter_context(nc.sbuf_tensor(n, s, d))
        WKV = sb("wkv_hi", [P, KC, 2 * INNER], F32R), sb("wkv_lo", [P, KC, 2 * INNER], F32R)
        C = sb("c_hi", [P, 2, KC, BLK], F32R), sb("c_lo", [P, 2, KC, BLK], F32R)
        RAW = sb("raw", [P, 2, KC, BLK])
        stage_queries(nc, x, wq, wkv, ctx_t, ident, q_hi, q_lo, WKV, C, RAW)
        stage_cross(nc, ctx_t, mask, q_hi, q_lo, o_part, WKV, C, RAW)
    clear_semaphores(nc)
    with ExitStack() as ctx:
        sb = lambda n, s, d=F32: ctx.enter_context(nc.sbuf_tensor(n, s, d))
        ROWS = sb("rows", [P, B, D])
        XT_hi = sb("xt_hi", [P, KC, TOK], F32R)
        XT_lo = sb("xt_lo", [P, KC, TOK], F32R)
        W8 = sb("w8", [P, B, E_ALL])
        with ExitStack() as inner:
            sb = lambda n, s, d=F32: inner.enter_context(nc.sbuf_tensor(n, s, d))
            RANKS = sb("ranks", [QL + KVL, TOK])
            keep = (XT_hi, XT_lo, RANKS[0:QL, :], RANKS[QL:, :], sb("krt", [P, B, ROPE]), sb("gate", [P, B, 3]))
            ROUND_RAW = sb("round_raw", [P, KC, NW])
            w_selk, w_selv, w_wink, w_winv = attend[4:]
            first_round = round_weights((w_selk, w_wink, w_selv, w_winv), ROUND_RAW, 0)
            stage_front(nc, x, o_part, x1, front, (ident, rope), keep, ROWS, first_round)
            stage_attend(nc, attend, (ident, rope, causal), keep, ROWS, ROUND_RAW)
        stage_project(nc, x1, x2, w_proj, ident, ROWS, XT_hi, XT_lo)
        clear_semaphores(nc)
        DENSE_RAW = ctx.enter_context(nc.sbuf_tensor("dense_raw", [P, GP, 2 * D], F32))
        first_pieces = [piece for q in range(GP) for piece in hidden_piece(dense[0], DENSE_RAW, q, q)]
        stage_ffn_attend(nc, ffn, (ident, rope_t, earlier), ROWS, XT_hi, XT_lo, W8, first_pieces)
        stage_dense(nc, x2, dense, norm2, ROWS, XT_hi, XT_lo, W8, DENSE_RAW, out)


FRONT = ["L0_xattn_Wo", "L0_xattn_bo"] + ["L0_attn_" + n for n in ("w_cq", "g_qnorm", "w_ckv", "g_kvnorm", "w_krope", "w_gate")]
ATTEND = ["L0_attn_" + n for n in ("w_dq_nope", "w_dq_rope", "w_dk_nope", "w_dv", "w_selk", "w_selv", "w_wink", "w_winv")]
FFN = ["L0_ffn_" + n for n in ("Wq", "Wk_c", "Wv_c", "Wk", "Wv", "Wo", "Wg_gate", "We_gate", "group_bias", "expert_bias", "norm1_w")]
DENSE = ["L0_ffn_" + n for n in ("W_shared_in", "W_shared_out", "W1_shared", "W2_experts")]


def tables():
    angle = np.outer(np.arange(P), 10000.0 ** (-np.arange(0, ROPE, 2) / ROPE))
    cos, sin = np.cos(angle), np.sin(angle)
    rope = np.stack([np.concatenate([cos, cos], 1), np.concatenate([sin, -sin], 1)], 1)
    angle = np.outer(np.arange(P), 10000.0 ** (-np.arange(0, HF, 2) / HF))
    cos, sin = np.cos(angle), np.sin(angle)
    pairs = lambda a, b: np.tile(np.stack([a, b], 2).reshape(P, HF).T, (P // HF, 1))
    rope_t = np.stack([pairs(cos, cos), pairs(-sin, sin)], 1)
    causal = np.zeros((P, 3, P))
    causal[:, 0] = causal[:, 2] = np.triu(np.full((P, P), NEG), 1)
    f = lambda a: np.ascontiguousarray(a, np.float32)
    return {"ident": f(np.eye(P)), "rope": f(rope), "causal": f(causal), "rope_t": f(rope_t), "earlier": f(np.tril(np.ones((EPG, EPG)), -1))}


def kernel(**inputs):
    import concourse.bacc as bacc
    from concourse.bass_utils import run_bass_kernel_spmd

    nc = bacc.Bacc("TRN2", target_bir_lowering=False, num_devices=1)
    ctx = np.asarray(inputs["ctx_1024"]).reshape(B * M // BLK, BLK, KC, P)
    mask = np.asarray(inputs["mask_BxS2_bk1"]).reshape(B, M // P, P)
    arrays = {
        "x": np.asarray(inputs["x"]),
        "ctx_t": ctx.transpose(0, 3, 2, 1),
        "mask": np.ascontiguousarray(mask.transpose(2, 0, 1)).reshape(P, P),
        **tables(),
        **{n: np.asarray(inputs[n]) for n in ["L0_xattn_Wq", "L0_xattn_Wkv", *FRONT, *ATTEND, "L0_attn_w_proj", *FFN, *DENSE, "L0_ffn_norm2_w"]},
    }
    arrays = {"in_" + n: np.ascontiguousarray(a) for n, a in arrays.items()}
    ap = {n[3:]: nc.dram_tensor(n, a.shape, mybir.dt.from_np(a.dtype), kind="ExternalInput").ap() for n, a in arrays.items()}
    out = nc.dram_tensor("out", (B, P, D), F32, kind="ExternalOutput").ap()
    program(nc, *(ap[n] for n in ("x", "ctx_t", "mask", "ident", "rope", "causal", "rope_t", "earlier", "L0_xattn_Wq", "L0_xattn_Wkv")),
            [ap[n] for n in FRONT], [ap[n] for n in ATTEND], ap["L0_attn_w_proj"], [ap[n] for n in FFN], [ap[n] for n in DENSE], ap["L0_ffn_norm2_w"], out)
    r = run_bass_kernel_spmd(nc, [arrays], core_ids=[0])
    return r.results[0]["out"]
```
